# Optimizing a Trainium2 kernel written in Bass

```python
import numpy as np
import jax
import jax.numpy as jnp

def _softmax(x, axis=-1):
    return jax.nn.softmax(x, axis=axis)

def _gelu(x):
    return jax.nn.gelu(x, approximate=True)

def _silu(x):
    return jax.nn.silu(x)

def _sigmoid(x):
    return jax.nn.sigmoid(x)

def _layernorm(x, axis=-1, eps=1e-05):
    m = jnp.mean(x, axis=axis, keepdims=True)
    v = jnp.var(x, axis=axis, keepdims=True)
    return (x - m) / jnp.sqrt(v + eps)

def _scatter_add(tgt, idx, src, axis=0):
    return tgt.at[idx].add(src)

def _segment_sum(src, seg, n):
    return jax.ops.segment_sum(src, seg, n)
kernel_name = 'mk_gnn_resnorm_d4_gnn_r8_19ff22'

def setup_inputs(seed: int=0):
    np.random.seed(seed)
    _w = jnp.asarray

    def _rec_inputs():
        import jax
        import jax.numpy as jnp
        _gk = jax.random.key(seed)
        x = -0.000202 + 1 * jax.random.normal(jax.random.fold_in(_gk, 1), (6250, 128), jnp.float32)
        _s = jax.random.randint(jax.random.fold_in(_gk, 2), (100000,), 0, 6250, jnp.int32)
        _d = jax.random.randint(jax.random.fold_in(_gk, 3), (100000,), 0, 6250, jnp.int32)
        _loop = jnp.arange(6250, dtype=jnp.int32)
        src = jnp.concatenate([_s, _d, _loop])
        dst = jnp.concatenate([_d, _s, _loop])
        _o = jnp.argsort(dst, stable=True)
        src = src[_o]
        dst = dst[_o]
        edge_attr_128 = -8.16379e-05 + 0.999858 * jax.random.normal(jax.random.fold_in(_gk, 12), (206250, 128), jnp.float32)
        return (x, src, dst, edge_attr_128)
    x, src, dst, edge_attr_128 = _rec_inputs()

    def _L0_gnn_setup():
        import jax, jax.numpy as jnp
        import numpy as np
        N_NODES = 6250
        N_EDGES = 100000
        F_X = 128
        F_E = 128
        HIDDEN = 512
        F_OUT = 128
        key = jax.random.key(seed)
        k1, k2, k3, k4, k5, k6 = jax.random.split(key, 6)
        nodes = jax.random.normal(k1, (N_NODES, F_X), dtype=jnp.float32)
        edge_attr = jax.random.normal(k2, (N_EDGES, F_E), dtype=jnp.float32)
        senders = jax.random.randint(k3, (N_EDGES,), 0, N_NODES, dtype=jnp.int32)
        receivers = jax.random.randint(k4, (N_EDGES,), 0, N_NODES, dtype=jnp.int32)
        W1 = jax.random.normal(k5, (F_E + F_X, HIDDEN), dtype=jnp.float32) * (1.0 / np.sqrt(F_E + F_X))
        b1 = jnp.zeros((HIDDEN,), dtype=jnp.float32)
        W2 = jax.random.normal(k6, (HIDDEN, F_OUT), dtype=jnp.float32) * (1.0 / np.sqrt(HIDDEN))
        b2 = jnp.zeros((F_OUT,), dtype=jnp.float32)
        return {'nodes': nodes, 'edge_attr': edge_attr, 'senders': senders, 'receivers': receivers, 'W1': W1, 'b1': b1, 'W2': W2, 'b2': b2}
    _L0_gnn_all = _L0_gnn_setup()
    _L0_gnn_in = {k: v for k, v in _L0_gnn_all.items() if k in ('W1', 'b1', 'W2', 'b2')}
    del _L0_gnn_all

    def _L1_gnn_setup():
        import jax, jax.numpy as jnp
        import numpy as np
        N = 6250
        E = 100000
        HID = 128
        NH = 8
        HD = HID // NH
        EPS = 1e-05

        def _layernorm(x, g, b):
            mu = jnp.mean(x, axis=-1, keepdims=True)
            var = jnp.mean(jnp.square(x - mu), axis=-1, keepdims=True)
            return (x - mu) * jax.lax.rsqrt(var + EPS) * g + b

        def _gmha(edge_index, h, WQ, bQ, WK, bK, WV, bV):
            Q = (h @ WQ + bQ).reshape(-1, NH, HD)
            K = (h @ WK + bK).reshape(-1, NH, HD)
            V = (h @ WV + bV).reshape(-1, NH, HD)
            src, dst = (edge_index[0], edge_index[1])
            q_dst = Q[dst]
            k_src = K[src]
            v_src = V[src]
            score = jnp.sum(q_dst * k_src, axis=-1) / np.sqrt(HD)
            score = jnp.clip(score, -5.0, 5.0)
            attn = jax.nn.softmax(score, axis=0)
            msg = attn[..., None] * v_src
            h_out = jnp.zeros_like(Q).at[dst].add(msg)
            return h_out.reshape(-1, NH * HD)
        key = jax.random.key(seed)
        ks = jax.random.split(key, 16)
        s = 1.0 / np.sqrt(HID)

        def lin(k):
            kw, kb = jax.random.split(k)
            W = jax.random.uniform(kw, (HID, HID), jnp.float32, -s, s)
            b = jax.random.uniform(kb, (HID,), jnp.float32, -s, s)
            return (W, b)
        WQ, bQ = lin(ks[0])
        WK, bK = lin(ks[1])
        WV, bV = lin(ks[2])
        WO, bO = lin(ks[3])
        W1, b1 = lin(ks[4])
        W2, b2 = lin(ks[5])
        return {'h': jax.random.normal(ks[6], (N, HID), jnp.float32), 'edge_index': jax.random.randint(ks[7], (2, E), 0, N, jnp.int32), 'WQ': WQ, 'bQ': bQ, 'WK': WK, 'bK': bK, 'WV': WV, 'bV': bV, 'WO': WO, 'bO': bO, 'W1': W1, 'b1': b1, 'W2': W2, 'b2': b2, 'ln1_g': jnp.ones((HID,), jnp.float32), 'ln1_b': jnp.zeros((HID,), jnp.float32), 'ln2_g': jnp.ones((HID,), jnp.float32), 'ln2_b': jnp.zeros((HID,), jnp.float32)}
    _L1_gnn_all = _L1_gnn_setup()
    _L1_gnn_in = {k: v for k, v in _L1_gnn_all.items() if k in ('WQ', 'bQ', 'WK', 'bK', 'WV', 'bV', 'WO', 'bO', 'W1', 'b1', 'W2', 'b2', 'ln1_g', 'ln1_b', 'ln2_g', 'ln2_b')}
    del _L1_gnn_all

    def _L2_gnn_setup():
        import jax, jax.numpy as jnp
        import numpy as np
        N_NODES = 6250
        N_EDGES = 100000
        D = 128

        def _mlp(h, W1, b1, W2, b2):
            return jax.nn.relu(h @ W1 + b1) @ W2 + b2
        key = jax.random.key(seed)
        ks = jax.random.split(key, 6)
        s = 0.05
        x = jax.random.normal(ks[0], (N_NODES, D), dtype=jnp.float32)
        edge_index = jax.random.randint(ks[1], (2, N_EDGES), 0, N_NODES, dtype=jnp.int64)
        We1 = jax.random.normal(ks[2], (2 * D, D), dtype=jnp.float32) * s
        be1 = jnp.zeros((D,), dtype=jnp.float32)
        We2 = jax.random.normal(ks[3], (D, D), dtype=jnp.float32) * s
        be2 = jnp.zeros((D,), dtype=jnp.float32)
        Wn1 = jax.random.normal(ks[4], (2 * D, D), dtype=jnp.float32) * s
        bn1 = jnp.zeros((D,), dtype=jnp.float32)
        Wn2 = jax.random.normal(ks[5], (D, D), dtype=jnp.float32) * s
        bn2 = jnp.zeros((D,), dtype=jnp.float32)
        return {'x': x, 'edge_index': edge_index, 'We1': We1, 'be1': be1, 'We2': We2, 'be2': be2, 'Wn1': Wn1, 'bn1': bn1, 'Wn2': Wn2, 'bn2': bn2}
    _L2_gnn_all = _L2_gnn_setup()
    _L2_gnn_in = {k: v for k, v in _L2_gnn_all.items() if k in ('We1', 'be1', 'We2', 'be2', 'Wn1', 'bn1', 'Wn2', 'bn2')}
    del _L2_gnn_all

    def _L3_gnn_setup():
        import jax, jax.numpy as jnp
        import numpy as np
        N_NODES = 6250
        N_EDGES = 75000
        IN_CH = 128
        OUT_CH = 128
        key = jax.random.key(seed)
        k1, k2, k3, k4 = jax.random.split(key, 4)
        x = jax.random.normal(k1, (N_NODES, IN_CH), dtype=jnp.float32)
        edge_index = jax.random.randint(k2, (2, N_EDGES), 0, N_NODES, dtype=jnp.int64)
        W = jax.random.normal(k3, (OUT_CH, IN_CH), dtype=jnp.float32) * (1.0 / np.sqrt(IN_CH))
        b = jax.random.normal(k4, (OUT_CH,), dtype=jnp.float32) * 0.01
        return {'x': x, 'edge_index': edge_index, 'W': W, 'b': b}
    _L3_gnn_all = _L3_gnn_setup()
    _L3_gnn_in = {k: v for k, v in _L3_gnn_all.items() if k in ('W', 'b')}
    del _L3_gnn_all
    return {'x': x, 'src': src, 'dst': dst, 'edge_attr_128': edge_attr_128, 'L0_gnn_W1': _L0_gnn_in['W1'], 'L0_gnn_b1': _L0_gnn_in['b1'], 'L0_gnn_W2': _L0_gnn_in['W2'], 'L0_gnn_b2': _L0_gnn_in['b2'], 'L1_gnn_WQ': _L1_gnn_in['WQ'], 'L1_gnn_bQ': _L1_gnn_in['bQ'], 'L1_gnn_WK': _L1_gnn_in['WK'], 'L1_gnn_bK': _L1_gnn_in['bK'], 'L1_gnn_WV': _L1_gnn_in['WV'], 'L1_gnn_bV': _L1_gnn_in['bV'], 'L1_gnn_WO': _L1_gnn_in['WO'], 'L1_gnn_bO': _L1_gnn_in['bO'], 'L1_gnn_W1': _L1_gnn_in['W1'], 'L1_gnn_b1': _L1_gnn_in['b1'], 'L1_gnn_W2': _L1_gnn_in['W2'], 'L1_gnn_b2': _L1_gnn_in['b2'], 'L1_gnn_ln1_g': _L1_gnn_in['ln1_g'], 'L1_gnn_ln1_b': _L1_gnn_in['ln1_b'], 'L1_gnn_ln2_g': _L1_gnn_in['ln2_g'], 'L1_gnn_ln2_b': _L1_gnn_in['ln2_b'], 'L2_gnn_We1': _L2_gnn_in['We1'], 'L2_gnn_be1': _L2_gnn_in['be1'], 'L2_gnn_We2': _L2_gnn_in['We2'], 'L2_gnn_be2': _L2_gnn_in['be2'], 'L2_gnn_Wn1': _L2_gnn_in['Wn1'], 'L2_gnn_bn1': _L2_gnn_in['bn1'], 'L2_gnn_Wn2': _L2_gnn_in['Wn2'], 'L2_gnn_bn2': _L2_gnn_in['bn2'], 'L3_gnn_W': _L3_gnn_in['W'], 'L3_gnn_b': _L3_gnn_in['b']}

def reference(x, src, dst, edge_attr_128, L0_gnn_W1, L0_gnn_b1, L0_gnn_W2, L0_gnn_b2, L1_gnn_WQ, L1_gnn_bQ, L1_gnn_WK, L1_gnn_bK, L1_gnn_WV, L1_gnn_bV, L1_gnn_WO, L1_gnn_bO, L1_gnn_W1, L1_gnn_b1, L1_gnn_W2, L1_gnn_b2, L1_gnn_ln1_g, L1_gnn_ln1_b, L1_gnn_ln2_g, L1_gnn_ln2_b, L2_gnn_We1, L2_gnn_be1, L2_gnn_We2, L2_gnn_be2, L2_gnn_Wn1, L2_gnn_bn1, L2_gnn_Wn2, L2_gnn_bn2, L3_gnn_W, L3_gnn_b):
    import jax
    import jax.numpy as jnp

    def _L0_gnn_ref(nodes, edge_attr, senders, receivers, W1, b1, W2, b2):
        import jax, jax.numpy as jnp
        import numpy as np
        N_NODES = 6250
        N_EDGES = 100000
        F_X = 128
        F_E = 128
        HIDDEN = 512
        F_OUT = 128
        agg = jax.ops.segment_sum(edge_attr, receivers, num_segments=N_NODES)
        x = jnp.concatenate([agg, nodes], axis=1)
        h = jax.nn.relu(x @ W1 + b1)
        return h @ W2 + b2

    def _L1_gnn_ref(h, edge_index, WQ, bQ, WK, bK, WV, bV, WO, bO, W1, b1, W2, b2, ln1_g, ln1_b, ln2_g, ln2_b):
        import jax, jax.numpy as jnp
        import numpy as np
        N = 6250
        E = 100000
        HID = 128
        NH = 8
        HD = HID // NH
        EPS = 1e-05

        def _layernorm(x, g, b):
            mu = jnp.mean(x, axis=-1, keepdims=True)
            var = jnp.mean(jnp.square(x - mu), axis=-1, keepdims=True)
            return (x - mu) * jax.lax.rsqrt(var + EPS) * g + b

        def _gmha(edge_index, h, WQ, bQ, WK, bK, WV, bV):
            Q = (h @ WQ + bQ).reshape(-1, NH, HD)
            K = (h @ WK + bK).reshape(-1, NH, HD)
            V = (h @ WV + bV).reshape(-1, NH, HD)
            src, dst = (edge_index[0], edge_index[1])
            q_dst = Q[dst]
            k_src = K[src]
            v_src = V[src]
            score = jnp.sum(q_dst * k_src, axis=-1) / np.sqrt(HD)
            score = jnp.clip(score, -5.0, 5.0)
            attn = jax.nn.softmax(score, axis=0)
            msg = attn[..., None] * v_src
            h_out = jnp.zeros_like(Q).at[dst].add(msg)
            return h_out.reshape(-1, NH * HD)
        h_rc = h
        a = _gmha(edge_index, h, WQ, bQ, WK, bK, WV, bV)
        a = a @ WO + bO
        x = _layernorm(h_rc + a, ln1_g, ln1_b)
        f = jax.nn.relu(x @ W1 + b1) @ W2 + b2
        return _layernorm(x + f, ln2_g, ln2_b)

    def _L2_gnn_ref(x, edge_index, We1, be1, We2, be2, Wn1, bn1, Wn2, bn2):
        import jax, jax.numpy as jnp
        import numpy as np
        N_NODES = 6250
        N_EDGES = 100000
        D = 128

        def _mlp(h, W1, b1, W2, b2):
            return jax.nn.relu(h @ W1 + b1) @ W2 + b2
        src = edge_index[0]
        dst = edge_index[1]
        e_in = jnp.concatenate([x[src], x[dst]], axis=-1)
        edge_new = _mlp(e_in, We1, be1, We2, be2)
        agg = jax.ops.segment_sum(edge_new, dst, num_segments=x.shape[0])
        mesh_new = _mlp(jnp.concatenate([x, agg], axis=-1), Wn1, bn1, Wn2, bn2)
        return x + mesh_new

    def _L3_gnn_ref(x, edge_index, W, b):
        import jax, jax.numpy as jnp
        import numpy as np
        N_NODES = 6250
        N_EDGES = 75000
        IN_CH = 128
        OUT_CH = 128
        row, col = (edge_index[0], edge_index[1])
        n = x.shape[0]
        deg = jax.ops.segment_sum(jnp.ones_like(row, dtype=x.dtype), row, num_segments=n)
        deg_inv_sqrt = jnp.where(deg > 0, jax.lax.rsqrt(jnp.where(deg > 0, deg, 1.0)), 0.0)
        norm = deg_inv_sqrt[row] * deg_inv_sqrt[col]
        msgs = norm[:, None] * x[col]
        agg = jax.ops.segment_sum(msgs, row, num_segments=n)
        return agg @ W.T + b
    edge_index = jnp.stack([src, dst])
    x = _layernorm(x + _L0_gnn_ref(x, edge_attr_128, src, dst, L0_gnn_W1, L0_gnn_b1, L0_gnn_W2, L0_gnn_b2), axis=-1)
    x = _layernorm(x + _L1_gnn_ref(x, edge_index, L1_gnn_WQ, L1_gnn_bQ, L1_gnn_WK, L1_gnn_bK, L1_gnn_WV, L1_gnn_bV, L1_gnn_WO, L1_gnn_bO, L1_gnn_W1, L1_gnn_b1, L1_gnn_W2, L1_gnn_b2, L1_gnn_ln1_g, L1_gnn_ln1_b, L1_gnn_ln2_g, L1_gnn_ln2_b), axis=-1)
    x = _layernorm(x + _L2_gnn_ref(x, edge_index, L2_gnn_We1, L2_gnn_be1, L2_gnn_We2, L2_gnn_be2, L2_gnn_Wn1, L2_gnn_bn1, L2_gnn_Wn2, L2_gnn_bn2), axis=-1)
    x = _layernorm(x + _L3_gnn_ref(x, edge_index, L3_gnn_W, L3_gnn_b), axis=-1)
    return x

_drawn_inputs = setup_inputs


def setup_inputs(seed=0):
    import zlib

    import numpy as np

    out = dict(_drawn_inputs(seed))
    spreads = {'L0_gnn_b1': (0.0, 0.399),
     'L0_gnn_b2': (0.0, 0.333),
     'L1_gnn_ln1_g': (1.0, 0.2),
     'L1_gnn_ln1_b': (0.0, 0.1),
     'L1_gnn_ln2_g': (1.0, 0.2),
     'L1_gnn_ln2_b': (0.0, 0.1),
     'L2_gnn_be1': (0.0, 0.1),
     'L2_gnn_be2': (0.0, 0.1),
     'L2_gnn_bn1': (0.0, 0.597),
     'L2_gnn_bn2': (0.0, 0.1)}
    factors = {'L1_gnn_WQ': 64.0,
     'L1_gnn_bQ': 200.0,
     'L1_gnn_WK': 64.0,
     'L1_gnn_bK': 200.0,
     'L1_gnn_WV': 64.0,
     'L1_gnn_bV': 200.0,
     'L1_gnn_WO': 64.0,
     'L1_gnn_b1': 7.355,
     'L3_gnn_b': 6.822}
    for name, (base, spread) in spreads.items():
        noise = np.random.default_rng([zlib.crc32(name.encode()), seed]).standard_normal(out[name].shape)
        drawn = base * np.exp(spread * noise) if base else spread * noise
        out[name] = jnp.asarray(drawn.astype(out[name].dtype))
    for name, factor in factors.items():
        out[name] = (out[name] * factor).astype(out[name].dtype)
    return out
```

```python
from contextlib import ExitStack

import concourse.bass as bass
from concourse import mybir

P = 128
D = 128
HEADS = 8
HEAD = D // HEADS
HIDDEN = 512
G = 4
SC = G * P
W = 32
U = 4
T = 512
TABLES = 8
LN_EPS = 1e-5
CLIP = 5.0

F32 = mybir.dt.float32
BF16 = mybir.dt.bfloat16
I32 = mybir.dt.int32
ALU = mybir.AluOpType
ACT = mybir.ActivationFunctionType
AX = mybir.AxisListType
ds = bass.ds

VECTORS = ["b1_0", "b1_1", "b1_2", "b1_3", "b2", "bO", "ln1_g", "ln1_b", "a_b1", "a_b2", "ln2_g", "ln2_b",
           "bn1", "bn2", "b3"]
VEC = {name: i for i, name in enumerate(VECTORS)}


def sizes(n_nodes, n_edges):
    node_cols = -(-(n_nodes + W) // T) * T
    superchunks = -(-n_edges // SC)
    superchunks = -(-superchunks // U) * U
    return node_cols, superchunks


def gnn_program(nc, xT, edge_attr, src_index, src_id, dst_id, dst_rows, edge_start, consts,
                w1, w2, wqkv, wo, aw1, aw2, we1, we2, wn1, wn2, w3t, vectors, row_bqkv, row_be1, row_be2, out):
    NODES = xT.shape[1]
    SCS = edge_start.shape[1]
    BODIES = SCS // U
    NTILES = NODES // T
    HI = NODES // P
    SPR = SCS // 4
    assert SPR <= P and SCS % U == 0 and HI <= P
    PASSES_MAX = NODES // W + 1
    ctx = ExitStack()
    with ctx:
        def sb(name, shape, dt=F32):
            return ctx.enter_context(nc.sbuf_tensor(name, shape, dt))

        def sem(name):
            return ctx.enter_context(nc.semaphore(name))

        x = sb("x", [P, NODES])
        acc = sb("acc", [P, NODES])
        count = sb("count", [1, NODES])
        src_num = sb("src_num", [P, SCS * G])
        src_hi = sb("src_hi", [P, SCS * G], BF16)
        src_lo = sb("src_lo", [P, SCS * G], BF16)
        rel0 = sb("rel0", [P, SCS, G])
        rel = sb("rel", [P, SCS, G])
        base0 = sb("base0", [1, SCS])
        base = sb("base", [1, SCS], I32)
        start = sb("start", [1, SCS], I32)
        pass_bodies = sb("pass_bodies", [1, 1], I32)
        cst = sb("cst", [P, 5 * P + W + 1])
        ident = cst[:, 0:P]
        lower = cst[:, P:2 * P]
        mean_m = cst[:, 2 * P:3 * P]
        iota_w = cst[:, 3 * P:3 * P + W]
        iota_p = cst[:, 3 * P + W:4 * P + W]
        spare_row = cst[:, 4 * P + W:4 * P + W + 1]
        head_of = cst[0:HEADS, 4 * P + W + 1:5 * P + W + 1]
        ones = sb("ones", [P, P])
        zeros = sb("zeros", [P, P])
        eps = sb("eps", [P, 1])
        w1_sb = sb("w1_sb", [P, 2, HIDDEN])
        w2_sb = sb("w2_sb", [P, HIDDEN // P, D])
        wqkv_sb = sb("wqkv_sb", [P, 3 * D])
        wo_sb = sb("wo_sb", [P, D])
        aw1_sb = sb("aw1_sb", [P, D])
        aw2_sb = sb("aw2_sb", [P, D])
        we1_sb = sb("we1_sb", [P, 2 * D])
        we2_sb = sb("we2_sb", [P, D])
        wn1_sb = sb("wn1_sb", [P, 2, D])
        wn2_sb = sb("wn2_sb", [P, D])
        w3t_sb = sb("w3t_sb", [P, D])
        vec = sb("vec", [P, len(VECTORS)])
        bqkv_sb = sb("bqkv_sb", [1, 3 * D])
        be1_sb = sb("be1_sb", [1, 2 * D])
        be2_sb = sb("be2_sb", [1, D])

        def v(name):
            return vec[:, VEC[name]:VEC[name] + 1]

        rows = sb("rows", [P, U, G * 2 * D])
        onehot = sb("onehot", [P, U, G, W])
        turned = sb("turned", [P, U, SC])
        onehot_t = turned[0:W, :, :]
        window = sb("window", [W, U, D])
        prod = sb("prod", [P, U, G * D])
        score = sb("score", [P, U, G * HEADS])
        clipped = sb("clipped", [P, U, G * HEADS])
        weight = sb("weight", [P, U, G * HEADS])
        weight_x = sb("weight_x", [P, U, G * D])
        index = sb("index", [P, U, G], I32)
        lo_hot = sb("lo_hot", [P, U, G, P], BF16)
        hi_hot = sb("hi_hot", [P, U, G, HI], BF16)
        same = lo_hot
        onehot_b = sb("onehot_b", [P, U, G, W], BF16)
        src_s = sb("src_s", [P, U, G])
        masked = sb("masked", [P, P])
        earlier = sb("earlier", [P, U, G])
        follows = sb("follows", [P, U, G])
        to_spare = sb("to_spare", [P, U, G])
        shift_by = sb("shift_by", [P, U, G])

        hid = turned
        tmp = prod[:, 0, :]
        res = prod[:, 1, :]
        cen = prod[:, 2, :]
        sqr = prod[:, 3, :]
        std = sb("std", [P, T])
        inv = sb("inv", [P, T])
        y = sb("y", [P, T])
        y2 = sb("y2", [P, T])
        node_rows = sb("node_rows", [P, T // P, 3 * D])
        z_heads = sb("z_heads", [HEADS, 1])
        inv_z = sb("inv_z", [P, 1])
        dis = sb("dis", [P, HI])
        deg_sb = sb("deg_sb", [P, HI])
        deg_pos = sb("deg_pos", [P, HI])
        dis_raw = sb("dis_raw", [P, HI])
        low_sb = sb("low_sb", [P, 8])
        small = sb("small", [1, 4])
        small_i = sb("small_i", [1, 4], I32)

        ps = [ctx.enter_context(nc.psum_tensor(f"ps{i}", [P, 512], F32)) for i in range(8)]

        sp_waited = sem("sp_waited")
        pool_waited = sem("pool_waited")

        q_rows = nc.dram_tensor("q_rows", (NODES, D), F32, kind="Internal").ap()
        kv_rows = nc.dram_tensor("kv_rows", (NODES, 2 * D), F32, kind="Internal").ap()
        a_rows = nc.dram_tensor("a_rows", (NODES, D), F32, kind="Internal").ap()
        b_rows = nc.dram_tensor("b_rows", (NODES, D), F32, kind="Internal").ap()
        y_rows = nc.dram_tensor("y_rows", (NODES, D), F32, kind="Internal").ap()
        table = [nc.dram_tensor(f"table{i}", (NODES + 2 * P, D), F32, kind="Internal").ap() for i in range(TABLES)]

        loaded = sem("loaded")
        rows_loaded = sem("rows_loaded")
        const_set = sem("const_set")
        dst_minmax = sem("dst_minmax")
        low_ready = sem("low_ready")
        range_max = sem("range_max")
        passes_f = sem("passes_f")
        passes_i = sem("passes_i")
        src_split = sem("src_split")
        wq_scaled = sem("wq_scaled")
        prep_dma = 18
        with nc.Block("prepare") as block:
            ids = rows[:, :, :].rearrange("p u c -> p (u c)").bitcast(I32)
            dst_i = ids[0:SPR, 0:4 * SC].rearrange("p (c e) -> p c e", c=4)
            ids2 = hid[:, :, :].rearrange("p u c -> p (u c)").bitcast(I32)
            dst_e = ids2[:, 0:SCS * G]
            src_e = acc[:, 0:SCS * G].bitcast(I32)
            src_w = acc[:, SCS * G:2 * SCS * G].bitcast(I32)

            @block.sync
            def _(sp):
                sp.dma_start(dst_i, dst_rows).then_inc(rows_loaded, 16)
                sp.dma_start(cst[:, :], consts).then_inc(rows_loaded, 16)
                sp.dma_start(dst_e, dst_id).then_inc(rows_loaded, 16)
                sp.dma_start(src_e, src_id).then_inc(rows_loaded, 16)
                for tile, dram in ((x, xT), (start, edge_start), (wqkv_sb, wqkv), (wo_sb, wo), (aw1_sb, aw1),
                                   (aw2_sb, aw2), (we2_sb, we2), (wn2_sb, wn2), (w3t_sb, w3t), (vec, vectors),
                                   (bqkv_sb, row_bqkv), (be1_sb, row_be1), (be2_sb, row_be2)):
                    sp.dma_start(tile[:, :], dram).then_inc(loaded, 16)
                sp.dma_start(we1_sb[:, 0:D], we1[0:D, :]).then_inc(loaded, 16)
                sp.dma_start(we1_sb[:, D:2 * D], we1[D:2 * D, :]).then_inc(loaded, 16)
                sp.dma_start(w1_sb[:, :, :], w1.rearrange("(b p) n -> p b n", p=P)).then_inc(loaded, 16)
                sp.dma_start(w2_sb[:, :, :], w2.rearrange("(b p) n -> p b n", p=P)).then_inc(loaded, 16)
                sp.dma_start(wn1_sb[:, :, :], wn1.rearrange("(b p) n -> p b n", p=P)).then_inc(loaded, 16)
                sp.wait_ge(loaded, 16 * prep_dma)

            @block.vector
            def _(dve):
                dve.memset(ones[:, :], 1.0).then_inc(const_set, 1)
                dve.memset(zeros[:, :], 0.0).then_inc(const_set, 1)
                dve.memset(eps[:, :], LN_EPS).then_inc(const_set, 1)
                dve.memset(count[:, :], 0.0).then_inc(const_set, 1)
                dve.wait_ge(rows_loaded, 64)
                dve.tensor_reduce(low_sb[0:SPR, 0:4], dst_i, AX.X, ALU.min).then_inc(dst_minmax, 1)
                dve.tensor_reduce(low_sb[0:SPR, 4:8], dst_i, AX.X, ALU.max).then_inc(dst_minmax, 1)
                dve.wait_ge(dst_minmax, 2)
                dve.tensor_tensor(low_sb[0:SPR, 4:8], low_sb[0:SPR, 4:8], low_sb[0:SPR, 0:4],
                                  ALU.subtract).then_inc(dst_minmax, 1)
                pad_row = rel[:, :, :].rearrange("p s g -> p (s g)")
                dve.tensor_scalar(pad_row, src_e, 0.0, float(NODES + P + 1), ALU.is_lt, ALU.mult).then_inc(src_split, 1)
                dve.wait_ge(src_split, 1)
                dve.tensor_tensor(src_num[:, :], src_e, pad_row, ALU.add).then_inc(src_split, 1)
                dve.tensor_scalar(src_w, src_e, 7, None, ALU.arith_shift_right).then_inc(src_split, 1)
                dve.wait_ge(src_split, 3)
                dve.tensor_copy(src_hi[:, :], src_w).then_inc(src_split, 1)
                dve.wait_ge(src_split, 4)
                dve.tensor_scalar(src_w, src_e, 127, None, ALU.bitwise_and).then_inc(src_split, 1)
                dve.wait_ge(src_split, 5)
                dve.tensor_copy(src_lo[:, :], src_w).then_inc(src_split, 1)
                dve.wait_ge(low_ready, 1)
                dve.tensor_copy(base0[:, :], ps[0][0:1, 0:SCS]).then_inc(range_max, 1)
                dve.tensor_reduce(small[:, 0:1], ps[1][0:1, 0:SCS], AX.X, ALU.max).then_inc(range_max, 1)
                dve.tensor_copy(rel0[:, :, :], dst_e.rearrange("p (s g) -> p s g", g=G)).then_inc(range_max, 1)
                dve.wait_ge(range_max, 3)
                dve.tensor_tensor(rel0[:, :, :], rel0[:, :, :],
                                  ps[2][:, 0:SCS].unsqueeze(2).broadcast_to([P, SCS, G]),
                                  ALU.subtract).then_inc(range_max, 1)
                dve.tensor_copy(small_i[:, 0:1], small[:, 0:1]).then_inc(passes_f, 1)
                dve.wait_ge(passes_f, 1)
                shift = W.bit_length() - 1
                dve.tensor_scalar(small_i[:, 1:2], small_i[:, 0:1], shift, None,
                                  ALU.arith_shift_right).then_inc(passes_f, 1)
                dve.wait_ge(passes_f, 2)
                dve.tensor_scalar(pass_bodies[:, :], small_i[:, 1:2], float(BODIES), float(BODIES), ALU.mult,
                                  ALU.add).then_inc(passes_i, 1)
                dve.wait_ge(loaded, 16 * prep_dma)
                dve.tensor_scalar(wqkv_sb[:, 0:D], wqkv_sb[:, 0:D], HEAD ** -0.5, None, ALU.mult).then_inc(wq_scaled, 1)
                dve.tensor_scalar(bqkv_sb[:, 0:D], bqkv_sb[:, 0:D], HEAD ** -0.5, None, ALU.mult).then_inc(wq_scaled, 1)
                dve.wait_ge(src_split, 6)
                dve.memset(acc[:, :], 0.0).then_inc(wq_scaled, 1)

            @block.tensor
            def _(pe):
                pe.wait_ge(const_set, 4)
                pe.wait_ge(rows_loaded, 64)
                pe.wait_ge(dst_minmax, 3)
                for c in range(4):
                    cols = slice(c * SPR, (c + 1) * SPR)
                    nc.tensor.matmul(ps[0][0:1, cols], low_sb[0:SPR, c:c + 1], ident[0:SPR, 0:SPR],
                                     start=True, stop=True)
                    nc.tensor.matmul(ps[1][0:1, cols], low_sb[0:SPR, 4 + c:5 + c], ident[0:SPR, 0:SPR],
                                     start=True, stop=True)
                    last = nc.tensor.matmul(ps[2][:, cols], low_sb[0:SPR, c:c + 1].broadcast_to([SPR, P]),
                                            ident[0:SPR, 0:SPR], start=True, stop=True)
                last.then_inc(low_ready, 1)

        def all_bodies(eng):
            return eng.value_load(pass_bodies[0:1, 0:1], min_val=BODIES, max_val=BODIES * PASSES_MAX)

        def windows_reset(dve, windows_set):
            dve.tensor_copy(rel[:, :, :], rel0[:, :, :]).then_inc(windows_set, 1)
            dve.tensor_scalar(base[:, :], base0[:, :], float(NODES - W), None, ALU.min).then_inc(windows_set, 1)

        def windows_move(dve, windows_moved):
            dve.tensor_scalar(rel[:, :, :], rel[:, :, :], float(W), None, ALU.subtract).then_inc(windows_moved, BODIES)
            dve.tensor_scalar(base[:, :], base[:, :], float(W), float(NODES - W), ALU.add,
                              ALU.min).then_inc(windows_moved, BODIES)

        mean_ready = sem("mean_ready")
        centred = sem("centred")
        squared = sem("squared")
        variance_ready = sem("variance_ready")
        std_ready = sem("std_ready")
        inverse_ready = sem("inverse_ready")
        normed = sem("normed")

        def norm_pe(pe, nth, n, ready, source):
            pe.wait_ge(ready, n + 1)
            nc.tensor.matmul(ps[6][:, :], mean_m, source[:, :], start=True, stop=True).then_inc(mean_ready, 1)
            pe.wait_ge(squared, nth + 1)
            nc.tensor.matmul(ps[7][:, :], mean_m, sqr[:, :], start=True, stop=True).then_inc(variance_ready, 1)

        def norm_act(act, nth):
            act.wait_ge(centred, nth + 1)
            act.activation(sqr[:, :], cen[:, :], ACT.Square).then_inc(squared, 1)
            act.wait_ge(variance_ready, nth + 1)
            act.activation(std[:, :], ps[7][:, :], ACT.Sqrt, bias=eps[:, :]).then_inc(std_ready, 1)

        def norm_dve(dve, nth, source, to):
            dve.wait_ge(mean_ready, nth + 1)
            dve.tensor_tensor(cen[:, :], source[:, :], ps[6][:, :], ALU.subtract).then_inc(centred, 1)
            dve.wait_ge(std_ready, nth + 1)
            dve.reciprocal(inv[:, :], std[:, :]).then_inc(inverse_ready, 1)
            dve.wait_ge(inverse_ready, nth + 1)
            dve.tensor_tensor(to[:, :], cen[:, :], inv[:, :], ALU.mult).then_inc(normed, 1)

        def one_hot(dve, out_ap, sc):
            return dve.tensor_tensor(out_ap, iota_w.unsqueeze(1).broadcast_to([P, G, W]),
                                     rel[:, ds(sc, 1), :].rearrange("p s g -> p (s g)").unsqueeze(2)
                                     .broadcast_to([P, G, W]), ALU.is_equal)


        edges_loaded = [sem(f"edges_loaded{k}") for k in range(U)]
        hot0 = sem("hot0")
        summed0 = sem("summed0")
        added0 = sem("added0")
        windows0 = sem("windows0")
        with nc.Block("layer0_edges") as block:
            @block.sync
            def _(sp):
                total = all_bodies(sp)
                sp.sem_inc(summed0, U)
                with sp.Fori(0, total, BODIES) as first, sp.Fori(0, BODIES) as i:
                    for k in range(U):
                        s = (first + i) * U + k
                        at = sp.value_load(start[0:1, ds(i * U + k, 1)], min_val=0, max_val=edge_attr.shape[0] - SC)
                        sp.wait_ge(summed0, s + 1)
                        sp.sem_inc(sp_waited, 1)
                        sp.dma_start(rows[:, k, 0:G * D],
                                     edge_attr[ds(at, SC), :].rearrange("(p g) f -> p (g f)", g=G)
                                     ).then_inc(edges_loaded[k], 16)

            @block.vector
            def _(dve):
                total = all_bodies(dve)
                dve.sem_inc(added0, U)
                windows_reset(dve, windows0)
                dve.wait_ge(windows0, 2)
                with dve.Fori(0, total, BODIES) as first:
                    with dve.Fori(0, BODIES) as i:
                        for k in range(U):
                            s = (first + i) * U + k
                            dve.wait_ge(summed0, s + 1)
                            one_hot(dve, onehot[:, k, :, :], i * U + k).then_inc(hot0, 1)
                        for k in range(U):
                            s = (first + i) * U + k
                            at = dve.value_load(base[0:1, ds(i * U + k, 1)], min_val=0, max_val=NODES - W)
                            dve.wait_ge(summed0, s + U + 1)
                            dve.wait_ge(added0, s + U)
                            dve.tensor_tensor(acc[:, ds(at, W)], acc[:, ds(at, W)], ps[k][:, 0:W],
                                              ALU.add).then_inc(added0, 1)
                    windows_move(dve, windows0)
                    dve.wait_ge(windows0, 2 * first + 2 * BODIES + 2)

            @block.tensor
            def _(pe):
                total = all_bodies(pe)
                with pe.Fori(0, total, BODIES) as first, pe.Fori(0, BODIES) as i:
                    for k in range(U):
                        s = (first + i) * U + k
                        pe.wait_ge(hot0, s + 1)
                        pe.wait_ge(edges_loaded[k], (first + i) * 16 + 16)
                        pe.wait_ge(added0, s + 1)
                        for g in range(G):
                            last = nc.tensor.matmul(ps[k][:, 0:W], rows[:, k, g * D:(g + 1) * D],
                                                    onehot[:, k, g, :], start=(g == 0), stop=(g == G - 1))
                        last.then_inc(summed0, 1)

        tile0 = sem("tile0")
        hidden_ps0 = sem("hidden_ps0")
        hidden0 = sem("hidden0")
        mlp0 = sem("mlp0")
        sum0 = sem("sum0")
        x_kept0 = sem("x_kept0")
        qkv_ps = sem("qkv_ps")
        qkv_rows = sem("qkv_rows")
        qkv_stored = sem("qkv_stored")
        with nc.Block("layer0_nodes") as block:
            @block.tensor
            def _(pe):
                with pe.Fori(0, NTILES) as n:
                    pe.wait_ge(tile0, n + 1)
                    for m in range(HIDDEN // P):
                        nc.tensor.matmul(ps[m][:, :], w1_sb[:, 0, m * P:(m + 1) * P], acc[:, ds(n * T, T)],
                                         start=True, stop=False)
                        nc.tensor.matmul(ps[m][:, :], w1_sb[:, 1, m * P:(m + 1) * P], x[:, ds(n * T, T)],
                                         start=False, stop=True).then_inc(hidden_ps0, 1)
                    for m in range(HIDDEN // P):
                        pe.wait_ge(hidden0, n * (HIDDEN // P) + m + 1)
                        last = nc.tensor.matmul(ps[4][:, :], w2_sb[:, m, :], hid[:, m, :],
                                                start=(m == 0), stop=(m == HIDDEN // P - 1))
                    last.then_inc(mlp0, 1)
                    norm_pe(pe, n, n, sum0, res)
                    pe.wait_ge(normed, n + 1)
                    for j in range(T // P):
                        nc.tensor.matmul(ps[j][:, 0:3 * D], y[:, j * P:(j + 1) * P], wqkv_sb[:, :],
                                         start=True, stop=False)
                        nc.tensor.matmul(ps[j][:, 0:3 * D], ones[0:1, 0:P], bqkv_sb[:, :],
                                         start=False, stop=True).then_inc(qkv_ps, 1)

            @block.scalar
            def _(act):
                with act.Fori(0, NTILES) as n:
                    for m in range(HIDDEN // P):
                        act.wait_ge(hidden_ps0, n * (HIDDEN // P) + m + 1)
                        act.activation(hid[:, m, :], ps[m][:, :], ACT.Relu, bias=v(f"b1_{m}")).then_inc(hidden0, 1)
                    norm_act(act, n)
                    act.wait_ge(normed, n + 1)
                    act.activation(x[:, ds(n * T, T)], y[:, :], ACT.Copy).then_inc(x_kept0, 1)
                    for j in range(T // P):
                        act.wait_ge(qkv_ps, n * (T // P) + j + 1)
                        act.activation(node_rows[:, j, :], ps[j][:, 0:3 * D], ACT.Copy).then_inc(qkv_rows, 1)

            @block.vector
            def _(dve):
                with dve.Fori(0, NTILES) as n:
                    dve.wait_ge(mlp0, n + 1)
                    dve.scalar_tensor_tensor(res[:, :], ps[4][:, :], v("b2"), x[:, ds(n * T, T)], ALU.add,
                                             ALU.add).then_inc(sum0, 1)
                    norm_dve(dve, n, res, y)

            @block.sync
            def _(sp):
                sp.sem_inc(tile0, 1)
                with sp.Fori(0, NTILES) as n:
                    sp.wait_ge(qkv_rows, n * (T // P) + T // P)
                    sp.sem_inc(sp_waited, 1)
                    sp.dma_start(q_rows[ds(n * T, T), :].rearrange("(j p) f -> p j f", p=P),
                                 node_rows[:, :, 0:D]).then_inc(qkv_stored, 16)
                    sp.dma_start(kv_rows[ds(n * T, T), :].rearrange("(j p) f -> p j f", p=P),
                                 node_rows[:, :, D:3 * D]).then_inc(qkv_stored, 16)
                    sp.wait_ge(qkv_stored, n * 32 + 32)
                    sp.sem_inc(sp_waited, 1)
                    sp.wait_ge(x_kept0, n + 1)
                    sp.sem_inc(tile0, 1)

        index_loaded1 = [sem(f"index_loaded1_{k}") for k in range(U)]
        window_loaded1 = [sem(f"window_loaded1_{k}") for k in range(U)]
        gathered1 = [sem(f"gathered1_{k}") for k in range(U)]
        hot1 = sem("hot1")
        turned1 = sem("turned1")
        hot_t1 = sem("hot_t1")
        expanded1 = sem("expanded1")
        product1 = sem("product1")
        score1 = sem("score1")
        clipped1 = sem("clipped1")
        weight1 = sem("weight1")
        message1 = sem("message1")
        summed1 = sem("summed1")
        added1 = sem("added1")
        windows1 = sem("windows1")
        window_ready1 = sem("window_ready1")
        z_zeroed = sem("z_zeroed")
        cleared1 = sem("cleared1")
        tables_zeroed = sem("tables_zeroed")
        Z = ps[7][0:HEADS, 0:W]
        with nc.Block("layer1_edges") as block:
            @block.sync
            def _(sp):
                total = all_bodies(sp)
                sp.sem_inc(message1, U)
                sp.sem_inc(expanded1, U)
                with sp.Fori(0, total, BODIES) as first:
                    sp.wait_ge(windows1, 2 * first + 2)
                    sp.sem_inc(sp_waited, 1)
                    with sp.Fori(0, BODIES) as i:
                        for k in range(U):
                            s = (first + i) * U + k
                            sp.wait_ge(message1, s + 1)
                            sp.sem_inc(sp_waited, 1)
                            sp.dma_start(index[:, k, :], src_index[:, ds((i * U + k) * G, G)]
                                         ).then_inc(index_loaded1[k], 16)
                            at = sp.value_load(base[0:1, ds(i * U + k, 1)], min_val=0, max_val=NODES - W)
                            sp.wait_ge(expanded1, s + 1)
                            sp.sem_inc(sp_waited, 1)
                            sp.dma_start(window[:, k, :], q_rows[ds(at, W), :]).then_inc(window_loaded1[k], 16)

            @block.gpsimd
            def _(pool):
                total = all_bodies(pool)
                with pool.Fori(0, total) as j:
                    for k in range(U):
                        pool.wait_ge(index_loaded1[k], j * 16 + 16)
                        pool.sem_inc(pool_waited, 1)
                        for g in range(G):
                            pool.indirect_dma_start(rows[:, k, g * 2 * D:(g + 1) * 2 * D], None, kv_rows[:, :],
                                                    bass.IndirectOffsetOnAxis(ap=index[:, k, g:g + 1], axis=0)
                                                    ).then_inc(gathered1[k], 16)

            @block.scalar
            def _(act):
                total = all_bodies(act)
                act.sem_inc(hot_t1, 2)
                for t in range(TABLES):
                    act.dma_start(table[t].rearrange("(j p) f -> p j f", p=P),
                                  zeros[:, :].unsqueeze(1).broadcast_to([P, NODES // P + 2, D])
                                  ).then_inc(tables_zeroed, 16)
                with act.Fori(0, total) as j:
                    def turn(k):
                        act.wait_ge(turned1, j * U + k + 1)
                        act.wait_ge(expanded1, j * U + k + 1)
                        act.activation(onehot_t[:, k, :], ps[k % 2][0:W, :], ACT.Copy).then_inc(hot_t1, 1)

                    def exp(k):
                        act.wait_ge(clipped1, j * U + k + 1)
                        act.wait_ge(summed1, j * U + k + 1)
                        act.activation(weight[:, k, :], clipped[:, k, :], ACT.Exp).then_inc(weight1, 1)

                    turn(0)
                    turn(1)
                    turn(2)
                    exp(0)
                    turn(3)
                    exp(1)
                    exp(2)
                    exp(3)
                act.wait_ge(tables_zeroed, 16 * TABLES)

            @block.vector
            def _(dve):
                total = all_bodies(dve)
                dve.sem_inc(product1, 2)
                dve.sem_inc(added1, 2)
                dve.memset(acc[:, :], 0.0).then_inc(cleared1, 1)
                windows_reset(dve, windows1)
                dve.wait_ge(windows1, 2)
                dve.wait_ge(cleared1, 1)
                with dve.Fori(0, total, BODIES) as first:
                    with dve.Fori(0, BODIES) as i:
                        def hot(k):
                            s = (first + i) * U + k
                            dve.wait_ge(summed1, s + 1)
                            one_hot(dve, onehot[:, k, :, :], i * U + k).then_inc(hot1, 1)

                        def scores(k):
                            s = (first + i) * U + k
                            dve.wait_ge(expanded1, s + U + 1)
                            dve.wait_ge(gathered1[k], (first + i) * 16 * G + 16 * G)
                            dve.tensor_tensor(prod[:, k, :].rearrange("p (g f) -> p g f", g=G),
                                              ps[2 + k % 2][:, :].rearrange("p (g f) -> p g f", g=G),
                                              rows[:, k, :].rearrange("p (g f) -> p g f", g=G)[:, :, 0:D],
                                              ALU.mult).then_inc(product1, 1)
                            dve.wait_ge(product1, s + 3)
                            dve.tensor_reduce(score[:, k, :], prod[:, k, :].rearrange("p (h c) -> p h c", c=HEAD),
                                              AX.X, ALU.add).then_inc(score1, 1)
                            dve.wait_ge(score1, s + 1)
                            dve.tensor_scalar(clipped[:, k, :], score[:, k, :], CLIP, -CLIP, ALU.min,
                                              ALU.max).then_inc(clipped1, 1)

                        def message(k):
                            s = (first + i) * U + k
                            dve.wait_ge(weight1, s + 1)
                            for g in range(G):
                                last = dve.tensor_tensor(
                                    prod[:, k, g * D:(g + 1) * D].rearrange("p (h c) -> p h c", c=HEAD),
                                    rows[:, k, g * 2 * D + D:(g + 1) * 2 * D].rearrange("p (h c) -> p h c", c=HEAD),
                                    weight[:, k, g * HEADS:(g + 1) * HEADS].unsqueeze(2)
                                    .broadcast_to([P, HEADS, HEAD]), ALU.mult)
                            last.then_inc(message1, 1)

                        def add(k):
                            s = (first + i) * U + k
                            at = dve.value_load(base[0:1, ds(i * U + k, 1)], min_val=0, max_val=NODES - W)
                            dve.wait_ge(summed1, s + U + 1)
                            dve.wait_ge(added1, s + 2)
                            dve.tensor_tensor(acc[:, ds(at, W)], acc[:, ds(at, W)], ps[4 + k % 2][:, 0:W],
                                              ALU.add).then_inc(added1, 1)

                        for k in range(U):
                            hot(k)
                        scores(0)
                        for k in range(1, U):
                            scores(k)
                            message(k - 1)
                            if k >= 2:
                                add(k - 2)
                        message(U - 1)
                        add(U - 2)
                        add(U - 1)
                    windows_move(dve, windows1)
                    dve.wait_ge(windows1, 2 * first + 2 * BODIES + 2)

            @block.tensor
            def _(pe):
                total = all_bodies(pe)
                pe.sem_inc(summed1, U)
                nc.tensor.matmul(Z, zeros[:, 0:HEADS], zeros[:, 0:W], start=True, stop=False, skip_group_check=True)
                with pe.Fori(0, total) as j:
                    def turn(k):
                        pe.wait_ge(hot1, j * U + k + 1)
                        pe.wait_ge(hot_t1, j * U + k + 1)
                        for g in range(G):
                            last = nc.tensor.transpose(ps[k % 2][0:W, g * P:(g + 1) * P], onehot[:, k, g, :], ident)
                        last.then_inc(turned1, 1)

                    def expand(k):
                        pe.wait_ge(hot_t1, j * U + k + 3)
                        pe.wait_ge(window_loaded1[k], j * 16 + 16)
                        pe.wait_ge(product1, j * U + k + 1)
                        for g in range(G):
                            last = nc.tensor.matmul(ps[2 + k % 2][:, g * P:(g + 1) * P],
                                                    onehot_t[:, k, g * P:(g + 1) * P], window[:, k, :],
                                                    start=True, stop=True)
                        last.then_inc(expanded1, 1)

                    def window_sum(k):
                        pe.wait_ge(message1, j * U + k + U + 1)
                        pe.wait_ge(added1, j * U + k + 1)
                        for g in range(G):
                            nc.tensor.matmul(ps[4 + k % 2][:, 0:W], prod[:, k, g * D:(g + 1) * D],
                                             onehot[:, k, g, :], start=(g == 0), stop=(g == G - 1))
                        for g in range(G):
                            last = nc.tensor.matmul(Z, weight[:, k, g * HEADS:(g + 1) * HEADS], onehot[:, k, g, :],
                                                    start=False, stop=False, skip_group_check=True)
                        last.then_inc(summed1, 1)

                    turn(0)
                    turn(1)
                    expand(0)
                    turn(2)
                    expand(1)
                    turn(3)
                    expand(2)
                    window_sum(0)
                    expand(3)
                    window_sum(1)
                    window_sum(2)
                    window_sum(3)

        tile1 = sem("tile1")
        z_summed = sem("z_summed")
        z_spread = sem("z_spread")
        heads1 = sem("heads1")
        out_ps1 = sem("out_ps1")
        att_bias1 = sem("att_bias1")
        sum1 = sem("sum1")
        scaled1a = sem("scaled1a")
        ffn_ps1 = sem("ffn_ps1")
        ffn_relu1 = sem("ffn_relu1")
        ffn_out1 = sem("ffn_out1")
        sum1b = sem("sum1b")
        scaled1b = sem("scaled1b")
        sum1c = sem("sum1c")
        x_kept1 = sem("x_kept1")
        ab_ps = sem("ab_ps")
        ab_rows = sem("ab_rows")
        ab_stored = sem("ab_stored")
        with nc.Block("layer1_nodes") as block:
            @block.tensor
            def _(pe):
                pe.wait_ge(z_summed, 1)
                nc.tensor.matmul(ps[6][:, 0:1], head_of, z_heads[:, :], start=True, stop=True).then_inc(z_spread, 1)
                with pe.Fori(0, NTILES) as n:
                    pe.wait_ge(heads1, n + 1)
                    nc.tensor.matmul(ps[0][:, :], wo_sb[:, :], tmp[:, :], start=True, stop=True).then_inc(out_ps1, 1)
                    norm_pe(pe, NTILES + 3 * n, n, sum1, res)
                    pe.wait_ge(scaled1a, n + 1)
                    nc.tensor.matmul(ps[1][:, :], aw1_sb[:, :], y2[:, :], start=True, stop=True).then_inc(ffn_ps1, 1)
                    pe.wait_ge(ffn_relu1, n + 1)
                    nc.tensor.matmul(ps[2][:, :], aw2_sb[:, :], hid[:, 0, :], start=True, stop=True).then_inc(ffn_out1, 1)
                    norm_pe(pe, NTILES + 3 * n + 1, n, sum1b, res)
                    norm_pe(pe, NTILES + 3 * n + 2, n, sum1c, res)
                    pe.wait_ge(normed, NTILES + 3 * n + 3)
                    for j in range(T // P):
                        nc.tensor.matmul(ps[j][:, 0:2 * D], y[:, j * P:(j + 1) * P], we1_sb[:, :],
                                         start=True, stop=False)
                        nc.tensor.matmul(ps[j][:, 0:2 * D], ones[0:1, 0:P], be1_sb[:, :],
                                         start=False, stop=True).then_inc(ab_ps, 1)

            @block.scalar
            def _(act):
                with act.Fori(0, NTILES) as n:
                    norm_act(act, NTILES + 3 * n)
                    act.wait_ge(ffn_ps1, n + 1)
                    act.activation(hid[:, 0, :], ps[1][:, :], ACT.Relu, bias=v("a_b1")).then_inc(ffn_relu1, 1)
                    norm_act(act, NTILES + 3 * n + 1)
                    norm_act(act, NTILES + 3 * n + 2)
                    act.wait_ge(normed, NTILES + 3 * n + 3)
                    act.activation(x[:, ds(n * T, T)], y[:, :], ACT.Copy).then_inc(x_kept1, 1)
                    for j in range(T // P):
                        act.wait_ge(ab_ps, n * (T // P) + j + 1)
                        act.activation(node_rows[:, j, 0:2 * D], ps[j][:, 0:2 * D], ACT.Copy).then_inc(ab_rows, 1)

            @block.vector
            def _(dve):
                dve.tensor_reduce(z_heads[:, :], Z, AX.X, ALU.add).then_inc(z_summed, 1)
                dve.wait_ge(z_spread, 1)
                dve.reciprocal(inv_z[:, :], ps[6][:, 0:1]).then_inc(z_summed, 1)
                dve.wait_ge(z_summed, 2)
                with dve.Fori(0, NTILES) as n:
                    dve.wait_ge(tile1, n + 1)
                    dve.tensor_scalar(tmp[:, :], acc[:, ds(n * T, T)], inv_z[:, :], None, ALU.mult).then_inc(heads1, 1)
                    dve.wait_ge(out_ps1, n + 1)
                    dve.scalar_tensor_tensor(res[:, :], ps[0][:, :], v("bO"), x[:, ds(n * T, T)], ALU.add,
                                             ALU.add).then_inc(sum1, 1)
                    norm_dve(dve, NTILES + 3 * n, res, y)
                    dve.wait_ge(normed, NTILES + 3 * n + 1)
                    dve.tensor_scalar(y2[:, :], y[:, :], v("ln1_g"), v("ln1_b"), ALU.mult, ALU.add).then_inc(scaled1a, 1)
                    dve.wait_ge(scaled1a, n + 1)
                    dve.wait_ge(ffn_out1, n + 1)
                    dve.scalar_tensor_tensor(res[:, :], ps[2][:, :], v("a_b2"), y2[:, :], ALU.add,
                                             ALU.add).then_inc(sum1b, 1)
                    norm_dve(dve, NTILES + 3 * n + 1, res, y)
                    dve.wait_ge(normed, NTILES + 3 * n + 2)
                    dve.tensor_scalar(y2[:, :], y[:, :], v("ln2_g"), v("ln2_b"), ALU.mult, ALU.add).then_inc(scaled1b, 1)
                    dve.wait_ge(scaled1b, n + 1)
                    dve.tensor_tensor(res[:, :], y2[:, :], x[:, ds(n * T, T)], ALU.add).then_inc(sum1c, 1)
                    norm_dve(dve, NTILES + 3 * n + 2, res, y)

            @block.sync
            def _(sp):
                sp.sem_inc(tile1, 1)
                with sp.Fori(0, NTILES) as n:
                    sp.wait_ge(ab_rows, n * (T // P) + T // P)
                    sp.sem_inc(sp_waited, 1)
                    sp.dma_start(a_rows[ds(n * T, T), :].rearrange("(j p) f -> p j f", p=P),
                                 node_rows[:, :, 0:D]).then_inc(ab_stored, 16)
                    sp.dma_start(b_rows[ds(n * T, T), :].rearrange("(j p) f -> p j f", p=P),
                                 node_rows[:, :, D:2 * D]).then_inc(ab_stored, 16)
                    sp.wait_ge(ab_stored, n * 32 + 32)
                    sp.sem_inc(sp_waited, 1)
                    sp.wait_ge(x_kept1, n + 1)
                    sp.sem_inc(tile1, 1)

        index_loaded2 = [sem(f"index_loaded2_{k}") for k in range(U)]
        window_loaded2 = [sem(f"window_loaded2_{k}") for k in range(U)]
        gathered2 = [sem(f"gathered2_{k}") for k in range(U)]
        hot2 = sem("hot2")
        turned2 = sem("turned2")
        hot_t2 = sem("hot_t2")
        expanded2 = sem("expanded2")
        pair2 = sem("pair2")
        relu2 = sem("relu2")
        split2 = sem("split2")
        summed2 = sem("summed2")
        added2 = sem("added2")
        windows2 = sem("windows2")
        cleared2 = sem("cleared2")
        deg_zeroed = sem("deg_zeroed")
        DEG = ps[7][:, 0:HI]
        with nc.Block("layer2_edges") as block:
            @block.sync
            def _(sp):
                total = all_bodies(sp)
                sp.sem_inc(relu2, U)
                sp.sem_inc(expanded2, U)
                with sp.Fori(0, total, BODIES) as first:
                    sp.wait_ge(windows2, 3 * first + 2)
                    sp.sem_inc(sp_waited, 1)
                    with sp.Fori(0, BODIES) as i:
                        for k in range(U):
                            s = (first + i) * U + k
                            sp.wait_ge(relu2, s + 1)
                            sp.sem_inc(sp_waited, 1)
                            sp.dma_start(index[:, k, :], src_index[:, ds((i * U + k) * G, G)]
                                         ).then_inc(index_loaded2[k], 16)
                            at = sp.value_load(base[0:1, ds(i * U + k, 1)], min_val=0, max_val=NODES - W)
                            sp.wait_ge(expanded2, s + 1)
                            sp.sem_inc(sp_waited, 1)
                            sp.dma_start(window[:, k, :], b_rows[ds(at, W), :]).then_inc(window_loaded2[k], 16)

            @block.gpsimd
            def _(pool):
                total = all_bodies(pool)
                with pool.Fori(0, total) as j:
                    for k in range(U):
                        pool.wait_ge(index_loaded2[k], j * 16 + 16)
                        pool.sem_inc(pool_waited, 1)
                        for g in range(G):
                            pool.indirect_dma_start(rows[:, k, g * D:(g + 1) * D], None, a_rows[:, :],
                                                    bass.IndirectOffsetOnAxis(ap=index[:, k, g:g + 1], axis=0)
                                                    ).then_inc(gathered2[k], 16)

            @block.scalar
            def _(act):
                total = all_bodies(act)
                act.sem_inc(hot_t2, 2)
                with act.Fori(0, total) as j:
                    def turn(k):
                        act.wait_ge(turned2, j * U + k + 1)
                        act.wait_ge(expanded2, j * U + k + 1)
                        act.activation(onehot_t[:, k, :], ps[k % 2][0:W, :], ACT.Copy).then_inc(hot_t2, 1)

                    def relu(k):
                        act.wait_ge(pair2, j * U + k + 3)
                        act.wait_ge(summed2, j * U + k + 1)
                        act.activation(rows[:, k, G * D:2 * G * D], prod[:, k, :], ACT.Relu).then_inc(relu2, 1)

                    turn(0)
                    turn(1)
                    turn(2)
                    relu(0)
                    turn(3)
                    relu(1)
                    relu(2)
                    relu(3)

            @block.vector
            def _(dve):
                total = all_bodies(dve)
                dve.sem_inc(pair2, 2)
                dve.sem_inc(added2, 4)
                dve.memset(acc[:, :], 0.0).then_inc(cleared2, 1)
                windows_reset(dve, windows2)
                dve.wait_ge(windows2, 2)
                dve.wait_ge(cleared2, 1)
                with dve.Fori(0, total, BODIES) as first:
                    with dve.Fori(0, BODIES) as i:
                        def hot(k):
                            s = (first + i) * U + k
                            dve.wait_ge(summed2, s + 1)
                            one_hot(dve, onehot[:, k, :, :], i * U + k).then_inc(hot2, 1)

                        def split(k):
                            col = (i * U + k) * G
                            dve.tensor_tensor(lo_hot[:, k, :, :], iota_p.unsqueeze(1).broadcast_to([P, G, P]),
                                              src_lo[:, ds(col, G)].unsqueeze(2).broadcast_to([P, G, P]),
                                              ALU.is_equal)
                            dve.tensor_tensor(hi_hot[:, k, :, :], iota_p[:, 0:HI].unsqueeze(1).broadcast_to([P, G, HI]),
                                              src_hi[:, ds(col, G)].unsqueeze(2).broadcast_to([P, G, HI]),
                                              ALU.is_equal).then_inc(split2, 1)

                        def pair(k):
                            s = (first + i) * U + k
                            dve.wait_ge(expanded2, s + U + 1)
                            dve.wait_ge(gathered2[k], (first + i) * 16 * G + 16 * G)
                            dve.wait_ge(relu2, s + 1)
                            dve.tensor_tensor(prod[:, k, :], ps[2 + k % 2][:, :], rows[:, k, 0:G * D],
                                              ALU.add).then_inc(pair2, 1)

                        def add(k):
                            s = (first + i) * U + k
                            at = dve.value_load(base[0:1, ds(i * U + k, 1)], min_val=0, max_val=NODES - W)
                            dve.wait_ge(summed2, s + U + 1)
                            dve.wait_ge(added2, 2 * s + 4)
                            dve.tensor_tensor(acc[:, ds(at, W)], acc[:, ds(at, W)], ps[4 + k % 2][:, 0:W],
                                              ALU.add).then_inc(added2, 1)
                            dve.tensor_tensor(count[:, ds(at, W)], count[:, ds(at, W)], ps[4 + k % 2][0:1, W:2 * W],
                                              ALU.add).then_inc(added2, 1)

                        for k in range(U):
                            hot(k)
                            split(k)
                        pair(0)
                        for k in range(1, U):
                            pair(k)
                            if k >= 2:
                                add(k - 2)
                        add(U - 2)
                        add(U - 1)
                    windows_move(dve, windows2)
                    dve.memset(src_hi[:, :], -1.0).then_inc(windows2, BODIES)
                    dve.wait_ge(windows2, 3 * first + 3 * BODIES + 2)

            @block.tensor
            def _(pe):
                total = all_bodies(pe)
                pe.sem_inc(summed2, U)
                nc.tensor.matmul(DEG, zeros[:, :], zeros[:, 0:HI], start=True, stop=False, skip_group_check=True)
                with pe.Fori(0, total) as j:
                    def turn(k):
                        pe.wait_ge(hot2, j * U + k + 1)
                        pe.wait_ge(hot_t2, j * U + k + 1)
                        for g in range(G):
                            last = nc.tensor.transpose(ps[k % 2][0:W, g * P:(g + 1) * P], onehot[:, k, g, :], ident)
                        last.then_inc(turned2, 1)

                    def expand(k):
                        pe.wait_ge(hot_t2, j * U + k + 3)
                        pe.wait_ge(window_loaded2[k], j * 16 + 16)
                        pe.wait_ge(pair2, j * U + k + 1)
                        for g in range(G):
                            last = nc.tensor.matmul(ps[2 + k % 2][:, g * P:(g + 1) * P],
                                                    onehot_t[:, k, g * P:(g + 1) * P], window[:, k, :],
                                                    start=True, stop=True)
                        last.then_inc(expanded2, 1)

                    def window_sum(k):
                        pe.wait_ge(split2, j * U + k + 1)
                        for g in range(G):
                            nc.tensor.matmul(DEG, lo_hot[:, k, g, :], hi_hot[:, k, g, :],
                                             start=False, stop=False, skip_group_check=True)
                        pe.wait_ge(relu2, j * U + k + U + 1)
                        pe.wait_ge(added2, 2 * (j * U + k) + 2)
                        for g in range(G):
                            nc.tensor.matmul(ps[4 + k % 2][:, 0:W], rows[:, k, (G + g) * D:(G + g + 1) * D],
                                             onehot[:, k, g, :], start=(g == 0), stop=(g == G - 1))
                        for g in range(G):
                            last = nc.tensor.matmul(ps[4 + k % 2][0:1, W:2 * W], ones[:, 0:1], onehot[:, k, g, :],
                                                    start=(g == 0), stop=(g == G - 1))
                        last.then_inc(summed2, 1)

                    turn(0)
                    turn(1)
                    expand(0)
                    turn(2)
                    expand(1)
                    turn(3)
                    expand(2)
                    window_sum(0)
                    expand(3)
                    window_sum(1)
                    window_sum(2)
                    window_sum(3)

        tile2 = sem("tile2")
        degree = sem("degree")
        degree_sqrt = sem("degree_sqrt")
        agg_ps2 = sem("agg_ps2")
        agg2 = sem("agg2")
        hidden_ps2 = sem("hidden_ps2")
        hidden2 = sem("hidden2")
        mlp2 = sem("mlp2")
        twice2 = sem("twice2")
        sum2 = sem("sum2")
        x_kept2 = sem("x_kept2")
        y_ps = sem("y_ps")
        y_scaled = sem("y_scaled")
        y_stored = sem("y_stored")
        with nc.Block("layer2_nodes") as block:
            @block.tensor
            def _(pe):
                with pe.Fori(0, NTILES) as n:
                    pe.wait_ge(tile2, n + 1)
                    nc.tensor.matmul(ps[0][:, :], we2_sb[:, :], acc[:, ds(n * T, T)], start=True, stop=False)
                    nc.tensor.matmul(ps[0][:, :], be2_sb[:, :], count[:, ds(n * T, T)],
                                     start=False, stop=True).then_inc(agg_ps2, 1)
                    pe.wait_ge(agg2, n + 1)
                    nc.tensor.matmul(ps[1][:, :], wn1_sb[:, 0, :], x[:, ds(n * T, T)], start=True, stop=False)
                    nc.tensor.matmul(ps[1][:, :], wn1_sb[:, 1, :], tmp[:, :],
                                     start=False, stop=True).then_inc(hidden_ps2, 1)
                    pe.wait_ge(hidden2, n + 1)
                    nc.tensor.matmul(ps[2][:, :], wn2_sb[:, :], hid[:, 0, :], start=True, stop=True).then_inc(mlp2, 1)
                    norm_pe(pe, 4 * NTILES + n, n, sum2, res)
                    pe.wait_ge(normed, 4 * NTILES + n + 1)
                    for j in range(T // P):
                        nc.tensor.transpose(ps[2 + j][:, 0:P], y[:, j * P:(j + 1) * P],
                                            ident).then_inc(y_ps, 1)

            @block.scalar
            def _(act):
                act.wait_ge(degree, 1)
                act.activation(dis_raw[:, :], deg_sb[:, :], ACT.Sqrt).then_inc(degree_sqrt, 1)
                with act.Fori(0, NTILES) as n:
                    act.wait_ge(agg_ps2, n + 1)
                    act.activation(tmp[:, :], ps[0][:, :], ACT.Copy).then_inc(agg2, 1)
                    act.wait_ge(hidden_ps2, n + 1)
                    act.activation(hid[:, 0, :], ps[1][:, :], ACT.Relu, bias=v("bn1")).then_inc(hidden2, 1)
                    norm_act(act, 4 * NTILES + n)
                    act.wait_ge(normed, 4 * NTILES + n + 1)
                    act.activation(x[:, ds(n * T, T)], y[:, :], ACT.Copy).then_inc(x_kept2, 1)

            @block.vector
            def _(dve):
                dve.tensor_scalar(deg_sb[:, :], DEG, 1.0, None, ALU.max).then_inc(degree, 1)
                dve.tensor_scalar(deg_pos[:, :], DEG, 0.0, None, ALU.is_gt).then_inc(degree, 1)
                dve.wait_ge(degree_sqrt, 1)
                dve.reciprocal(dis_raw[:, :], dis_raw[:, :]).then_inc(degree, 1)
                dve.wait_ge(degree, 3)
                dve.tensor_tensor(dis[:, :], dis_raw[:, :], deg_pos[:, :], ALU.mult).then_inc(degree, 1)
                dve.wait_ge(degree, 4)
                with dve.Fori(0, NTILES) as n:
                    dve.wait_ge(tile2, n + 1)
                    dve.tensor_scalar(y2[:, :], x[:, ds(n * T, T)], 2.0, v("bn2"), ALU.mult, ALU.add).then_inc(twice2, 1)
                    dve.wait_ge(twice2, n + 1)
                    dve.wait_ge(mlp2, n + 1)
                    dve.tensor_tensor(res[:, :], ps[2][:, :], y2[:, :], ALU.add).then_inc(sum2, 1)
                    norm_dve(dve, 4 * NTILES + n, res, y)
                    for j in range(T // P):
                        dve.wait_ge(y_ps, n * (T // P) + j + 1)
                        dve.tensor_scalar(node_rows[:, j, 0:D], ps[2 + j][:, 0:P],
                                          dis[:, ds(n * (T // P) + j, 1)], None, ALU.mult).then_inc(y_scaled, 1)

            @block.sync
            def _(sp):
                sp.sem_inc(tile2, 1)
                with sp.Fori(0, NTILES) as n:
                    sp.wait_ge(y_scaled, n * (T // P) + T // P)
                    sp.sem_inc(sp_waited, 1)
                    sp.dma_start(y_rows[ds(n * T, T), :].rearrange("(j p) f -> p j f", p=P),
                                 node_rows[:, :, 0:D]).then_inc(y_stored, 16)
                    sp.wait_ge(y_stored, n * 16 + 16)
                    sp.sem_inc(sp_waited, 1)
                    sp.wait_ge(x_kept2, n + 1)
                    sp.sem_inc(tile2, 1)

        window_loaded3 = [sem(f"window_loaded3_{k}") for k in range(U)]
        scattered = [sem(f"scattered{k}") for k in range(U)]
        landed = [sem(f"landed{k}") for k in range(U)]
        picked3 = sem("picked3")
        hot3 = sem("hot3")
        spread3 = sem("spread3")
        same3 = sem("same3")
        earlier3 = sem("earlier3")
        follows3 = sem("follows3")
        to_spare3 = sem("to_spare3")
        shift3 = sem("shift3")
        target3 = sem("target3")
        counted3 = sem("counted3")
        counts3 = sem("counts3")
        expanded3 = sem("expanded3")
        value3 = sem("value3")
        windows3 = sem("windows3")
        with nc.Block("layer3_edges") as block:
            @block.sync
            def _(sp):
                total = all_bodies(sp)
                for k in range(U):
                    sp.sem_inc(landed[k], 1)
                with sp.Fori(0, total) as j:
                    for k in range(U):
                        sp.wait_ge(scattered[k], j * 16 * G + 16 * G)
                        sp.sem_inc(landed[k], 1)

            @block.scalar
            def _(act):
                total = all_bodies(act)
                act.sem_inc(counts3, 2)
                act.sem_inc(value3, 2)
                act.sem_inc(expanded3, U)
                with act.Fori(0, total, BODIES) as first:
                  act.wait_ge(windows3, 2 * first + 2)
                  with act.Fori(0, BODIES) as i:
                    j = first + i
                    for k in range(U):
                        at = act.value_load(base[0:1, ds(i * U + k, 1)], min_val=0, max_val=NODES - W)
                        act.wait_ge(expanded3, j * U + k + 1)
                        act.dma_start(window[:, k, :], y_rows[ds(at, W), :]).then_inc(window_loaded3[k], 16)

                    def counts(k):
                        act.wait_ge(counted3, j * U + k + U + 1)
                        act.wait_ge(expanded3, j * U + k + 1)
                        act.activation(onehot_t[:, k, :], ps[2 + k % 2][0:W, :], ACT.Copy).then_inc(counts3, 1)

                    def values(k):
                        act.wait_ge(expanded3, j * U + k + U + 1)
                        act.wait_ge(landed[k], j + 1)
                        act.activation(rows[:, k, 0:G * D], ps[4 + k % 2][:, :], ACT.Copy).then_inc(value3, 1)

                    counts(0)
                    for k in range(1, U):
                        counts(k)
                        values(k - 1)
                    values(U - 1)

            @block.gpsimd
            def _(pool):
                total = all_bodies(pool)
                with pool.Fori(0, total) as j:
                    for k in range(U):
                        pool.wait_ge(value3, j * U + k + 3)
                        pool.wait_ge(target3, j * U + k + 1)
                        pool.sem_inc(pool_waited, 1)
                        pool.wait_ge(landed[(k + 2) % U], j + 1 + (1 if k >= 2 else 0))
                        pool.sem_inc(pool_waited, 1)
                        for g in range(G):
                            pool.indirect_dma_start(table[(k % 2) * G + g][:, :],
                                                    bass.IndirectOffsetOnAxis(ap=index[:, k, g:g + 1], axis=0),
                                                    rows[:, k, g * D:(g + 1) * D], None,
                                                    compute_op=ALU.add).then_inc(scattered[k], 16)

            @block.vector
            def _(dve):
                total = all_bodies(dve)
                dve.sem_inc(same3, 2)
                dve.sem_inc(earlier3, 1)
                windows_reset(dve, windows3)
                dve.wait_ge(windows3, 2)
                with dve.Fori(0, total, BODIES) as first:
                    with dve.Fori(0, BODIES) as i:
                        def hot(k):
                            s = (first + i) * U + k
                            dve.wait_ge(counted3, s + 1)
                            dve.tensor_copy(src_s[:, k, :], src_num[:, ds((i * U + k) * G, G)]).then_inc(picked3, 1)
                            one_hot(dve, onehot_b[:, k, :, :], i * U + k).then_inc(hot3, 1)

                        def equal(k):
                            s = (first + i) * U + k
                            dve.wait_ge(picked3, s + 1)
                            dve.wait_ge(spread3, s + 1)
                            dve.tensor_tensor(same[:, k, :, :], ps[k % 2][:, :].rearrange("p (g e) -> p g e", g=G),
                                              src_s[:, k, :].unsqueeze(2).broadcast_to([P, G, P]),
                                              ALU.is_equal).then_inc(same3, 1)

                        def targets(k):
                            s = (first + i) * U + k
                            dve.wait_ge(same3, s + 3)
                            for g in range(G):
                                dve.wait_ge(earlier3, s * G + g + 1)
                                dve.tensor_tensor_reduce(masked[:, :], same[:, k, g, :], lower, 1.0, 0.0, ALU.mult,
                                                         ALU.add, earlier[:, k, g:g + 1]).then_inc(earlier3, 1)
                            dve.tensor_scalar(to_spare[:, k, :], src_s[:, k, :], -1.0, spare_row[:, :], ALU.mult,
                                              ALU.add).then_inc(to_spare3, 1)
                            dve.wait_ge(earlier3, s * G + G + 1)
                            dve.wait_ge(to_spare3, s + 1)
                            dve.scalar_tensor_tensor(shift_by[:, k, :], earlier[:, k, :], 0.0, to_spare[:, k, :],
                                                     ALU.is_gt, ALU.mult).then_inc(shift3, 1)
                            dve.wait_ge(shift3, s + 1)
                            dve.wait_ge(landed[k], first + i + 1)
                            dve.tensor_tensor(index[:, k, :], src_s[:, k, :], shift_by[:, k, :],
                                              ALU.add).then_inc(target3, 1)

                        hot(0)
                        hot(1)
                        equal(0)
                        targets(0)
                        hot(2)
                        equal(1)
                        targets(1)
                        hot(3)
                        equal(2)
                        targets(2)
                        equal(3)
                        targets(3)
                    windows_move(dve, windows3)
                    dve.wait_ge(windows3, 2 * first + 2 * BODIES + 2)

            @block.tensor
            def _(pe):
                total = all_bodies(pe)
                pe.sem_inc(counted3, U)
                with pe.Fori(0, total) as j:
                    def spread(k):
                        pe.wait_ge(picked3, j * U + k + 1)
                        pe.wait_ge(same3, j * U + k + 1)
                        for g in range(G):
                            last = nc.tensor.matmul(ps[k % 2][:, g * P:(g + 1) * P],
                                                    src_s[:, k, g:g + 1].broadcast_to([P, P]), ident,
                                                    start=True, stop=True)
                        last.then_inc(spread3, 1)

                    def counts(k):
                        pe.wait_ge(same3, j * U + k + 3)
                        pe.wait_ge(hot3, j * U + k + 1)
                        pe.wait_ge(counts3, j * U + k + 1)
                        for g in range(G):
                            last = nc.tensor.matmul(ps[2 + k % 2][0:W, g * P:(g + 1) * P], onehot_b[:, k, g, :],
                                                    same[:, k, g, :], start=True, stop=True)
                        last.then_inc(counted3, 1)

                    def expand(k):
                        pe.wait_ge(counts3, j * U + k + 3)
                        pe.wait_ge(window_loaded3[k], j * 16 + 16)
                        pe.wait_ge(value3, j * U + k + 1)
                        for g in range(G):
                            last = nc.tensor.matmul(ps[4 + k % 2][:, g * P:(g + 1) * P],
                                                    onehot_t[:, k, g * P:(g + 1) * P], window[:, k, :],
                                                    start=True, stop=True)
                        last.then_inc(expanded3, 1)

                    spread(0)
                    spread(1)
                    counts(0)
                    for k in range(2, U):
                        spread(k)
                        counts(k - 1)
                        expand(k - 2)
                    counts(U - 1)
                    expand(U - 2)
                    expand(U - 1)


        tile3 = sem("tile3")
        tables_loaded = sem("tables_loaded")
        diag3 = sem("diag3")
        agg_ps3 = sem("agg_ps3")
        agg3 = sem("agg3")
        lin3 = sem("lin3")
        sum3 = sem("sum3")
        out_stored = sem("out_stored")
        parts = rows[:, :, :].rearrange("p u c -> p (u c)").rearrange("p (t j f) -> p t j f", t=TABLES, f=D)
        diag = hid[:, 1, :]
        with nc.Block("layer3_nodes") as block:
            @block.tensor
            def _(pe):
                with pe.Fori(0, NTILES) as n:
                    pe.wait_ge(tables_loaded, n * 16 * TABLES + 16 * TABLES)
                    for j in range(T // P):
                        pe.wait_ge(diag3, n * (T // P) + j + 1)
                        for t in range(TABLES):
                            last = nc.tensor.matmul(ps[0][:, j * P:(j + 1) * P], parts[:, t, j, :],
                                                    diag[:, j * P:(j + 1) * P], start=(t == 0), stop=(t == TABLES - 1))
                    last.then_inc(agg_ps3, 1)
                    pe.wait_ge(agg3, n + 1)
                    nc.tensor.matmul(ps[1][:, :], w3t_sb[:, :], tmp[:, :], start=True, stop=True).then_inc(lin3, 1)
                    norm_pe(pe, 5 * NTILES + n, n, sum3, res)

            @block.scalar
            def _(act):
                with act.Fori(0, NTILES) as n:
                    act.wait_ge(agg_ps3, n + 1)
                    act.activation(tmp[:, :], ps[0][:, :], ACT.Copy).then_inc(agg3, 1)
                    norm_act(act, 5 * NTILES + n)

            @block.vector
            def _(dve):
                with dve.Fori(0, NTILES) as n:
                    dve.wait_ge(tile3, n + 1)
                    for j in range(T // P):
                        dve.tensor_scalar(diag[:, j * P:(j + 1) * P], ident, dis[:, ds(n * (T // P) + j, 1)], None,
                                          ALU.mult).then_inc(diag3, 1)
                    dve.wait_ge(lin3, n + 1)
                    dve.scalar_tensor_tensor(res[:, :], ps[1][:, :], v("b3"), x[:, ds(n * T, T)], ALU.add,
                                             ALU.add).then_inc(sum3, 1)
                    norm_dve(dve, 5 * NTILES + n, res, y)

            @block.sync
            def _(sp):
                sp.sem_inc(tile3, 1)
                with sp.Fori(0, NTILES) as n:
                    sp.wait_ge(tile3, n + 1)
                    sp.sem_inc(sp_waited, 1)
                    for t in range(TABLES):
                        sp.dma_start(parts[:, t, :, :],
                                     table[t][ds(n * T, T), :].rearrange("(j p) f -> p j f", p=P)
                                     ).then_inc(tables_loaded, 16)
                    sp.wait_ge(normed, 5 * NTILES + n + 1)
                    sp.sem_inc(sp_waited, 1)
                    sp.dma_start(out[:, ds(n * T, T)], y[:, :]).then_inc(out_stored, 16)
                    sp.wait_ge(out_stored, n * 16 + 16)
                    sp.sem_inc(tile3, 1)
                sp.wait_ge(out_stored, 16 * NTILES)


def layouts(inputs):
    import numpy as np
    a = {k: np.asarray(x) for k, x in inputs.items()}
    n, e = a["x"].shape[0], a["src"].shape[0]
    nodes, scs = sizes(n, e)
    first = np.arange(scs) * SC
    start = np.minimum(first, e - SC).astype(np.int32)
    edge = (start[:, None] + np.arange(SC)[None, :])
    own = edge >= first[:, None]
    place = lambda m: np.ascontiguousarray(m.reshape(scs, P, G).transpose(1, 0, 2).reshape(P, scs * G))
    minus = np.int32(-1)
    by_rows = a["dst"][np.where(own, edge, e - 1)]
    xt = np.zeros((P, nodes), np.float32)
    xt[:, :n] = a["x"].T
    ramp = np.broadcast_to(np.arange(P, dtype=np.float32), (P, P))
    consts = np.concatenate([np.eye(P, dtype=np.float32), np.tril(np.ones((P, P), np.float32), -1),
                             np.full((P, P), 1.0 / D, np.float32), ramp[:, :W], ramp,
                             nodes + np.arange(P, dtype=np.float32)[:, None],
                             (np.arange(P)[:, None] == np.arange(P)[None, :] // HEAD).astype(np.float32)], axis=1)
    b1 = a["L0_gnn_b1"].reshape(4, P)
    vectors = np.stack([*b1, a["L0_gnn_b2"], a["L1_gnn_bO"], a["L1_gnn_ln1_g"], a["L1_gnn_ln1_b"], a["L1_gnn_b1"],
                        a["L1_gnn_b2"], a["L1_gnn_ln2_g"], a["L1_gnn_ln2_b"], a["L2_gnn_bn1"], a["L2_gnn_bn2"],
                        a["L3_gnn_b"]], axis=1)
    be1 = a["L2_gnn_be1"]
    return {
        "xT": xt, "edge_attr": a["edge_attr_128"],
        "src_index": place(np.where(own, a["src"][edge], np.int32(0))),
        "src_id": place(np.where(own, a["src"][edge], minus)),
        "dst_id": place(np.where(own, a["dst"][edge], minus)),
        "dst_rows": np.ascontiguousarray(by_rows.reshape(4, scs // 4, SC).transpose(1, 0, 2)),
        "edge_start": start[None, :], "consts": np.ascontiguousarray(consts),
        "w1": a["L0_gnn_W1"], "w2": a["L0_gnn_W2"],
        "wqkv": np.concatenate([a["L1_gnn_WQ"], a["L1_gnn_WK"], a["L1_gnn_WV"]], axis=1),
        "wo": a["L1_gnn_WO"], "aw1": a["L1_gnn_W1"], "aw2": a["L1_gnn_W2"],
        "we1": a["L2_gnn_We1"], "we2": a["L2_gnn_We2"], "wn1": a["L2_gnn_Wn1"], "wn2": a["L2_gnn_Wn2"],
        "w3t": np.ascontiguousarray(a["L3_gnn_W"].T), "vectors": np.ascontiguousarray(vectors),
        "row_bqkv": np.concatenate([a["L1_gnn_bQ"], a["L1_gnn_bK"], a["L1_gnn_bV"]])[None, :],
        "row_be1": np.concatenate([np.zeros_like(be1), be1])[None, :], "row_be2": a["L2_gnn_be2"][None, :],
    }


def kernel(**inputs):
    import numpy as np
    import concourse.bacc as bacc
    from concourse import mybir as mb
    from concourse.bass_utils import run_bass_kernel_spmd

    n = np.asarray(inputs["x"]).shape[0]
    arrays = layouts(inputs)
    nc = bacc.Bacc("TRN2", target_bir_lowering=False, num_devices=1)
    args = {}
    for name, a in arrays.items():
        args[name] = nc.dram_tensor(f"in_{name}", a.shape, mb.dt.from_np(a.dtype), kind="ExternalInput").ap()
    nodes = arrays["xT"].shape[1]
    args["out"] = nc.dram_tensor("out_0", (P, nodes), mb.dt.float32, kind="ExternalOutput").ap()
    gnn_program(nc, **args)
    r = run_bass_kernel_spmd(nc, [{f"in_{name}": a for name, a in arrays.items()}], core_ids=[0])
    return np.ascontiguousarray(r.results[0]["out_0"][:, :n].T)
```

```python
from contextlib import ExitStack

import concourse.bass as bass
from concourse import mybir

P = 128
D = 128
HEADS = 8
HEAD = D // HEADS
HIDDEN = 512
G = 4
SC = G * P
W = 32
U = 4
T = 256
TJ = T // P
LANES = 2
TABLES = 8
LN_EPS = 1e-5
CLIP = 5.0

F32 = mybir.dt.float32
BF16 = mybir.dt.bfloat16
I32 = mybir.dt.int32
ALU = mybir.AluOpType
ACT = mybir.ActivationFunctionType
AX = mybir.AxisListType
ds = bass.ds

VECTORS = ["b1_0", "b1_1", "b1_2", "b1_3", "b2", "bO", "ln1_g", "ln1_b", "a_b1", "a_b2", "ln2_g", "ln2_b",
           "bn1", "bn2", "b3"]
VEC = {name: i for i, name in enumerate(VECTORS)}


def sizes(n_nodes, n_edges):
    node_cols = -(-(n_nodes + W) // (LANES * T)) * LANES * T
    superchunks = -(-n_edges // SC)
    superchunks = -(-superchunks // U) * U
    return node_cols, superchunks


def gnn_program(nc, xT, edge_attr, src_index, src_id, dst_id, dst_rows, edge_start, consts,
                w1, w2, wqkv, wo, aw1, aw2, we1, we2, wn1, wn2, w3t, vectors, row_bqkv, row_be1, row_be2, out):
    NODES = xT.shape[1]
    SCS = edge_start.shape[1]
    BODIES = SCS // U
    NTILES = NODES // T
    STEPS = NTILES // LANES
    HI = NODES // P
    SPR = SCS // 4
    assert SPR <= P and SCS % U == 0 and HI <= P
    PASSES_MAX = NODES // W + 1
    ctx = ExitStack()
    with ctx:
        def sb(name, shape, dt=F32):
            return ctx.enter_context(nc.sbuf_tensor(name, shape, dt))

        def sem(name):
            return ctx.enter_context(nc.semaphore(name))

        x = sb("x", [P, NODES])
        acc = sb("acc", [P, NODES])
        count = sb("count", [1, NODES])
        src_num = sb("src_num", [P, SCS * G])
        src_hi = sb("src_hi", [P, SCS * G], BF16)
        src_lo = sb("src_lo", [P, SCS * G], BF16)
        rel0 = sb("rel0", [P, SCS, G])
        rel = sb("rel", [P, SCS, G])
        base0 = sb("base0", [1, SCS])
        base = sb("base", [1, SCS], I32)
        start = sb("start", [1, SCS], I32)
        pass_bodies = sb("pass_bodies", [1, 1], I32)
        cst = sb("cst", [P, 5 * P + W + 1])
        ident = cst[:, 0:P]
        lower = cst[:, P:2 * P]
        centre_m = cst[:, 2 * P:3 * P]
        iota_w = cst[:, 3 * P:3 * P + W]
        iota_p = cst[:, 3 * P + W:4 * P + W]
        spare_row = cst[:, 4 * P + W:4 * P + W + 1]
        head_of = cst[0:HEADS, 4 * P + W + 1:5 * P + W + 1]
        ones = sb("ones", [P, P])
        zeros = sb("zeros", [P, P])
        mean_col = sb("mean_col", [P, 1])
        eps = sb("eps", [P, 1])
        w1_sb = sb("w1_sb", [P, 2, HIDDEN])
        w2_sb = sb("w2_sb", [P, HIDDEN // P, D])
        wqkv_sb = sb("wqkv_sb", [P, 3 * D])
        wo_sb = sb("wo_sb", [P, D])
        aw1_sb = sb("aw1_sb", [P, D])
        aw2_sb = sb("aw2_sb", [P, D])
        we1_sb = sb("we1_sb", [P, 2 * D])
        we2_sb = sb("we2_sb", [P, D])
        wn1_sb = sb("wn1_sb", [P, 2, D])
        wn2_sb = sb("wn2_sb", [P, D])
        w3t_sb = sb("w3t_sb", [P, D])
        vec = sb("vec", [P, len(VECTORS)])
        bqkv_sb = sb("bqkv_sb", [1, 3 * D])
        be1_sb = sb("be1_sb", [1, 2 * D])
        be2_sb = sb("be2_sb", [1, D])

        def v(name):
            return vec[:, VEC[name]:VEC[name] + 1]

        rows = sb("rows", [P, U, G * 2 * D])
        onehot = sb("onehot", [P, U, G, W])
        turned = sb("turned", [P, U, SC])
        onehot_t = turned[0:W, :, 0:SC // 2].bitcast(BF16)
        window = sb("window", [W, U, 3 * D], BF16)
        ones_b = sb("ones_b", [P, 1], BF16)
        ident_b = sb("ident_b", [P, P], BF16)
        turned_ps = [ctx.enter_context(nc.psum_tensor(f"turned_ps{i}", [P, 2 * SC], BF16)) for i in range(2)]
        prod = sb("prod", [P, U, G * D])
        score = sb("score", [P, U, G * HEADS])
        clipped = sb("clipped", [P, U, G * HEADS])
        weight = sb("weight", [P, U, G * HEADS])
        weight_x = sb("weight_x", [P, U, G * D])
        index = sb("index", [P, U, G], I32)
        lo_hot = sb("lo_hot", [P, U, G, P], BF16)
        hi_hot = sb("hi_hot", [P, U, G, HI], BF16)
        same = lo_hot
        onehot_b = sb("onehot_b", [P, U, G, W], BF16)
        src_s = sb("src_s", [P, U, G])
        masked = sb("masked", [P, P])
        earlier = sb("earlier", [P, U, G])
        follows = sb("follows", [P, U, G])
        to_spare = sb("to_spare", [P, U, G])
        shift_by = sb("shift_by", [P, U, G])

        hid = [turned[:, 2 * l:2 * l + 2, :].rearrange("p a n -> p (a n)").rearrange("p (m n) -> p m n", n=T)
               for l in range(LANES)]
        tmp = [prod[:, 0, l * T:(l + 1) * T] for l in range(LANES)]
        res = [prod[:, 1, l * T:(l + 1) * T] for l in range(LANES)]
        cen = [prod[:, 2, l * T:(l + 1) * T] for l in range(LANES)]
        sqr = [prod[:, 3, l * T:(l + 1) * T] for l in range(LANES)]
        std = [sb(f"std{l}", [P, TJ]) for l in range(LANES)]
        inv = [sb(f"inv{l}", [P, TJ]) for l in range(LANES)]
        y = [sb(f"y{l}", [P, T]) for l in range(LANES)]
        y2 = [sb(f"y2{l}", [P, T]) for l in range(LANES)]
        node_rows = [sb(f"node_rows{l}", [P, TJ, 3 * D]) for l in range(LANES)]
        bias_qkv = sb("bias_qkv", [P, 3 * D])
        bias_ab = sb("bias_ab", [P, 2 * D])
        sqrt_of = sb("sqrt_of", [1, 2])
        parts_b = [sb(f"parts_b{l}", [P, TJ, 3 * D], BF16) for l in range(LANES)]
        rest = [sb(f"rest{l}", [P, TJ, D]) for l in range(LANES)]
        z_heads = sb("z_heads", [HEADS, 1])
        inv_z = sb("inv_z", [P, 1])
        dis = sb("dis", [P, HI])
        deg_sb = sb("deg_sb", [P, HI])
        deg_pos = sb("deg_pos", [P, HI])
        dis_raw = sb("dis_raw", [P, HI])
        low_sb = sb("low_sb", [P, 8])
        small = sb("small", [1, 4])
        small_i = sb("small_i", [1, 4], I32)

        ps = [turned_ps[i][:, :].bitcast(F32) for i in range(2)]
        ps += [ctx.enter_context(nc.psum_tensor(f"ps{i}", [P, 512], F32)) for i in range(2, 8)]

        sp_waited = sem("sp_waited")
        pool_waited = sem("pool_waited")

        q_rows = nc.dram_tensor("q_rows", (NODES, 3 * D), BF16, kind="Internal").ap()
        kv_rows = nc.dram_tensor("kv_rows", (NODES, 2 * D), F32, kind="Internal").ap()
        a_rows = nc.dram_tensor("a_rows", (NODES, D), F32, kind="Internal").ap()
        b_rows = nc.dram_tensor("b_rows", (NODES, 3 * D), BF16, kind="Internal").ap()
        y_rows = nc.dram_tensor("y_rows", (NODES, 3 * D), BF16, kind="Internal").ap()
        table = [nc.dram_tensor(f"table{i}", (NODES + 2 * P, D), F32, kind="Internal").ap() for i in range(TABLES)]

        loaded = sem("loaded")
        rows_loaded = sem("rows_loaded")
        const_set = sem("const_set")
        dst_minmax = sem("dst_minmax")
        low_ready = sem("low_ready")
        range_max = sem("range_max")
        passes_f = sem("passes_f")
        passes_i = sem("passes_i")
        src_split = sem("src_split")
        wq_scaled = sem("wq_scaled")
        biases_spread = sem("biases_spread")
        prep_dma = 18
        with nc.Block("prepare") as block:
            ids = rows[:, :, :].rearrange("p u c -> p (u c)").bitcast(I32)
            dst_i = ids[0:SPR, 0:4 * SC].rearrange("p (c e) -> p c e", c=4)
            ids2 = turned[:, :, :].rearrange("p u c -> p (u c)").bitcast(I32)
            dst_e = ids2[:, 0:SCS * G]
            src_e = acc[:, 0:SCS * G].bitcast(I32)
            src_w = acc[:, SCS * G:2 * SCS * G].bitcast(I32)

            @block.sync
            def _(sp):
                sp.dma_start(dst_i, dst_rows).then_inc(rows_loaded, 16)
                sp.dma_start(cst[:, :], consts).then_inc(rows_loaded, 16)
                sp.dma_start(dst_e, dst_id).then_inc(rows_loaded, 16)
                sp.dma_start(src_e, src_id).then_inc(rows_loaded, 16)
                for tile, dram in ((x, xT), (start, edge_start), (wqkv_sb, wqkv), (wo_sb, wo), (aw1_sb, aw1),
                                   (aw2_sb, aw2), (we2_sb, we2), (wn2_sb, wn2), (w3t_sb, w3t), (vec, vectors),
                                   (bqkv_sb, row_bqkv), (be1_sb, row_be1), (be2_sb, row_be2)):
                    sp.dma_start(tile[:, :], dram).then_inc(loaded, 16)
                sp.dma_start(we1_sb[:, 0:D], we1[0:D, :]).then_inc(loaded, 16)
                sp.dma_start(we1_sb[:, D:2 * D], we1[D:2 * D, :]).then_inc(loaded, 16)
                sp.dma_start(w1_sb[:, :, :], w1.rearrange("(b p) n -> p b n", p=P)).then_inc(loaded, 16)
                sp.dma_start(w2_sb[:, :, :], w2.rearrange("(b p) n -> p b n", p=P)).then_inc(loaded, 16)
                sp.dma_start(wn1_sb[:, :, :], wn1.rearrange("(b p) n -> p b n", p=P)).then_inc(loaded, 16)
                sp.wait_ge(loaded, 16 * prep_dma)

            @block.vector
            def _(dve):
                dve.memset(ones[:, :], 1.0).then_inc(const_set, 1)
                dve.memset(zeros[:, :], 0.0).then_inc(const_set, 1)
                dve.memset(eps[:, :], LN_EPS).then_inc(const_set, 1)
                dve.memset(mean_col[:, :], 1.0 / D).then_inc(const_set, 1)
                dve.memset(sqrt_of[:, :], 1.0).then_inc(const_set, 1)
                dve.memset(count[:, :], 0.0).then_inc(const_set, 1)
                dve.memset(ones_b[:, :], 1.0).then_inc(const_set, 1)
                dve.wait_ge(rows_loaded, 64)
                dve.tensor_copy(ident_b[:, :], ident).then_inc(const_set, 1)
                dve.tensor_reduce(low_sb[0:SPR, 0:4], dst_i, AX.X, ALU.min).then_inc(dst_minmax, 1)
                dve.tensor_reduce(low_sb[0:SPR, 4:8], dst_i, AX.X, ALU.max).then_inc(dst_minmax, 1)
                dve.wait_ge(dst_minmax, 2)
                dve.tensor_tensor(low_sb[0:SPR, 4:8], low_sb[0:SPR, 4:8], low_sb[0:SPR, 0:4],
                                  ALU.subtract).then_inc(dst_minmax, 1)
                pad_row = rel[:, :, :].rearrange("p s g -> p (s g)")
                dve.tensor_scalar(pad_row, src_e, 0.0, float(NODES + P + 1), ALU.is_lt, ALU.mult).then_inc(src_split, 1)
                dve.wait_ge(src_split, 1)
                dve.tensor_tensor(src_num[:, :], src_e, pad_row, ALU.add).then_inc(src_split, 1)
                dve.tensor_scalar(src_w, src_e, 7, None, ALU.arith_shift_right).then_inc(src_split, 1)
                dve.wait_ge(src_split, 3)
                dve.tensor_copy(src_hi[:, :], src_w).then_inc(src_split, 1)
                dve.wait_ge(src_split, 4)
                dve.tensor_scalar(src_w, src_e, 127, None, ALU.bitwise_and).then_inc(src_split, 1)
                dve.wait_ge(src_split, 5)
                dve.tensor_copy(src_lo[:, :], src_w).then_inc(src_split, 1)
                dve.wait_ge(low_ready, 1)
                dve.tensor_copy(base0[:, :], ps[0][0:1, 0:SCS]).then_inc(range_max, 1)
                dve.tensor_reduce(small[:, 0:1], ps[1][0:1, 0:SCS], AX.X, ALU.max).then_inc(range_max, 1)
                dve.tensor_copy(rel0[:, :, :], dst_e.rearrange("p (s g) -> p s g", g=G)).then_inc(range_max, 1)
                dve.wait_ge(range_max, 3)
                dve.tensor_tensor(rel0[:, :, :], rel0[:, :, :],
                                  ps[2][:, 0:SCS].unsqueeze(2).broadcast_to([P, SCS, G]),
                                  ALU.subtract).then_inc(range_max, 1)
                dve.tensor_copy(small_i[:, 0:1], small[:, 0:1]).then_inc(passes_f, 1)
                dve.wait_ge(passes_f, 1)
                shift = W.bit_length() - 1
                dve.tensor_scalar(small_i[:, 1:2], small_i[:, 0:1], shift, None,
                                  ALU.arith_shift_right).then_inc(passes_f, 1)
                dve.wait_ge(passes_f, 2)
                dve.tensor_scalar(pass_bodies[:, :], small_i[:, 1:2], float(BODIES), float(BODIES), ALU.mult,
                                  ALU.add).then_inc(passes_i, 1)
                dve.wait_ge(loaded, 16 * prep_dma)
                dve.tensor_scalar(wqkv_sb[:, 0:D], wqkv_sb[:, 0:D], HEAD ** -0.5, None, ALU.mult).then_inc(wq_scaled, 1)
                dve.tensor_scalar(bqkv_sb[:, 0:D], bqkv_sb[:, 0:D], HEAD ** -0.5, None, ALU.mult).then_inc(wq_scaled, 1)
                dve.wait_ge(src_split, 6)
                dve.memset(acc[:, :], 0.0).then_inc(wq_scaled, 1)
                dve.wait_ge(biases_spread, 1)
                dve.tensor_copy(bias_qkv[:, :], ps[3][:, 0:3 * D]).then_inc(wq_scaled, 1)
                dve.tensor_copy(bias_ab[:, :], ps[4][:, 0:2 * D]).then_inc(wq_scaled, 1)

            @block.tensor
            def _(pe):
                pe.wait_ge(const_set, 6)
                pe.wait_ge(rows_loaded, 64)
                pe.wait_ge(dst_minmax, 3)
                for c in range(4):
                    cols = slice(c * SPR, (c + 1) * SPR)
                    nc.tensor.matmul(ps[0][0:1, cols], low_sb[0:SPR, c:c + 1], ident[0:SPR, 0:SPR],
                                     start=True, stop=True)
                    nc.tensor.matmul(ps[1][0:1, cols], low_sb[0:SPR, 4 + c:5 + c], ident[0:SPR, 0:SPR],
                                     start=True, stop=True)
                    last = nc.tensor.matmul(ps[2][:, cols], low_sb[0:SPR, c:c + 1].broadcast_to([SPR, P]),
                                            ident[0:SPR, 0:SPR], start=True, stop=True)
                last.then_inc(low_ready, 1)
                pe.wait_ge(loaded, 16 * prep_dma)
                pe.wait_ge(wq_scaled, 2)
                nc.tensor.matmul(ps[3][:, 0:3 * D], ones[0:1, 0:P], bqkv_sb[:, :], start=True, stop=True)
                nc.tensor.matmul(ps[4][:, 0:2 * D], ones[0:1, 0:P], be1_sb[:, :],
                                 start=True, stop=True).then_inc(biases_spread, 1)

        def all_bodies(eng):
            return eng.value_load(pass_bodies[0:1, 0:1], min_val=BODIES, max_val=BODIES * PASSES_MAX)

        def window_starts(eng_type, i):
            return nc.values_load_multi_w_load_instructions(base[0:1, ds(i * U, U)], engines=(eng_type,),
                                                            min_val=0, max_val=NODES - W)[1]

        def windows_reset(dve, windows_set):
            dve.tensor_copy(rel[:, :, :], rel0[:, :, :]).then_inc(windows_set, 1)
            dve.tensor_scalar(base[:, :], base0[:, :], float(NODES - W), None, ALU.min).then_inc(windows_set, 1)

        def windows_move(dve, windows_moved):
            dve.tensor_scalar(rel[:, :, :], rel[:, :, :], float(W), None, ALU.subtract).then_inc(windows_moved, BODIES)
            dve.tensor_scalar(base[:, :], base[:, :], float(W), float(NODES - W), ALU.add,
                              ALU.min).then_inc(windows_moved, BODIES)

        def bank(l, b):
            return ps[4 * l + b]

        def columns(c):
            return ds(c * T, T)

        centred_ps = sem("centred_ps")
        squared = sem("squared")
        centred = sem("centred")
        variance_ps = sem("variance_ps")
        std_ready = sem("std_ready")
        inverse_ready = sem("inverse_ready")
        inverse_ps = sem("inverse_ps")
        normed = sem("normed")

        def norm_pe(pe, nth, ready, count_of):
            for l in range(LANES):
                pe.wait_ge(ready, count_of(l) + 1)
                nc.tensor.matmul(bank(l, 1)[:, 0:T], centre_m, res[l], start=True, stop=True).then_inc(centred_ps, 1)
            for l in range(LANES):
                pe.wait_ge(squared, nth + l + 1)
                for j in range(TJ):
                    last = nc.tensor.matmul(bank(l, 2)[:, j:j + 1], sqr[l][:, j * P:(j + 1) * P], mean_col[:, :],
                                            start=True, stop=True)
                last.then_inc(variance_ps, 1)
            for l in range(LANES):
                pe.wait_ge(inverse_ready, nth + l + 1)
                for j in range(TJ):
                    last = nc.tensor.matmul(bank(l, 3)[:, j * P:(j + 1) * P],
                                            inv[l][:, j:j + 1].broadcast_to([P, P]), ident, start=True, stop=True)
                last.then_inc(inverse_ps, 1)

        def norm_act(act, nth):
            for l in range(LANES):
                act.wait_ge(centred_ps, nth + l + 1)
                act.activation(sqr[l], bank(l, 1)[:, 0:T], ACT.Square).then_inc(squared, 1)
                act.activation(cen[l], bank(l, 1)[:, 0:T], ACT.Copy).then_inc(centred, 1)
            for l in range(LANES):
                act.wait_ge(variance_ps, nth + l + 1)
                act.activation(std[l][:, :], bank(l, 2)[:, 0:TJ], ACT.Sqrt, bias=eps[:, :]).then_inc(std_ready, 1)

        def norm_dve(dve, nth):
            for l in range(LANES):
                dve.wait_ge(std_ready, nth + l + 1)
                dve.reciprocal(inv[l][:, :], std[l][:, :]).then_inc(inverse_ready, 1)
            for l in range(LANES):
                dve.wait_ge(centred, nth + l + 1)
                dve.wait_ge(inverse_ps, nth + l + 1)
                dve.tensor_tensor(y[l][:, :], cen[l], bank(l, 3)[:, 0:T], ALU.mult).then_inc(normed, 1)

        split_step = sem("split_step")
        SPLITS = 4

        def split_rows(pool, done, l, col):
            part = lambda q: parts_b[l][:, :, q * D:(q + 1) * D]
            whole = node_rows[l][:, :, col:col + D]
            pool.tensor_copy(part(0), whole).then_inc(split_step, 1)
            pool.wait_ge(split_step, done * SPLITS + 1)
            pool.sem_inc(pool_waited, 1)
            pool.tensor_tensor(rest[l][:, :, :], whole, part(0), ALU.subtract).then_inc(split_step, 1)
            pool.wait_ge(split_step, done * SPLITS + 2)
            pool.sem_inc(pool_waited, 1)
            pool.tensor_copy(part(1), rest[l][:, :, :]).then_inc(split_step, 1)
            pool.wait_ge(split_step, done * SPLITS + 3)
            pool.sem_inc(pool_waited, 1)
            pool.tensor_tensor(part(2), rest[l][:, :, :], part(1), ALU.subtract).then_inc(split_step, 1)

        def load_sqrt_table(act):
            act.activation(sqrt_of[:, 1:2], sqrt_of[:, 0:1], ACT.Sqrt)

        def one_hot(dve, to, i, first=0, number=U):
            return dve.tensor_tensor(to[:, first:first + number, :, :].rearrange("p u g w -> p (u g) w"),
                                     iota_w.unsqueeze(1).broadcast_to([P, number * G, W]),
                                     rel[:, ds(i * U + first, number), :].rearrange("p s g -> p (s g)").unsqueeze(2)
                                     .broadcast_to([P, number * G, W]), ALU.is_equal)


        edges_loaded = [sem(f"edges_loaded{k}") for k in range(U)]
        hot0 = sem("hot0")
        summed0 = sem("summed0")
        added0 = sem("added0")
        windows0 = sem("windows0")
        with nc.Block("layer0_edges") as block:
            @block.sync
            def _(sp):
                total = all_bodies(sp)
                sp.sem_inc(summed0, U)
                with sp.Fori(0, total, BODIES) as first, sp.Fori(0, BODIES) as i:
                    for k in range(U):
                        s = (first + i) * U + k
                        at = sp.value_load(start[0:1, ds(i * U + k, 1)], min_val=0, max_val=edge_attr.shape[0] - SC)
                        sp.wait_ge(summed0, s + 1)
                        sp.sem_inc(sp_waited, 1)
                        sp.dma_start(rows[:, k, 0:G * D],
                                     edge_attr[ds(at, SC), :].rearrange("(p g) f -> p (g f)", g=G)
                                     ).then_inc(edges_loaded[k], 16)

            @block.vector
            def _(dve):
                total = all_bodies(dve)
                dve.sem_inc(added0, U)
                windows_reset(dve, windows0)
                dve.wait_ge(windows0, 2)
                with dve.Fori(0, total, BODIES) as first:
                    with dve.Fori(0, BODIES) as i:
                        at = window_starts(mybir.EngineType.DVE, i)
                        dve.wait_ge(summed0, (first + i) * U + U)
                        one_hot(dve, onehot, i).then_inc(hot0, U)
                        for k in range(U):
                            s = (first + i) * U + k
                            dve.wait_ge(summed0, s + U + 1)
                            dve.wait_ge(added0, s + U)
                            dve.tensor_tensor(acc[:, ds(at[k], W)], acc[:, ds(at[k], W)], ps[k][:, 0:W],
                                              ALU.add).then_inc(added0, 1)
                    windows_move(dve, windows0)
                    dve.wait_ge(windows0, 2 * first + 2 * BODIES + 2)

            @block.tensor
            def _(pe):
                total = all_bodies(pe)
                with pe.Fori(0, total, BODIES) as first, pe.Fori(0, BODIES) as i:
                    for k in range(U):
                        s = (first + i) * U + k
                        pe.wait_ge(hot0, s + 1)
                        pe.wait_ge(edges_loaded[k], (first + i) * 16 + 16)
                        pe.wait_ge(added0, s + 1)
                        for g in range(G):
                            last = nc.tensor.matmul(ps[k][:, 0:W], rows[:, k, g * D:(g + 1) * D],
                                                    onehot[:, k, g, :], start=(g == 0), stop=(g == G - 1))
                        last.then_inc(summed0, 1)

        tile0 = sem("tile0")
        hidden_ps0 = sem("hidden_ps0")
        hidden0 = sem("hidden0")
        mlp0 = sem("mlp0")
        sum0 = sem("sum0")
        x_kept = sem("x_kept")
        qkv_ps = sem("qkv_ps")
        qkv_rows = sem("qkv_rows")
        qkv_stored = sem("qkv_stored")
        MB = HIDDEN // P
        with nc.Block("layer0_nodes") as block:
            @block.tensor
            def _(pe):
                with pe.Fori(0, STEPS) as n:
                    for l in range(LANES):
                        c = n * LANES + l
                        pe.wait_ge(tile0, c + 1)
                        for m in range(MB):
                            nc.tensor.matmul(bank(l, m)[:, 0:T], w1_sb[:, 0, m * P:(m + 1) * P], acc[:, columns(c)],
                                             start=True, stop=False)
                            nc.tensor.matmul(bank(l, m)[:, 0:T], w1_sb[:, 1, m * P:(m + 1) * P], x[:, columns(c)],
                                             start=False, stop=True).then_inc(hidden_ps0, 1)
                    for l in range(LANES):
                        for m in range(MB):
                            pe.wait_ge(hidden0, (n * LANES + l) * MB + m + 1)
                            last = nc.tensor.matmul(bank(l, 0)[:, 0:T], w2_sb[:, m, :], hid[l][:, m, :],
                                                    start=(m == 0), stop=(m == MB - 1))
                        last.then_inc(mlp0, 1)
                    norm_pe(pe, n * LANES, sum0, lambda l: n * LANES + l)
                    for l in range(LANES):
                        pe.wait_ge(normed, n * LANES + l + 1)
                        for j in range(TJ):
                            nc.tensor.matmul(bank(l, j)[:, 0:3 * D], y[l][:, j * P:(j + 1) * P], wqkv_sb[:, :],
                                             start=True, stop=True).then_inc(qkv_ps, 1)

            @block.scalar
            def _(act):
                with act.Fori(0, STEPS) as n:
                    load_sqrt_table(act)
                    for l in range(LANES):
                        for m in range(MB):
                            act.wait_ge(hidden_ps0, (n * LANES + l) * MB + m + 1)
                            act.activation(hid[l][:, m, :], bank(l, m)[:, 0:T], ACT.Relu,
                                           bias=v(f"b1_{m}")).then_inc(hidden0, 1)
                    norm_act(act, n * LANES)
                    for l in range(LANES):
                        act.wait_ge(normed, n * LANES + l + 1)
                        act.activation(x[:, columns(n * LANES + l)], y[l][:, :], ACT.Copy).then_inc(x_kept, 1)

            @block.vector
            def _(dve):
                with dve.Fori(0, STEPS) as n:
                    for l in range(LANES):
                        c = n * LANES + l
                        dve.wait_ge(mlp0, c + 1)
                        dve.scalar_tensor_tensor(res[l], bank(l, 0)[:, 0:T], v("b2"), x[:, columns(c)], ALU.add,
                                                 ALU.add).then_inc(sum0, 1)
                    norm_dve(dve, n * LANES)
                    for l in range(LANES):
                        for j in range(TJ):
                            dve.wait_ge(qkv_ps, (n * LANES + l) * TJ + j + 1)
                            dve.tensor_tensor(node_rows[l][:, j, :], bank(l, j)[:, 0:3 * D], bias_qkv[:, :],
                                              ALU.add).then_inc(qkv_rows, 1)

            @block.gpsimd
            def _(pool):
                with pool.Fori(0, STEPS) as n:
                    for l in range(LANES):
                        c = n * LANES + l
                        pool.wait_ge(qkv_rows, c * TJ + TJ)
                        pool.sem_inc(pool_waited, 1)
                        split_rows(pool, 0 + c, l, 0)

            @block.sync
            def _(sp):
                sp.sem_inc(tile0, LANES)
                with sp.Fori(0, STEPS) as n:
                    for l in range(LANES):
                        c = n * LANES + l
                        sp.wait_ge(qkv_rows, c * TJ + TJ)
                        sp.sem_inc(sp_waited, 1)
                        sp.wait_ge(split_step, (0 + c) * SPLITS + SPLITS)
                        sp.sem_inc(sp_waited, 1)
                        sp.dma_start(q_rows[columns(c), :].rearrange("(j p) f -> p j f", p=P),
                                     parts_b[l][:, :, :]).then_inc(qkv_stored, 16)
                        sp.dma_start(kv_rows[columns(c), :].rearrange("(j p) f -> p j f", p=P),
                                     node_rows[l][:, :, D:3 * D]).then_inc(qkv_stored, 16)
                        sp.wait_ge(qkv_stored, c * 32 + 32)
                        sp.sem_inc(sp_waited, 1)
                        sp.wait_ge(x_kept, c + 1)
                        sp.sem_inc(tile0, 1)

        index_loaded1 = [sem(f"index_loaded1_{k}") for k in range(U)]
        window_loaded1 = [sem(f"window_loaded1_{k}") for k in range(U)]
        gathered1 = [sem(f"gathered1_{k}") for k in range(U)]
        hot1 = sem("hot1")
        hot_f1 = sem("hot_f1")
        turned1 = sem("turned1")
        hot_t1 = sem("hot_t1")
        expanded1 = sem("expanded1")
        product1 = sem("product1")
        score1 = sem("score1")
        clipped1 = sem("clipped1")
        weight1 = sem("weight1")
        message1 = sem("message1")
        summed1 = sem("summed1")
        added1 = sem("added1")
        windows1 = sem("windows1")
        cleared1 = sem("cleared1")
        tables_zeroed = sem("tables_zeroed")
        Z = ps[7][0:HEADS, 0:W]
        with nc.Block("layer1_edges") as block:
            @block.sync
            def _(sp):
                total = all_bodies(sp)
                sp.sem_inc(message1, U)
                sp.sem_inc(expanded1, U)
                with sp.Fori(0, total, BODIES) as first:
                    sp.wait_ge(windows1, 2 * first + 2)
                    sp.sem_inc(sp_waited, 1)
                    with sp.Fori(0, BODIES) as i:
                        at = window_starts(mybir.EngineType.SP, i)
                        for k in range(U):
                            s = (first + i) * U + k
                            sp.wait_ge(message1, s + 1)
                            sp.sem_inc(sp_waited, 1)
                            sp.dma_start(index[:, k, :], src_index[:, ds((i * U + k) * G, G)]
                                         ).then_inc(index_loaded1[k], 16)
                            sp.wait_ge(expanded1, s + 1)
                            sp.sem_inc(sp_waited, 1)
                            sp.dma_start(window[:, k, :], q_rows[ds(at[k], W), :]).then_inc(window_loaded1[k], 16)

            @block.gpsimd
            def _(pool):
                total = all_bodies(pool)
                with pool.Fori(0, total) as j:
                    for k in range(U):
                        pool.wait_ge(index_loaded1[k], j * 16 + 16)
                        pool.sem_inc(pool_waited, 1)
                        for g in range(G):
                            pool.indirect_dma_start(rows[:, k, g * 2 * D:(g + 1) * 2 * D], None, kv_rows[:, :],
                                                    bass.IndirectOffsetOnAxis(ap=index[:, k, g:g + 1], axis=0)
                                                    ).then_inc(gathered1[k], 16)

            @block.scalar
            def _(act):
                total = all_bodies(act)
                act.sem_inc(hot_t1, 2)
                for t in range(TABLES):
                    act.dma_start(table[t].rearrange("(j p) f -> p j f", p=P),
                                  zeros[:, :].unsqueeze(1).broadcast_to([P, NODES // P + 2, D])
                                  ).then_inc(tables_zeroed, 16)
                with act.Fori(0, total) as j:
                    def turn(k):
                        act.wait_ge(turned1, j * U + k + 1)
                        act.wait_ge(expanded1, j * U + k + 1)
                        act.activation(onehot_t[:, k, :], turned_ps[k % 2][0:W, 0:SC], ACT.Copy).then_inc(hot_t1, 1)

                    def exp(k):
                        act.wait_ge(clipped1, j * U + k + 1)
                        act.wait_ge(summed1, j * U + k + 1)
                        act.activation(weight[:, k, :], clipped[:, k, :], ACT.Exp).then_inc(weight1, 1)

                    turn(0)
                    turn(1)
                    turn(2)
                    exp(0)
                    turn(3)
                    exp(1)
                    exp(2)
                    exp(3)
                act.wait_ge(tables_zeroed, 16 * TABLES)

            @block.vector
            def _(dve):
                total = all_bodies(dve)
                dve.sem_inc(product1, 2)
                dve.sem_inc(added1, 2)
                dve.memset(acc[:, :], 0.0).then_inc(cleared1, 1)
                windows_reset(dve, windows1)
                dve.wait_ge(windows1, 2)
                dve.wait_ge(cleared1, 1)
                with dve.Fori(0, total, BODIES) as first:
                    with dve.Fori(0, BODIES) as i:
                        at = window_starts(mybir.EngineType.DVE, i)
                        def scores(k):
                            s = (first + i) * U + k
                            dve.wait_ge(expanded1, s + U + 1)
                            dve.wait_ge(gathered1[k], (first + i) * 16 * G + 16 * G)
                            dve.tensor_tensor(prod[:, k, :].rearrange("p (g f) -> p g f", g=G),
                                              ps[2 + k % 2][:, :].rearrange("p (g f) -> p g f", g=G),
                                              rows[:, k, :].rearrange("p (g f) -> p g f", g=G)[:, :, 0:D],
                                              ALU.mult).then_inc(product1, 1)
                            dve.wait_ge(product1, s + 3)
                            dve.tensor_reduce(score[:, k, :], prod[:, k, :].rearrange("p (h c) -> p h c", c=HEAD),
                                              AX.X, ALU.add).then_inc(score1, 1)
                            dve.wait_ge(score1, s + 1)
                            dve.tensor_scalar(clipped[:, k, :], score[:, k, :], CLIP, -CLIP, ALU.min,
                                              ALU.max).then_inc(clipped1, 1)

                        def message(k):
                            s = (first + i) * U + k
                            dve.wait_ge(weight1, s + 1)
                            dve.tensor_tensor(
                                prod[:, k, :].rearrange("p (g h c) -> p g h c", g=G, c=HEAD),
                                rows[:, k, :].rearrange("p (g f) -> p g f", g=G)[:, :, D:2 * D]
                                .rearrange("p g (h c) -> p g h c", c=HEAD),
                                weight[:, k, :].rearrange("p (g h) -> p g h", g=G).unsqueeze(3)
                                .broadcast_to([P, G, HEADS, HEAD]), ALU.mult).then_inc(message1, 1)

                        def add(k):
                            s = (first + i) * U + k
                            dve.wait_ge(summed1, s + U + 1)
                            dve.wait_ge(added1, s + 2)
                            dve.tensor_tensor(acc[:, ds(at[k], W)], acc[:, ds(at[k], W)], ps[4 + k % 2][:, 0:W],
                                              ALU.add).then_inc(added1, 1)

                        dve.wait_ge(summed1, (first + i) * U + U)
                        one_hot(dve, onehot_b, i).then_inc(hot1, U)
                        one_hot(dve, onehot, i).then_inc(hot_f1, U)
                        scores(0)
                        for k in range(1, U):
                            scores(k)
                            message(k - 1)
                            if k >= 2:
                                add(k - 2)
                        message(U - 1)
                        add(U - 2)
                        add(U - 1)
                    windows_move(dve, windows1)
                    dve.wait_ge(windows1, 2 * first + 2 * BODIES + 2)

            @block.tensor
            def _(pe):
                total = all_bodies(pe)
                pe.sem_inc(summed1, U)
                nc.tensor.matmul(Z, zeros[:, 0:HEADS], zeros[:, 0:W], start=True, stop=False, skip_group_check=True)
                with pe.Fori(0, total) as j:
                    def turn(k):
                        pe.wait_ge(hot1, j * U + k + 1)
                        pe.wait_ge(hot_t1, j * U + k + 1)
                        for g in range(G):
                            last = nc.tensor.transpose(turned_ps[k % 2][0:W, g * P:(g + 1) * P], onehot_b[:, k, g, :],
                                                       ident_b[:, :])
                        last.then_inc(turned1, 1)

                    def expand(k):
                        pe.wait_ge(hot_t1, j * U + k + 3)
                        pe.wait_ge(window_loaded1[k], j * 16 + 16)
                        pe.wait_ge(product1, j * U + k + 1)
                        for g in range(G):
                            for part in range(3):
                                last = nc.tensor.matmul(ps[2 + k % 2][:, g * P:(g + 1) * P],
                                                        onehot_t[:, k, g * P:(g + 1) * P],
                                                        window[:, k, part * D:(part + 1) * D],
                                                        start=(part == 0), stop=(part == 2))
                        last.then_inc(expanded1, 1)

                    def window_sum(k):
                        pe.wait_ge(message1, j * U + k + U + 1)
                        pe.wait_ge(hot_f1, j * U + k + 1)
                        pe.wait_ge(added1, j * U + k + 1)
                        for g in range(G):
                            nc.tensor.matmul(ps[4 + k % 2][:, 0:W], prod[:, k, g * D:(g + 1) * D],
                                             onehot[:, k, g, :], start=(g == 0), stop=(g == G - 1))
                        for g in range(G):
                            last = nc.tensor.matmul(Z, weight[:, k, g * HEADS:(g + 1) * HEADS], onehot[:, k, g, :],
                                                    start=False, stop=False, skip_group_check=True)
                        last.then_inc(summed1, 1)

                    turn(0)
                    turn(1)
                    expand(0)
                    turn(2)
                    expand(1)
                    turn(3)
                    expand(2)
                    window_sum(0)
                    expand(3)
                    window_sum(1)
                    window_sum(2)
                    window_sum(3)

        tile1 = sem("tile1")
        z_summed = sem("z_summed")
        z_spread = sem("z_spread")
        heads1 = sem("heads1")
        out_ps1 = sem("out_ps1")
        sum1a = sem("sum1a")
        scaled1a = sem("scaled1a")
        ffn_ps1 = sem("ffn_ps1")
        ffn_relu1 = sem("ffn_relu1")
        ffn_out1 = sem("ffn_out1")
        sum1b = sem("sum1b")
        scaled1b = sem("scaled1b")
        sum1c = sem("sum1c")
        ab_ps = sem("ab_ps")
        ab_rows = sem("ab_rows")
        ab_stored = sem("ab_stored")

        def nth1(n, q):
            return (n * 3 + q) * LANES + NTILES

        with nc.Block("layer1_nodes") as block:
            @block.tensor
            def _(pe):
                pe.wait_ge(z_summed, 1)
                nc.tensor.matmul(ps[6][:, 0:1], head_of, z_heads[:, :], start=True, stop=True).then_inc(z_spread, 1)
                with pe.Fori(0, STEPS) as n:
                    def tile(l):
                        return n * LANES + l

                    for l in range(LANES):
                        pe.wait_ge(heads1, tile(l) + 1)
                        nc.tensor.matmul(bank(l, 0)[:, 0:T], wo_sb[:, :], tmp[l],
                                         start=True, stop=True).then_inc(out_ps1, 1)
                    norm_pe(pe, nth1(n, 0), sum1a, tile)
                    for l in range(LANES):
                        pe.wait_ge(scaled1a, tile(l) + 1)
                        nc.tensor.matmul(bank(l, 0)[:, 0:T], aw1_sb[:, :], y2[l][:, :],
                                         start=True, stop=True).then_inc(ffn_ps1, 1)
                    for l in range(LANES):
                        pe.wait_ge(ffn_relu1, tile(l) + 1)
                        nc.tensor.matmul(bank(l, 2)[:, 0:T], aw2_sb[:, :], hid[l][:, 0, :],
                                         start=True, stop=True).then_inc(ffn_out1, 1)
                    norm_pe(pe, nth1(n, 1), sum1b, tile)
                    norm_pe(pe, nth1(n, 2), sum1c, tile)
                    for l in range(LANES):
                        pe.wait_ge(normed, nth1(n, 2) + l + 1)
                        for j in range(TJ):
                            nc.tensor.matmul(bank(l, j)[:, 0:2 * D], y[l][:, j * P:(j + 1) * P], we1_sb[:, :],
                                             start=True, stop=True).then_inc(ab_ps, 1)

            @block.scalar
            def _(act):
                with act.Fori(0, STEPS) as n:
                    load_sqrt_table(act)
                    norm_act(act, nth1(n, 0))
                    for l in range(LANES):
                        act.wait_ge(ffn_ps1, n * LANES + l + 1)
                        act.activation(hid[l][:, 0, :], bank(l, 0)[:, 0:T], ACT.Relu,
                                       bias=v("a_b1")).then_inc(ffn_relu1, 1)
                    norm_act(act, nth1(n, 1))
                    norm_act(act, nth1(n, 2))
                    for l in range(LANES):
                        act.wait_ge(normed, nth1(n, 2) + l + 1)
                        act.activation(x[:, columns(n * LANES + l)], y[l][:, :], ACT.Copy).then_inc(x_kept, 1)

            @block.vector
            def _(dve):
                dve.tensor_reduce(z_heads[:, :], Z, AX.X, ALU.add).then_inc(z_summed, 1)
                dve.wait_ge(z_spread, 1)
                dve.reciprocal(inv_z[:, :], ps[6][:, 0:1]).then_inc(z_summed, 1)
                dve.wait_ge(z_summed, 2)
                with dve.Fori(0, STEPS) as n:
                    for l in range(LANES):
                        c = n * LANES + l
                        dve.wait_ge(tile1, c + 1)
                        dve.tensor_scalar(tmp[l], acc[:, columns(c)], inv_z[:, :], None, ALU.mult).then_inc(heads1, 1)
                    for l in range(LANES):
                        c = n * LANES + l
                        dve.wait_ge(out_ps1, c + 1)
                        dve.scalar_tensor_tensor(res[l], bank(l, 0)[:, 0:T], v("bO"), x[:, columns(c)], ALU.add,
                                                 ALU.add).then_inc(sum1a, 1)
                    norm_dve(dve, nth1(n, 0))
                    for l in range(LANES):
                        dve.wait_ge(normed, nth1(n, 0) + l + 1)
                        dve.tensor_scalar(y2[l][:, :], y[l][:, :], v("ln1_g"), v("ln1_b"), ALU.mult,
                                          ALU.add).then_inc(scaled1a, 1)
                    for l in range(LANES):
                        dve.wait_ge(scaled1a, n * LANES + l + 1)
                        dve.wait_ge(ffn_out1, n * LANES + l + 1)
                        dve.scalar_tensor_tensor(res[l], bank(l, 2)[:, 0:T], v("a_b2"), y2[l][:, :], ALU.add,
                                                 ALU.add).then_inc(sum1b, 1)
                    norm_dve(dve, nth1(n, 1))
                    for l in range(LANES):
                        dve.wait_ge(normed, nth1(n, 1) + l + 1)
                        dve.tensor_scalar(y2[l][:, :], y[l][:, :], v("ln2_g"), v("ln2_b"), ALU.mult,
                                          ALU.add).then_inc(scaled1b, 1)
                    for l in range(LANES):
                        dve.wait_ge(scaled1b, n * LANES + l + 1)
                        dve.tensor_tensor(res[l], y2[l][:, :], x[:, columns(n * LANES + l)], ALU.add).then_inc(sum1c, 1)
                    norm_dve(dve, nth1(n, 2))
                    for l in range(LANES):
                        for j in range(TJ):
                            dve.wait_ge(ab_ps, (n * LANES + l) * TJ + j + 1)
                            dve.tensor_tensor(node_rows[l][:, j, 0:2 * D], bank(l, j)[:, 0:2 * D], bias_ab[:, :],
                                              ALU.add).then_inc(ab_rows, 1)

            @block.gpsimd
            def _(pool):
                with pool.Fori(0, STEPS) as n:
                    for l in range(LANES):
                        c = n * LANES + l
                        pool.wait_ge(ab_rows, c * TJ + TJ)
                        pool.sem_inc(pool_waited, 1)
                        split_rows(pool, NTILES + c, l, D)

            @block.sync
            def _(sp):
                sp.sem_inc(tile1, LANES)
                with sp.Fori(0, STEPS) as n:
                    for l in range(LANES):
                        c = n * LANES + l
                        sp.wait_ge(ab_rows, c * TJ + TJ)
                        sp.sem_inc(sp_waited, 1)
                        sp.dma_start(a_rows[columns(c), :].rearrange("(j p) f -> p j f", p=P),
                                     node_rows[l][:, :, 0:D]).then_inc(ab_stored, 16)
                        sp.wait_ge(split_step, (NTILES + c) * SPLITS + SPLITS)
                        sp.sem_inc(sp_waited, 1)
                        sp.dma_start(b_rows[columns(c), :].rearrange("(j p) f -> p j f", p=P),
                                     parts_b[l][:, :, :]).then_inc(ab_stored, 16)
                        sp.wait_ge(ab_stored, c * 32 + 32)
                        sp.sem_inc(sp_waited, 1)
                        sp.wait_ge(x_kept, NTILES + c + 1)
                        sp.sem_inc(tile1, 1)

        index_loaded2 = [sem(f"index_loaded2_{k}") for k in range(U)]
        window_loaded2 = [sem(f"window_loaded2_{k}") for k in range(U)]
        gathered2 = [sem(f"gathered2_{k}") for k in range(U)]
        hot2 = sem("hot2")
        hot_f2 = sem("hot_f2")
        turned2 = sem("turned2")
        hot_t2 = sem("hot_t2")
        expanded2 = sem("expanded2")
        pair2 = sem("pair2")
        relu2 = sem("relu2")
        split2 = sem("split2")
        summed2 = sem("summed2")
        added2 = sem("added2")
        windows2 = sem("windows2")
        cleared2 = sem("cleared2")
        DEG = ps[7][:, 0:HI]
        with nc.Block("layer2_edges") as block:
            @block.sync
            def _(sp):
                total = all_bodies(sp)
                sp.sem_inc(relu2, U)
                sp.sem_inc(expanded2, U)
                with sp.Fori(0, total, BODIES) as first:
                    sp.wait_ge(windows2, 3 * first + 2)
                    sp.sem_inc(sp_waited, 1)
                    with sp.Fori(0, BODIES) as i:
                        at = window_starts(mybir.EngineType.SP, i)
                        for k in range(U):
                            s = (first + i) * U + k
                            sp.wait_ge(relu2, s + 1)
                            sp.sem_inc(sp_waited, 1)
                            sp.dma_start(index[:, k, :], src_index[:, ds((i * U + k) * G, G)]
                                         ).then_inc(index_loaded2[k], 16)
                            sp.wait_ge(expanded2, s + 1)
                            sp.sem_inc(sp_waited, 1)
                            sp.dma_start(window[:, k, :], b_rows[ds(at[k], W), :]).then_inc(window_loaded2[k], 16)

            @block.gpsimd
            def _(pool):
                total = all_bodies(pool)
                with pool.Fori(0, total) as j:
                    for k in range(U):
                        pool.wait_ge(index_loaded2[k], j * 16 + 16)
                        pool.sem_inc(pool_waited, 1)
                        for g in range(G):
                            pool.indirect_dma_start(rows[:, k, g * D:(g + 1) * D], None, a_rows[:, :],
                                                    bass.IndirectOffsetOnAxis(ap=index[:, k, g:g + 1], axis=0)
                                                    ).then_inc(gathered2[k], 16)

            @block.scalar
            def _(act):
                total = all_bodies(act)
                act.sem_inc(hot_t2, 2)
                with act.Fori(0, total) as j:
                    def turn(k):
                        act.wait_ge(turned2, j * U + k + 1)
                        act.wait_ge(expanded2, j * U + k + 1)
                        act.activation(onehot_t[:, k, :], turned_ps[k % 2][0:W, 0:SC], ACT.Copy).then_inc(hot_t2, 1)

                    def relu(k):
                        act.wait_ge(pair2, j * U + k + 3)
                        act.wait_ge(summed2, j * U + k + 1)
                        act.activation(rows[:, k, G * D:2 * G * D], prod[:, k, :], ACT.Relu).then_inc(relu2, 1)

                    turn(0)
                    turn(1)
                    turn(2)
                    relu(0)
                    turn(3)
                    relu(1)
                    relu(2)
                    relu(3)

            @block.vector
            def _(dve):
                total = all_bodies(dve)
                dve.sem_inc(pair2, 2)
                dve.sem_inc(added2, 4)
                dve.memset(acc[:, :], 0.0).then_inc(cleared2, 1)
                windows_reset(dve, windows2)
                dve.wait_ge(windows2, 2)
                dve.wait_ge(cleared2, 1)
                with dve.Fori(0, total, BODIES) as first:
                    with dve.Fori(0, BODIES) as i:
                        at = window_starts(mybir.EngineType.DVE, i)
                        def split(k):
                            col = (i * U + k) * G
                            dve.tensor_tensor(lo_hot[:, k, :, :], iota_p.unsqueeze(1).broadcast_to([P, G, P]),
                                              src_lo[:, ds(col, G)].unsqueeze(2).broadcast_to([P, G, P]),
                                              ALU.is_equal)
                            dve.tensor_tensor(hi_hot[:, k, :, :], iota_p[:, 0:HI].unsqueeze(1).broadcast_to([P, G, HI]),
                                              src_hi[:, ds(col, G)].unsqueeze(2).broadcast_to([P, G, HI]),
                                              ALU.is_equal).then_inc(split2, 1)

                        def pair(k):
                            s = (first + i) * U + k
                            dve.wait_ge(expanded2, s + U + 1)
                            dve.wait_ge(gathered2[k], (first + i) * 16 * G + 16 * G)
                            dve.wait_ge(relu2, s + 1)
                            dve.tensor_tensor(prod[:, k, :], ps[2 + k % 2][:, :], rows[:, k, 0:G * D],
                                              ALU.add).then_inc(pair2, 1)

                        def add(k):
                            s = (first + i) * U + k
                            dve.wait_ge(summed2, s + U + 1)
                            dve.wait_ge(added2, 2 * s + 4)
                            dve.tensor_tensor(acc[:, ds(at[k], W)], acc[:, ds(at[k], W)], ps[4 + k % 2][:, 0:W],
                                              ALU.add).then_inc(added2, 1)
                            dve.tensor_tensor(count[:, ds(at[k], W)], count[:, ds(at[k], W)], ps[4 + k % 2][0:1, W:2 * W],
                                              ALU.add).then_inc(added2, 1)

                        dve.wait_ge(summed2, (first + i) * U + U)
                        one_hot(dve, onehot_b, i).then_inc(hot2, U)
                        one_hot(dve, onehot, i).then_inc(hot_f2, U)
                        split(0)
                        pair(0)
                        for k in range(1, U):
                            split(k)
                            pair(k)
                            if k >= 2:
                                add(k - 2)
                        add(U - 2)
                        add(U - 1)
                    windows_move(dve, windows2)
                    dve.memset(src_hi[:, :], -1.0).then_inc(windows2, BODIES)
                    dve.wait_ge(windows2, 3 * first + 3 * BODIES + 2)

            @block.tensor
            def _(pe):
                total = all_bodies(pe)
                pe.sem_inc(summed2, U)
                nc.tensor.matmul(DEG, zeros[:, :], zeros[:, 0:HI], start=True, stop=False, skip_group_check=True)
                with pe.Fori(0, total) as j:
                    def turn(k):
                        pe.wait_ge(hot2, j * U + k + 1)
                        pe.wait_ge(hot_t2, j * U + k + 1)
                        for g in range(G):
                            last = nc.tensor.transpose(turned_ps[k % 2][0:W, g * P:(g + 1) * P], onehot_b[:, k, g, :],
                                                       ident_b[:, :])
                        last.then_inc(turned2, 1)

                    def expand(k):
                        pe.wait_ge(hot_t2, j * U + k + 3)
                        pe.wait_ge(window_loaded2[k], j * 16 + 16)
                        pe.wait_ge(pair2, j * U + k + 1)
                        for g in range(G):
                            for part in range(3):
                                last = nc.tensor.matmul(ps[2 + k % 2][:, g * P:(g + 1) * P],
                                                        onehot_t[:, k, g * P:(g + 1) * P],
                                                        window[:, k, part * D:(part + 1) * D],
                                                        start=(part == 0), stop=(part == 2))
                        last.then_inc(expanded2, 1)

                    def window_sum(k):
                        pe.wait_ge(split2, j * U + k + 1)
                        for g in range(G):
                            nc.tensor.matmul(DEG, lo_hot[:, k, g, :], hi_hot[:, k, g, :],
                                             start=False, stop=False, skip_group_check=True)
                        pe.wait_ge(relu2, j * U + k + U + 1)
                        pe.wait_ge(hot_f2, j * U + k + 1)
                        pe.wait_ge(added2, 2 * (j * U + k) + 2)
                        for g in range(G):
                            nc.tensor.matmul(ps[4 + k % 2][:, 0:W], rows[:, k, (G + g) * D:(G + g + 1) * D],
                                             onehot[:, k, g, :], start=(g == 0), stop=(g == G - 1))
                        for g in range(G):
                            last = nc.tensor.matmul(ps[4 + k % 2][0:1, W:2 * W], ones_b[:, :], onehot_b[:, k, g, :],
                                                    start=(g == 0), stop=(g == G - 1))
                        last.then_inc(summed2, 1)

                    turn(0)
                    turn(1)
                    expand(0)
                    turn(2)
                    expand(1)
                    turn(3)
                    expand(2)
                    window_sum(0)
                    expand(3)
                    window_sum(1)
                    window_sum(2)
                    window_sum(3)

        tile2 = sem("tile2")
        degree = sem("degree")
        degree_sqrt = sem("degree_sqrt")
        agg_ps2 = sem("agg_ps2")
        agg2 = sem("agg2")
        hidden_ps2 = sem("hidden_ps2")
        hidden2 = sem("hidden2")
        mlp2 = sem("mlp2")
        twice2 = sem("twice2")
        sum2 = sem("sum2")
        y_ps = sem("y_ps")
        y_scaled = sem("y_scaled")
        y_stored = sem("y_stored")
        with nc.Block("layer2_nodes") as block:
            @block.tensor
            def _(pe):
                with pe.Fori(0, STEPS) as n:
                    def tile(l):
                        return n * LANES + l

                    for l in range(LANES):
                        pe.wait_ge(tile2, tile(l) + 1)
                        nc.tensor.matmul(bank(l, 0)[:, 0:T], we2_sb[:, :], acc[:, columns(tile(l))],
                                         start=True, stop=False)
                        nc.tensor.matmul(bank(l, 0)[:, 0:T], be2_sb[:, :], count[:, columns(tile(l))],
                                         start=False, stop=True).then_inc(agg_ps2, 1)
                    for l in range(LANES):
                        nc.tensor.matmul(bank(l, 2)[:, 0:T], wn1_sb[:, 0, :], x[:, columns(tile(l))],
                                         start=True, stop=False)
                        pe.wait_ge(agg2, tile(l) + 1)
                        nc.tensor.matmul(bank(l, 2)[:, 0:T], wn1_sb[:, 1, :], tmp[l],
                                         start=False, stop=True).then_inc(hidden_ps2, 1)
                    for l in range(LANES):
                        pe.wait_ge(hidden2, tile(l) + 1)
                        nc.tensor.matmul(bank(l, 0)[:, 0:T], wn2_sb[:, :], hid[l][:, 0, :],
                                         start=True, stop=True).then_inc(mlp2, 1)
                    norm_pe(pe, 4 * NTILES + n * LANES, sum2, tile)
                    for l in range(LANES):
                        pe.wait_ge(normed, 4 * NTILES + tile(l) + 1)
                        for j in range(TJ):
                            nc.tensor.transpose(bank(l, 2 * j)[:, 0:P], y[l][:, j * P:(j + 1) * P],
                                                ident).then_inc(y_ps, 1)

            @block.scalar
            def _(act):
                act.wait_ge(degree, 1)
                act.activation(dis_raw[:, :], deg_sb[:, :], ACT.Sqrt).then_inc(degree_sqrt, 1)
                with act.Fori(0, STEPS) as n:
                    load_sqrt_table(act)
                    for l in range(LANES):
                        act.wait_ge(agg_ps2, n * LANES + l + 1)
                        act.activation(tmp[l], bank(l, 0)[:, 0:T], ACT.Copy).then_inc(agg2, 1)
                    for l in range(LANES):
                        act.wait_ge(hidden_ps2, n * LANES + l + 1)
                        act.activation(hid[l][:, 0, :], bank(l, 2)[:, 0:T], ACT.Relu,
                                       bias=v("bn1")).then_inc(hidden2, 1)
                    norm_act(act, 4 * NTILES + n * LANES)
                    for l in range(LANES):
                        act.wait_ge(normed, 4 * NTILES + n * LANES + l + 1)
                        act.activation(x[:, columns(n * LANES + l)], y[l][:, :], ACT.Copy).then_inc(x_kept, 1)

            @block.vector
            def _(dve):
                dve.tensor_scalar(deg_sb[:, :], DEG, 1.0, None, ALU.max).then_inc(degree, 1)
                dve.tensor_scalar(deg_pos[:, :], DEG, 0.0, None, ALU.is_gt).then_inc(degree, 1)
                dve.wait_ge(degree_sqrt, 1)
                dve.reciprocal(dis_raw[:, :], dis_raw[:, :]).then_inc(degree, 1)
                dve.wait_ge(degree, 3)
                dve.tensor_tensor(dis[:, :], dis_raw[:, :], deg_pos[:, :], ALU.mult).then_inc(degree, 1)
                dve.wait_ge(degree, 4)
                with dve.Fori(0, STEPS) as n:
                    for l in range(LANES):
                        c = n * LANES + l
                        dve.wait_ge(tile2, c + 1)
                        dve.tensor_scalar(y2[l][:, :], x[:, columns(c)], 2.0, v("bn2"), ALU.mult,
                                          ALU.add).then_inc(twice2, 1)
                    for l in range(LANES):
                        dve.wait_ge(twice2, n * LANES + l + 1)
                        dve.wait_ge(mlp2, n * LANES + l + 1)
                        dve.tensor_tensor(res[l], bank(l, 0)[:, 0:T], y2[l][:, :], ALU.add).then_inc(sum2, 1)
                    norm_dve(dve, 4 * NTILES + n * LANES)
                    for l in range(LANES):
                        for j in range(TJ):
                            t = (n * LANES + l) * TJ + j
                            dve.wait_ge(y_ps, t + 1)
                            dve.tensor_scalar(node_rows[l][:, j, 0:D], bank(l, 2 * j)[:, 0:P], dis[:, ds(t, 1)], None,
                                              ALU.mult).then_inc(y_scaled, 1)

            @block.gpsimd
            def _(pool):
                with pool.Fori(0, STEPS) as n:
                    for l in range(LANES):
                        c = n * LANES + l
                        pool.wait_ge(y_scaled, c * TJ + TJ)
                        pool.sem_inc(pool_waited, 1)
                        split_rows(pool, 2 * NTILES + c, l, 0)

            @block.sync
            def _(sp):
                sp.sem_inc(tile2, LANES)
                with sp.Fori(0, STEPS) as n:
                    for l in range(LANES):
                        c = n * LANES + l
                        sp.wait_ge(y_scaled, c * TJ + TJ)
                        sp.sem_inc(sp_waited, 1)
                        sp.wait_ge(split_step, (2 * NTILES + c) * SPLITS + SPLITS)
                        sp.sem_inc(sp_waited, 1)
                        sp.dma_start(y_rows[columns(c), :].rearrange("(j p) f -> p j f", p=P),
                                     parts_b[l][:, :, :]).then_inc(y_stored, 16)
                        sp.wait_ge(y_stored, c * 16 + 16)
                        sp.sem_inc(sp_waited, 1)
                        sp.wait_ge(x_kept, 2 * NTILES + c + 1)
                        sp.sem_inc(tile2, 1)

        window_loaded3 = [sem(f"window_loaded3_{k}") for k in range(U)]
        scattered = [sem(f"scattered{k}") for k in range(U)]
        landed = [sem(f"landed{k}") for k in range(U)]
        picked3 = sem("picked3")
        hot3 = sem("hot3")
        spread3 = sem("spread3")
        same3 = sem("same3")
        earlier3 = sem("earlier3")
        follows3 = sem("follows3")
        to_spare3 = sem("to_spare3")
        shift3 = sem("shift3")
        target3 = sem("target3")
        counted3 = sem("counted3")
        counts3 = sem("counts3")
        expanded3 = sem("expanded3")
        value3 = sem("value3")
        windows3 = sem("windows3")
        with nc.Block("layer3_edges") as block:
            @block.sync
            def _(sp):
                total = all_bodies(sp)
                for k in range(U):
                    sp.sem_inc(landed[k], 1)
                with sp.Fori(0, total) as j:
                    for k in range(U):
                        sp.wait_ge(scattered[k], j * 16 * G + 16 * G)
                        sp.sem_inc(landed[k], 1)

            @block.scalar
            def _(act):
                total = all_bodies(act)
                act.sem_inc(counts3, 2)
                act.sem_inc(value3, 2)
                act.sem_inc(expanded3, U)
                with act.Fori(0, total, BODIES) as first:
                  act.wait_ge(windows3, 2 * first + 2)
                  with act.Fori(0, BODIES) as i:
                    at = window_starts(mybir.EngineType.Activation, i)
                    j = first + i
                    for k in range(U):
                        act.wait_ge(expanded3, j * U + k + 1)
                        act.dma_start(window[:, k, :], y_rows[ds(at[k], W), :]).then_inc(window_loaded3[k], 16)

                    def counts(k):
                        act.wait_ge(counted3, j * U + k + U + 1)
                        act.wait_ge(expanded3, j * U + k + 1)
                        act.activation(onehot_t[:, k, :], ps[2 + k % 2][0:W, :], ACT.Copy).then_inc(counts3, 1)

                    def values(k):
                        act.wait_ge(expanded3, j * U + k + U + 1)
                        act.wait_ge(landed[k], j + 1)
                        act.activation(rows[:, k, 0:G * D], ps[4 + k % 2][:, :], ACT.Copy).then_inc(value3, 1)

                    counts(0)
                    for k in range(1, U):
                        counts(k)
                        values(k - 1)
                    values(U - 1)

            @block.gpsimd
            def _(pool):
                total = all_bodies(pool)
                with pool.Fori(0, total) as j:
                    for k in range(U):
                        pool.wait_ge(value3, j * U + k + 3)
                        pool.wait_ge(target3, j * U + k + 1)
                        pool.sem_inc(pool_waited, 1)
                        pool.wait_ge(landed[(k + 2) % U], j + 1 + (1 if k >= 2 else 0))
                        pool.sem_inc(pool_waited, 1)
                        for g in range(G):
                            pool.indirect_dma_start(table[(k % 2) * G + g][:, :],
                                                    bass.IndirectOffsetOnAxis(ap=index[:, k, g:g + 1], axis=0),
                                                    rows[:, k, g * D:(g + 1) * D], None,
                                                    compute_op=ALU.add).then_inc(scattered[k], 16)

            @block.vector
            def _(dve):
                total = all_bodies(dve)
                dve.sem_inc(same3, 2)
                dve.sem_inc(earlier3, 1)
                windows_reset(dve, windows3)
                dve.wait_ge(windows3, 2)
                with dve.Fori(0, total, BODIES) as first:
                    with dve.Fori(0, BODIES) as i:
                        def hot(k):
                            s = (first + i) * U + k
                            dve.wait_ge(counted3, s + 1)
                            dve.tensor_copy(src_s[:, k, :], src_num[:, ds((i * U + k) * G, G)]).then_inc(picked3, 1)
                            one_hot(dve, onehot_b, i, k, 1).then_inc(hot3, 1)

                        def equal(k):
                            s = (first + i) * U + k
                            dve.wait_ge(picked3, s + 1)
                            dve.wait_ge(spread3, s + 1)
                            dve.tensor_tensor(same[:, k, :, :], ps[k % 2][:, :].rearrange("p (g e) -> p g e", g=G),
                                              src_s[:, k, :].unsqueeze(2).broadcast_to([P, G, P]),
                                              ALU.is_equal).then_inc(same3, 1)

                        def targets(k):
                            s = (first + i) * U + k
                            dve.wait_ge(same3, s + 3)
                            for g in range(G):
                                dve.wait_ge(earlier3, s * G + g + 1)
                                dve.tensor_tensor_reduce(masked[:, :], same[:, k, g, :], lower, 1.0, 0.0, ALU.mult,
                                                         ALU.add, earlier[:, k, g:g + 1]).then_inc(earlier3, 1)
                            dve.tensor_scalar(to_spare[:, k, :], src_s[:, k, :], -1.0, spare_row[:, :], ALU.mult,
                                              ALU.add).then_inc(to_spare3, 1)
                            dve.wait_ge(earlier3, s * G + G + 1)
                            dve.wait_ge(to_spare3, s + 1)
                            dve.scalar_tensor_tensor(shift_by[:, k, :], earlier[:, k, :], 0.0, to_spare[:, k, :],
                                                     ALU.is_gt, ALU.mult).then_inc(shift3, 1)
                            dve.wait_ge(shift3, s + 1)
                            dve.wait_ge(landed[k], first + i + 1)
                            dve.tensor_tensor(index[:, k, :], src_s[:, k, :], shift_by[:, k, :],
                                              ALU.add).then_inc(target3, 1)

                        hot(0)
                        hot(1)
                        equal(0)
                        targets(0)
                        hot(2)
                        equal(1)
                        targets(1)
                        hot(3)
                        equal(2)
                        targets(2)
                        equal(3)
                        targets(3)
                    windows_move(dve, windows3)
                    dve.wait_ge(windows3, 2 * first + 2 * BODIES + 2)

            @block.tensor
            def _(pe):
                total = all_bodies(pe)
                pe.sem_inc(counted3, U)
                with pe.Fori(0, total) as j:
                    def spread(k):
                        pe.wait_ge(picked3, j * U + k + 1)
                        pe.wait_ge(same3, j * U + k + 1)
                        for g in range(G):
                            last = nc.tensor.matmul(ps[k % 2][:, g * P:(g + 1) * P],
                                                    src_s[:, k, g:g + 1].broadcast_to([P, P]), ident,
                                                    start=True, stop=True)
                        last.then_inc(spread3, 1)

                    def counts(k):
                        pe.wait_ge(same3, j * U + k + 3)
                        pe.wait_ge(hot3, j * U + k + 1)
                        pe.wait_ge(counts3, j * U + k + 1)
                        for g in range(G):
                            last = nc.tensor.matmul(ps[2 + k % 2][0:W, g * P:(g + 1) * P], onehot_b[:, k, g, :],
                                                    same[:, k, g, :], start=True, stop=True)
                        last.then_inc(counted3, 1)

                    def expand(k):
                        pe.wait_ge(counts3, j * U + k + 3)
                        pe.wait_ge(window_loaded3[k], j * 16 + 16)
                        pe.wait_ge(value3, j * U + k + 1)
                        for g in range(G):
                            for part in range(3):
                                last = nc.tensor.matmul(ps[4 + k % 2][:, g * P:(g + 1) * P],
                                                        onehot_t[:, k, g * P:(g + 1) * P],
                                                        window[:, k, part * D:(part + 1) * D],
                                                        start=(part == 0), stop=(part == 2))
                        last.then_inc(expanded3, 1)

                    spread(0)
                    spread(1)
                    counts(0)
                    for k in range(2, U):
                        spread(k)
                        counts(k - 1)
                        expand(k - 2)
                    counts(U - 1)
                    expand(U - 2)
                    expand(U - 1)


        tile3 = sem("tile3")
        tables_loaded = [sem(f"tables_loaded{l}") for l in range(LANES)]
        diag3 = sem("diag3")
        agg_ps3 = sem("agg_ps3")
        agg3 = sem("agg3")
        lin3 = sem("lin3")
        sum3 = sem("sum3")
        out_stored = sem("out_stored")
        parts = [rows[:, 2 * l:2 * l + 2, :].rearrange("p u c -> p (u c)")
                 .rearrange("p (t j f) -> p t j f", t=TABLES, f=D) for l in range(LANES)]
        diag = [hid[l][:, 1, :] for l in range(LANES)]
        nth3 = 5 * NTILES
        with nc.Block("layer3_nodes") as block:
            @block.tensor
            def _(pe):
                with pe.Fori(0, STEPS) as n:
                    def tile(l):
                        return n * LANES + l

                    for l in range(LANES):
                        pe.wait_ge(tables_loaded[l], n * 16 * TABLES + 16 * TABLES)
                        pe.wait_ge(diag3, tile(l) * TJ + TJ)
                        for j in range(TJ):
                            for t in range(TABLES):
                                last = nc.tensor.matmul(bank(l, 0)[:, j * P:(j + 1) * P], parts[l][:, t, j, :],
                                                        diag[l][:, j * P:(j + 1) * P],
                                                        start=(t == 0), stop=(t == TABLES - 1))
                        last.then_inc(agg_ps3, 1)
                    for l in range(LANES):
                        pe.wait_ge(agg3, tile(l) + 1)
                        nc.tensor.matmul(bank(l, 2)[:, 0:T], w3t_sb[:, :], tmp[l], start=True, stop=True).then_inc(lin3, 1)
                    norm_pe(pe, nth3 + n * LANES, sum3, tile)

            @block.scalar
            def _(act):
                with act.Fori(0, STEPS) as n:
                    load_sqrt_table(act)
                    for l in range(LANES):
                        act.wait_ge(agg_ps3, n * LANES + l + LANES + 1)
                        act.activation(tmp[l], bank(l, 0)[:, 0:T], ACT.Copy).then_inc(agg3, 1)
                    norm_act(act, nth3 + n * LANES)

            @block.vector
            def _(dve):
                with dve.Fori(0, STEPS) as n:
                    for l in range(LANES):
                        c = n * LANES + l
                        dve.wait_ge(tile3, c + 1)
                        for j in range(TJ):
                            dve.tensor_scalar(diag[l][:, j * P:(j + 1) * P], ident, dis[:, ds(c * TJ + j, 1)], None,
                                              ALU.mult).then_inc(diag3, 1)
                    for l in range(LANES):
                        c = n * LANES + l
                        dve.wait_ge(lin3, c + 1)
                        dve.scalar_tensor_tensor(res[l], bank(l, 2)[:, 0:T], v("b3"), x[:, columns(c)], ALU.add,
                                                 ALU.add).then_inc(sum3, 1)
                    norm_dve(dve, nth3 + n * LANES)

            @block.sync
            def _(sp):
                sp.sem_inc(agg_ps3, LANES)
                with sp.Fori(0, STEPS) as n:
                    for l in range(LANES):
                        c = n * LANES + l
                        sp.wait_ge(agg_ps3, c + 1)
                        sp.sem_inc(sp_waited, 1)
                        for t in range(TABLES):
                            sp.dma_start(parts[l][:, t, :, :],
                                         table[t][columns(c), :].rearrange("(j p) f -> p j f", p=P)
                                         ).then_inc(tables_loaded[l], 16)

            @block.gpsimd
            def _(pool):
                pool.sem_inc(tile3, LANES)
                with pool.Fori(0, STEPS) as n:
                    for l in range(LANES):
                        c = n * LANES + l
                        pool.wait_ge(normed, nth3 + c + 1)
                        pool.sem_inc(pool_waited, 1)
                        pool.dma_start(out[:, columns(c)], y[l][:, :]).then_inc(out_stored, 16)
                        pool.wait_ge(out_stored, c * 16 + 16)
                        pool.sem_inc(tile3, 1)
                pool.wait_ge(out_stored, 16 * NTILES)


def layouts(inputs):
    import numpy as np
    a = {k: np.asarray(x) for k, x in inputs.items()}
    n, e = a["x"].shape[0], a["src"].shape[0]
    nodes, scs = sizes(n, e)
    first = np.arange(scs) * SC
    start = np.minimum(first, e - SC).astype(np.int32)
    edge = (start[:, None] + np.arange(SC)[None, :])
    own = edge >= first[:, None]
    place = lambda m: np.ascontiguousarray(m.reshape(scs, P, G).transpose(1, 0, 2).reshape(P, scs * G))
    minus = np.int32(-1)
    by_rows = a["dst"][np.where(own, edge, e - 1)]
    xt = np.zeros((P, nodes), np.float32)
    xt[:, :n] = a["x"].T
    ramp = np.broadcast_to(np.arange(P, dtype=np.float32), (P, P))
    consts = np.concatenate([np.eye(P, dtype=np.float32), np.tril(np.ones((P, P), np.float32), -1),
                             np.eye(P, dtype=np.float32) - np.float32(1.0 / D), ramp[:, :W], ramp,
                             nodes + np.arange(P, dtype=np.float32)[:, None],
                             (np.arange(P)[:, None] == np.arange(P)[None, :] // HEAD).astype(np.float32)], axis=1)
    b1 = a["L0_gnn_b1"].reshape(4, P)
    vectors = np.stack([*b1, a["L0_gnn_b2"], a["L1_gnn_bO"], a["L1_gnn_ln1_g"], a["L1_gnn_ln1_b"], a["L1_gnn_b1"],
                        a["L1_gnn_b2"], a["L1_gnn_ln2_g"], a["L1_gnn_ln2_b"], a["L2_gnn_bn1"], a["L2_gnn_bn2"],
                        a["L3_gnn_b"]], axis=1)
    be1 = a["L2_gnn_be1"]
    return {
        "xT": xt, "edge_attr": a["edge_attr_128"],
        "src_index": place(np.where(own, a["src"][edge], np.int32(0))),
        "src_id": place(np.where(own, a["src"][edge], minus)),
        "dst_id": place(np.where(own, a["dst"][edge], minus)),
        "dst_rows": np.ascontiguousarray(by_rows.reshape(4, scs // 4, SC).transpose(1, 0, 2)),
        "edge_start": start[None, :], "consts": np.ascontiguousarray(consts),
        "w1": a["L0_gnn_W1"], "w2": a["L0_gnn_W2"],
        "wqkv": np.concatenate([a["L1_gnn_WQ"], a["L1_gnn_WK"], a["L1_gnn_WV"]], axis=1),
        "wo": a["L1_gnn_WO"], "aw1": a["L1_gnn_W1"], "aw2": a["L1_gnn_W2"],
        "we1": a["L2_gnn_We1"], "we2": a["L2_gnn_We2"], "wn1": a["L2_gnn_Wn1"], "wn2": a["L2_gnn_Wn2"],
        "w3t": np.ascontiguousarray(a["L3_gnn_W"].T), "vectors": np.ascontiguousarray(vectors),
        "row_bqkv": np.concatenate([a["L1_gnn_bQ"], a["L1_gnn_bK"], a["L1_gnn_bV"]])[None, :],
        "row_be1": np.concatenate([np.zeros_like(be1), be1])[None, :], "row_be2": a["L2_gnn_be2"][None, :],
    }


def kernel(**inputs):
    import numpy as np
    import concourse.bacc as bacc
    from concourse import mybir as mb
    from concourse.bass_utils import run_bass_kernel_spmd

    n = np.asarray(inputs["x"]).shape[0]
    arrays = layouts(inputs)
    nc = bacc.Bacc("TRN2", target_bir_lowering=False, num_devices=1)
    args = {}
    for name, a in arrays.items():
        args[name] = nc.dram_tensor(f"in_{name}", a.shape, mb.dt.from_np(a.dtype), kind="ExternalInput").ap()
    nodes = arrays["xT"].shape[1]
    args["out"] = nc.dram_tensor("out_0", (P, nodes), mb.dt.float32, kind="ExternalOutput").ap()
    gnn_program(nc, **args)
    r = run_bass_kernel_spmd(nc, [{f"in_{name}": a for name, a in arrays.items()}], core_ids=[0])
    return np.ascontiguousarray(r.results[0]["out_0"][:, :n].T)
```

```python
from contextlib import ExitStack

import concourse.bass as bass
from concourse import mybir

P = 128
D = 128
HEADS = 8
HEAD = D // HEADS
HIDDEN = 512
G = 4
SC = G * P
W = 32
U = 4
U0 = 2 * U
SPLIT0 = 3
AHEAD0 = 3
T = 256
TJ = T // P
LANES = 2
TABLES = 8
LN_EPS = 1e-5
CLIP = 5.0

F32 = mybir.dt.float32
BF16 = mybir.dt.bfloat16
I32 = mybir.dt.int32
I16 = mybir.dt.int16
ALU = mybir.AluOpType
ACT = mybir.ActivationFunctionType
AX = mybir.AxisListType
ds = bass.ds

VECTORS = ["b1_0", "b1_1", "b1_2", "b1_3", "b2", "bO", "ln1_g", "ln1_b", "a_b1", "a_b2", "ln2_g", "ln2_b",
           "bn1", "bn2", "b3"]
VEC = {name: i for i, name in enumerate(VECTORS)}


def sizes(n_nodes, n_edges):
    node_cols = -(-(n_nodes + W) // (LANES * T)) * LANES * T
    superchunks = -(-n_edges // SC)
    return node_cols, -(-superchunks // U0) * U0, -(-superchunks // U) * U


def gnn_program(nc, xT, edge_attr, src_index, src_id, dst_id, dst_rows, consts,
                w1, w2, wqkv, wo, aw1, aw2, we1, we2, wn1, wn2, w3t, vectors, row_bqkv, row_be1, row_be2, out):
    NODES = xT.shape[1]
    SCS = src_id.shape[1] // G
    E = edge_attr.shape[0]
    BODIES0 = SCS // U0
    BODIES = sizes(1, E)[2] // U
    NTILES = NODES // T
    STEPS = NTILES // LANES
    HI = NODES // P
    SPR = SCS // 4
    assert SPR <= P and E >= SC and HI <= P
    PASSES_MAX = NODES // W + 1
    ctx = ExitStack()
    with ctx:
        def sb(name, shape, dt=F32):
            return ctx.enter_context(nc.sbuf_tensor(name, shape, dt))

        def sem(name):
            return ctx.enter_context(nc.semaphore(name))

        x = sb("x", [P, NODES])
        acc = sb("acc", [P, NODES])
        count = sb("count", [1, NODES])
        src_num = sb("src_num", [P, SCS * G])
        src_hi = sb("src_hi", [P, SCS * G], BF16)
        src_lo = sb("src_lo", [P, SCS * G], BF16)
        rel0 = sb("rel0", [P, SCS, G])
        rel = sb("rel", [P, SCS, G])
        base0 = sb("base0", [1, SCS])
        base = sb("base", [1, SCS], I32)
        pass_bodies = sb("pass_bodies", [1, 2], I32)
        cst = sb("cst", [P, 5 * P + W + 2])
        ident = cst[:, 0:P]
        lower = cst[:, P:2 * P]
        centre_m = cst[:, 2 * P:3 * P]
        iota_w = cst[:, 3 * P:3 * P + W]
        iota_p = cst[:, 3 * P + W:4 * P + W]
        spare_row = cst[:, 4 * P + W:4 * P + W + 1]
        head_of = cst[0:HEADS, 4 * P + W + 1:5 * P + W + 1]
        node_col = cst[0:3 * W, 5 * P + W + 1:5 * P + W + 2]
        ones = sb("ones", [P, P])
        zeros = sb("zeros", [P, P])
        mean_col = sb("mean_col", [P, 1])
        eps = sb("eps", [P, 1])
        w1_sb = sb("w1_sb", [P, 2, HIDDEN])
        w2_sb = sb("w2_sb", [P, HIDDEN // P, D])
        wqkv_sb = sb("wqkv_sb", [P, 3 * D])
        wo_sb = sb("wo_sb", [P, D])
        aw1_sb = sb("aw1_sb", [P, D])
        aw2_sb = sb("aw2_sb", [P, D])
        we1_sb = sb("we1_sb", [P, 2 * D])
        we2_sb = sb("we2_sb", [P, D])
        wn1_sb = sb("wn1_sb", [P, 2, D])
        wn2_sb = sb("wn2_sb", [P, D])
        w3t_sb = sb("w3t_sb", [P, D])
        vec = sb("vec", [P, len(VECTORS)])
        bqkv_sb = sb("bqkv_sb", [1, 3 * D])
        be1_sb = sb("be1_sb", [1, 2 * D])
        be2_sb = sb("be2_sb", [1, D])

        def v(name):
            return vec[:, VEC[name]:VEC[name] + 1]

        rows = sb("rows", [P, U, G * 2 * D])
        onehot = sb("onehot", [P, U, G, W])
        turned = sb("turned", [P, U, SC])
        onehot_t = turned[0:W, :, 0:SC // 2].bitcast(BF16)
        window = sb("window", [W, U, 3 * D], BF16)
        window_p = sb("window_p", [3 * W, U, D], BF16)
        dst_free = sb("dst_free", [3 * W, U * SC], I16)
        onehot_p = turned[0:3 * W, :, 0:SC // 2].bitcast(BF16)
        node_of0 = sb("node_of0", [3 * W, SCS])
        node_of = sb("node_of", [3 * W, SCS])
        prod = sb("prod", [P, U, G * D])
        score = sb("score", [P, U, G * HEADS])
        clipped = sb("clipped", [P, U, G * HEADS])
        weight = sb("weight", [P, U, G * HEADS])
        weight_x = sb("weight_x", [P, U, G * D])
        index = sb("index", [P, U, G], I32)
        lo_hot = sb("lo_hot", [P, U, G, P], BF16)
        hi_hot = sb("hi_hot", [P, U, G, HI], BF16)
        edges0 = rows[:, :, :].rearrange("p u (h c) -> p (u h) c", h=2)
        edges0_top = rows[:, :, :].rearrange("p u c -> p (u c)").bitcast(BF16).rearrange("p (u c) -> p u c", u=U0)
        rest0 = prod
        rest0_top = prod[:, :, :].rearrange("p u c -> p (u c)").bitcast(BF16).rearrange("p (u c) -> p u c", u=U)
        part0 = turned[:, :, 0:SC // 2].bitcast(BF16)
        onehot0_b = lo_hot[:, :, :, :].rearrange("p u g e -> p (u g e)")[:, 0:U0 * SPLIT0 * W].rearrange(
            "p (u g w) -> p u g w", g=SPLIT0, w=W)
        onehot0_f = onehot[:, :, :, :].rearrange("p u g w -> p (u g w)")[:, 0:U0 * (G - SPLIT0) * W].rearrange(
            "p (u g w) -> p u g w", g=G - SPLIT0, w=W)
        same = lo_hot
        onehot_b = sb("onehot_b", [P, U, G, W], BF16)
        src_s = sb("src_s", [P, U, G])
        masked = sb("masked", [P, P])
        earlier = sb("earlier", [P, U, G])
        to_spare = sb("to_spare", [P, U, G])
        shift_by = sb("shift_by", [P, U, G])

        hid = [turned[:, 2 * l:2 * l + 2, :].rearrange("p a n -> p (a n)").rearrange("p (m n) -> p m n", n=T)
               for l in range(LANES)]
        tmp = [prod[:, 0, l * T:(l + 1) * T] for l in range(LANES)]
        res = [prod[:, 1, l * T:(l + 1) * T] for l in range(LANES)]
        cen = [prod[:, 2, l * T:(l + 1) * T] for l in range(LANES)]
        sqr = [prod[:, 3, l * T:(l + 1) * T] for l in range(LANES)]
        std = [sb(f"std{l}", [P, TJ]) for l in range(LANES)]
        inv = [sb(f"inv{l}", [P, TJ]) for l in range(LANES)]
        y = [sb(f"y{l}", [P, T]) for l in range(LANES)]
        y2 = [sb(f"y2{l}", [P, T]) for l in range(LANES)]
        node_rows = [sb(f"node_rows{l}", [P, TJ, 3 * D]) for l in range(LANES)]
        bias_qkv = sb("bias_qkv", [P, 3 * D])
        bias_ab = sb("bias_ab", [P, 2 * D])
        sqrt_of = sb("sqrt_of", [1, 2])
        parts_b = [sb(f"parts_b{l}", [P, TJ, 3 * D], BF16) for l in range(LANES)]
        rest = [sb(f"rest{l}", [P, TJ, D]) for l in range(LANES)]
        z_heads = sb("z_heads", [HEADS, 1])
        inv_z = sb("inv_z", [P, 1])
        dis = sb("dis", [P, HI])
        deg_sb = sb("deg_sb", [P, HI])
        deg_pos = sb("deg_pos", [P, HI])
        dis_raw = sb("dis_raw", [P, HI])
        low_sb = sb("low_sb", [P, 8])
        small = sb("small", [1, 4])
        small_i = sb("small_i", [1, 4], I32)

        ps = [ctx.enter_context(nc.psum_tensor(f"ps{i}", [P, 512], F32)) for i in range(8)]

        sp_waited = sem("sp_waited")
        pool_waited = sem("pool_waited")

        q_rows = nc.dram_tensor("q_rows", (NODES, 3 * D), BF16, kind="Internal").ap()
        kv_rows = nc.dram_tensor("kv_rows", (NODES, 2 * D), F32, kind="Internal").ap()
        a_rows = nc.dram_tensor("a_rows", (NODES, D), F32, kind="Internal").ap()
        b_rows = nc.dram_tensor("b_rows", (NODES, 3 * D), BF16, kind="Internal").ap()
        y_rows = nc.dram_tensor("y_rows", (NODES, 3 * D), BF16, kind="Internal").ap()
        dst_list = nc.dram_tensor("dst_list", (4, SPR, SC), I16, kind="Internal").ap()
        table = [nc.dram_tensor(f"table{i}", (NODES + 2 * P, D), F32, kind="Internal").ap() for i in range(TABLES)]

        loaded = sem("loaded")
        rows_loaded = sem("rows_loaded")
        const_set = sem("const_set")
        dst_minmax = sem("dst_minmax")
        low_ready = sem("low_ready")
        range_max = sem("range_max")
        passes_f = sem("passes_f")
        passes_i = sem("passes_i")
        src_split = sem("src_split")
        wq_scaled = sem("wq_scaled")
        biases_spread = sem("biases_spread")
        dst_narrow = sem("dst_narrow")
        list_stored = sem("list_stored")
        prep_dma = 17
        with nc.Block("prepare") as block:
            ids = rows[:, :, :].rearrange("p u c -> p (u c)").bitcast(I32)
            dst_i = ids[0:SPR, 0:4 * SC].rearrange("p (c e) -> p c e", c=4)
            ids2 = turned[:, :, :].rearrange("p u c -> p (u c)").bitcast(I32)
            dst_e = ids2[:, 0:SCS * G]
            assert NODES < 2 ** 15
            dst_16 = prod[0:SPR, 0:2, :].rearrange("p u c -> p (u c)").bitcast(I16).rearrange("p (c e) -> p c e", c=4)
            src_e = acc[:, 0:SCS * G].bitcast(I32)
            src_w = acc[:, SCS * G:2 * SCS * G].bitcast(I32)

            @block.sync
            def _(sp):
                sp.dma_start(dst_i, dst_rows).then_inc(rows_loaded, 16)
                sp.dma_start(cst[:, :], consts).then_inc(rows_loaded, 16)
                sp.dma_start(dst_e, dst_id).then_inc(rows_loaded, 16)
                sp.dma_start(src_e, src_id).then_inc(rows_loaded, 16)
                for tile, dram in ((x, xT), (wqkv_sb, wqkv), (wo_sb, wo), (aw1_sb, aw1),
                                   (aw2_sb, aw2), (we2_sb, we2), (wn2_sb, wn2), (w3t_sb, w3t), (vec, vectors),
                                   (bqkv_sb, row_bqkv), (be1_sb, row_be1), (be2_sb, row_be2)):
                    sp.dma_start(tile[:, :], dram).then_inc(loaded, 16)
                sp.dma_start(we1_sb[:, 0:D], we1[0:D, :]).then_inc(loaded, 16)
                sp.dma_start(we1_sb[:, D:2 * D], we1[D:2 * D, :]).then_inc(loaded, 16)
                sp.dma_start(w1_sb[:, :, :], w1.rearrange("(b p) n -> p b n", p=P)).then_inc(loaded, 16)
                sp.dma_start(w2_sb[:, :, :], w2.rearrange("(b p) n -> p b n", p=P)).then_inc(loaded, 16)
                sp.dma_start(wn1_sb[:, :, :], wn1.rearrange("(b p) n -> p b n", p=P)).then_inc(loaded, 16)
                sp.wait_ge(dst_narrow, 1)
                sp.dma_start(dst_list.rearrange("c p e -> p c e"), dst_16).then_inc(list_stored, 16)
                sp.wait_ge(list_stored, 16)
                sp.wait_ge(loaded, 16 * prep_dma)

            @block.vector
            def _(dve):
                dve.memset(ones[:, :], 1.0).then_inc(const_set, 1)
                dve.memset(zeros[:, :], 0.0).then_inc(const_set, 1)
                dve.memset(eps[:, :], LN_EPS).then_inc(const_set, 1)
                dve.memset(mean_col[:, :], 1.0 / D).then_inc(const_set, 1)
                dve.memset(sqrt_of[:, :], 1.0).then_inc(const_set, 1)
                dve.memset(count[:, :], 0.0).then_inc(const_set, 1)
                dve.wait_ge(rows_loaded, 64)
                dve.tensor_reduce(low_sb[0:SPR, 0:4], dst_i, AX.X, ALU.min).then_inc(dst_minmax, 1)
                dve.tensor_reduce(low_sb[0:SPR, 4:8], dst_i, AX.X, ALU.max).then_inc(dst_minmax, 1)
                dve.tensor_copy(dst_16, dst_i).then_inc(dst_narrow, 1)
                dve.wait_ge(dst_minmax, 2)
                dve.tensor_tensor(low_sb[0:SPR, 4:8], low_sb[0:SPR, 4:8], low_sb[0:SPR, 0:4],
                                  ALU.subtract).then_inc(dst_minmax, 1)
                pad_row = rel[:, :, :].rearrange("p s g -> p (s g)")
                dve.tensor_scalar(pad_row, src_e, 0.0, float(NODES + P + 1), ALU.is_lt, ALU.mult).then_inc(src_split, 1)
                dve.wait_ge(src_split, 1)
                dve.tensor_tensor(src_num[:, :], src_e, pad_row, ALU.add).then_inc(src_split, 1)
                dve.tensor_scalar(src_w, src_e, 7, None, ALU.arith_shift_right).then_inc(src_split, 1)
                dve.wait_ge(src_split, 3)
                dve.tensor_copy(src_hi[:, :], src_w).then_inc(src_split, 1)
                dve.wait_ge(src_split, 4)
                dve.tensor_scalar(src_w, src_e, 127, None, ALU.bitwise_and).then_inc(src_split, 1)
                dve.wait_ge(src_split, 5)
                dve.tensor_copy(src_lo[:, :], src_w).then_inc(src_split, 1)
                dve.wait_ge(low_ready, 1)
                dve.tensor_copy(base0[:, :], ps[0][0:1, 0:SCS]).then_inc(range_max, 1)
                dve.tensor_reduce(small[:, 0:1], ps[1][0:1, 0:SCS], AX.X, ALU.max).then_inc(range_max, 1)
                dve.tensor_copy(rel0[:, :, :], dst_e.rearrange("p (s g) -> p s g", g=G)).then_inc(range_max, 1)
                dve.wait_ge(range_max, 3)
                dve.tensor_tensor(rel0[:, :, :], rel0[:, :, :],
                                  ps[2][:, 0:SCS].unsqueeze(2).broadcast_to([P, SCS, G]),
                                  ALU.subtract).then_inc(range_max, 1)
                dve.tensor_scalar(node_of0[:, :], ps[2][0:3 * W, 0:SCS], node_col, None, ALU.add).then_inc(range_max, 1)
                dve.tensor_copy(small_i[:, 0:1], small[:, 0:1]).then_inc(passes_f, 1)
                dve.wait_ge(passes_f, 1)
                shift = W.bit_length() - 1
                dve.tensor_scalar(small_i[:, 1:2], small_i[:, 0:1], shift, None,
                                  ALU.arith_shift_right).then_inc(passes_f, 1)
                dve.wait_ge(passes_f, 2)
                for col, bodies in ((0, BODIES0), (1, BODIES)):
                    dve.tensor_scalar(pass_bodies[:, col:col + 1], small_i[:, 1:2], float(bodies), float(bodies),
                                      ALU.mult, ALU.add).then_inc(passes_i, 1)
                dve.wait_ge(loaded, 16 * prep_dma)
                dve.tensor_scalar(wqkv_sb[:, 0:D], wqkv_sb[:, 0:D], HEAD ** -0.5, None, ALU.mult).then_inc(wq_scaled, 1)
                dve.tensor_scalar(bqkv_sb[:, 0:D], bqkv_sb[:, 0:D], HEAD ** -0.5, None, ALU.mult).then_inc(wq_scaled, 1)
                dve.wait_ge(src_split, 6)
                dve.memset(acc[:, :], 0.0).then_inc(wq_scaled, 1)
                dve.wait_ge(biases_spread, 1)
                dve.tensor_copy(bias_qkv[:, :], ps[3][:, 0:3 * D]).then_inc(wq_scaled, 1)
                dve.tensor_copy(bias_ab[:, :], ps[4][:, 0:2 * D]).then_inc(wq_scaled, 1)

            @block.tensor
            def _(pe):
                pe.wait_ge(const_set, 6)
                pe.wait_ge(rows_loaded, 64)
                pe.wait_ge(dst_minmax, 3)
                for c in range(4):
                    cols = slice(c * SPR, (c + 1) * SPR)
                    nc.tensor.matmul(ps[0][0:1, cols], low_sb[0:SPR, c:c + 1], ident[0:SPR, 0:SPR],
                                     start=True, stop=True)
                    nc.tensor.matmul(ps[1][0:1, cols], low_sb[0:SPR, 4 + c:5 + c], ident[0:SPR, 0:SPR],
                                     start=True, stop=True)
                    last = nc.tensor.matmul(ps[2][:, cols], low_sb[0:SPR, c:c + 1].broadcast_to([SPR, P]),
                                            ident[0:SPR, 0:SPR], start=True, stop=True)
                last.then_inc(low_ready, 1)
                pe.wait_ge(loaded, 16 * prep_dma)
                pe.wait_ge(wq_scaled, 2)
                nc.tensor.matmul(ps[3][:, 0:3 * D], ones[0:1, 0:P], bqkv_sb[:, :], start=True, stop=True)
                nc.tensor.matmul(ps[4][:, 0:2 * D], ones[0:1, 0:P], be1_sb[:, :],
                                 start=True, stop=True).then_inc(biases_spread, 1)

        def all_bodies(eng, col=1, bodies=BODIES):
            return eng.value_load(pass_bodies[0:1, col:col + 1], min_val=bodies, max_val=bodies * PASSES_MAX)

        def window_starts(eng_type, i, number=U):
            return nc.values_load_multi_w_load_instructions(base[0:1, ds(i * number, number)], engines=(eng_type,),
                                                            min_val=0, max_val=NODES - W)[1]

        def windows_reset(dve, windows_set):
            dve.tensor_copy(rel[:, :, :], rel0[:, :, :]).then_inc(windows_set, 1)
            dve.tensor_scalar(base[:, :], base0[:, :], float(NODES - W), None, ALU.min).then_inc(windows_set, 1)

        def nodes_reset(dve, windows_set):
            dve.tensor_copy(node_of[:, :], node_of0[:, :]).then_inc(windows_set, 1)

        def nodes_move(dve, windows_moved):
            dve.tensor_scalar(node_of[:, :], node_of[:, :], float(W), None, ALU.add).then_inc(windows_moved, BODIES)

        def windows_move(dve, windows_moved, bodies=BODIES):
            dve.tensor_scalar(rel[:, :, :], rel[:, :, :], float(W), None, ALU.subtract).then_inc(windows_moved, bodies)
            dve.tensor_scalar(base[:, :], base[:, :], float(W), float(NODES - W), ALU.add,
                              ALU.min).then_inc(windows_moved, bodies)

        def bank(l, b):
            return ps[4 * l + b]

        def columns(c):
            return ds(c * T, T)

        centred_ps = sem("centred_ps")
        squared = sem("squared")
        centred = sem("centred")
        variance_ps = sem("variance_ps")
        std_ready = sem("std_ready")
        inverse_ready = sem("inverse_ready")
        inverse_ps = sem("inverse_ps")
        normed = sem("normed")

        def norm_pe(pe, nth, ready, count_of):
            for l in range(LANES):
                pe.wait_ge(ready, count_of(l) + 1)
                nc.tensor.matmul(bank(l, 1)[:, 0:T], centre_m, res[l], start=True, stop=True).then_inc(centred_ps, 1)
            for l in range(LANES):
                pe.wait_ge(squared, nth + l + 1)
                for j in range(TJ):
                    last = nc.tensor.matmul(bank(l, 2)[:, j:j + 1], sqr[l][:, j * P:(j + 1) * P], mean_col[:, :],
                                            start=True, stop=True)
                last.then_inc(variance_ps, 1)
            for l in range(LANES):
                pe.wait_ge(inverse_ready, nth + l + 1)
                for j in range(TJ):
                    last = nc.tensor.matmul(bank(l, 3)[:, j * P:(j + 1) * P],
                                            inv[l][:, j:j + 1].broadcast_to([P, P]), ident, start=True, stop=True)
                last.then_inc(inverse_ps, 1)

        def norm_act(act, nth):
            for l in range(LANES):
                act.wait_ge(centred_ps, nth + l + 1)
                act.activation(sqr[l], bank(l, 1)[:, 0:T], ACT.Square).then_inc(squared, 1)
                act.activation(cen[l], bank(l, 1)[:, 0:T], ACT.Copy).then_inc(centred, 1)
            for l in range(LANES):
                act.wait_ge(variance_ps, nth + l + 1)
                act.activation(std[l][:, :], bank(l, 2)[:, 0:TJ], ACT.Sqrt, bias=eps[:, :]).then_inc(std_ready, 1)

        def norm_dve(dve, nth):
            for l in range(LANES):
                dve.wait_ge(std_ready, nth + l + 1)
                dve.reciprocal(inv[l][:, :], std[l][:, :]).then_inc(inverse_ready, 1)
            for l in range(LANES):
                dve.wait_ge(centred, nth + l + 1)
                dve.wait_ge(inverse_ps, nth + l + 1)
                dve.tensor_tensor(y[l][:, :], cen[l], bank(l, 3)[:, 0:T], ALU.mult).then_inc(normed, 1)

        split_step = sem("split_step")
        SPLITS = 4

        def split_rows(pool, done, l, col):
            part = lambda q: parts_b[l][:, :, q * D:(q + 1) * D]
            whole = node_rows[l][:, :, col:col + D]
            pool.tensor_copy(part(0), whole).then_inc(split_step, 1)
            pool.wait_ge(split_step, done * SPLITS + 1)
            pool.sem_inc(pool_waited, 1)
            pool.tensor_tensor(rest[l][:, :, :], whole, part(0), ALU.subtract).then_inc(split_step, 1)
            pool.wait_ge(split_step, done * SPLITS + 2)
            pool.sem_inc(pool_waited, 1)
            pool.tensor_copy(part(1), rest[l][:, :, :]).then_inc(split_step, 1)
            pool.wait_ge(split_step, done * SPLITS + 3)
            pool.sem_inc(pool_waited, 1)
            pool.tensor_tensor(part(2), rest[l][:, :, :], part(1), ALU.subtract).then_inc(split_step, 1)

        def load_sqrt_table(act):
            act.activation(sqrt_of[:, 1:2], sqrt_of[:, 0:1], ACT.Sqrt)

        def one_hot(dve, to, i, first=0, number=U):
            return dve.tensor_tensor(to[:, first:first + number, :, :].rearrange("p u g w -> p (u g) w"),
                                     iota_w.unsqueeze(1).broadcast_to([P, number * G, W]),
                                     rel[:, ds(i * U + first, number), :].rearrange("p s g -> p (s g)").unsqueeze(2)
                                     .broadcast_to([P, number * G, W]), ALU.is_equal)


        edges_loaded = [sem(f"edges_loaded{k}") for k in range(U0)]
        hot0 = sem("hot0")
        summed0 = sem("summed0")
        added0 = sem("added0")
        rests0 = sem("rests0")
        parts0 = sem("parts0")
        windows0 = sem("windows0")
        with nc.Block("layer0_edges") as block:
            @block.sync
            def _(sp):
                total = all_bodies(sp, 0, BODIES0)
                sp.sem_inc(summed0, U0)
                with sp.Fori(0, total, BODIES0) as first:
                    def load(s, k, at):
                        sp.wait_ge(summed0, s + 1)
                        sp.sem_inc(sp_waited, 1)
                        sp.dma_start(edges0[:, k, :], edge_attr[at, :].rearrange("(p g) f -> p (g f)", g=G)
                                     ).then_inc(edges_loaded[k], 16)

                    with sp.Fori(0, BODIES0 - 1) as i:
                        for k in range(U0):
                            load((first + i) * U0 + k, k, ds((i * U0 + k) * SC, SC))
                    for k in range(U0):
                        s = (BODIES0 - 1) * U0 + k
                        at = min(s * SC, E - SC)
                        load(first * U0 + s, k, slice(at, at + SC))
                for k in range(AHEAD0):
                    load(total * U0 + k, k, slice(k * SC, (k + 1) * SC))

            @block.gpsimd
            def _(pool):
                total = all_bodies(pool, 0, BODIES0)
                with pool.Fori(0, total) as j:
                    for k in range(U0):
                        pool.wait_ge(rests0, j * U0 + k + 1)
                        pool.wait_ge(summed0, j * U0 + k + U0 - U + 1)
                        pool.sem_inc(pool_waited, 1)
                        pool.tensor_tensor(part0[:, k % U, 0:SPLIT0 * D], rest0[:, k % U, 0:SPLIT0 * D],
                                           rest0_top[:, k % U, 1:2 * SPLIT0 * D:2], ALU.subtract).then_inc(parts0, 1)

            @block.vector
            def _(dve):
                total = all_bodies(dve, 0, BODIES0)
                dve.sem_inc(added0, U0)

                def remains(j, k):
                    dve.wait_ge(edges_loaded[k], j * 16 + 16)
                    dve.tensor_tensor(rest0[:, k % U, 0:SPLIT0 * D], edges0[:, k, 0:SPLIT0 * D],
                                      edges0_top[:, k, 1:2 * SPLIT0 * D:2], ALU.subtract).then_inc(rests0, 1)

                windows_reset(dve, windows0)
                dve.wait_ge(windows0, 2)
                for k in range(AHEAD0):
                    remains(0, k)
                with dve.Fori(0, total, BODIES0) as first:
                    with dve.Fori(0, BODIES0) as i:
                        dve.wait_ge(summed0, (first + i) * U0 + U0)
                        for to, g, e in ((onehot0_b, 0, SPLIT0), (onehot0_f, SPLIT0, G)):
                            dve.tensor_tensor(to[:, :, :, :], iota_w.unsqueeze(1).unsqueeze(1)
                                              .broadcast_to([P, U0, e - g, W]),
                                              rel[:, ds(i * U0, U0), g:e].unsqueeze(3)
                                              .broadcast_to([P, U0, e - g, W]), ALU.is_equal).then_inc(hot0, U0)
                        at = window_starts(mybir.EngineType.DVE, i, U0)
                        for k in range(U0):
                            s = (first + i) * U0 + k
                            remains(first + i + (k + AHEAD0) // U0, (k + AHEAD0) % U0)
                            dve.wait_ge(summed0, s + U0 + 1)
                            dve.wait_ge(added0, s + U0)
                            dve.tensor_tensor(acc[:, ds(at[k], W)], acc[:, ds(at[k], W)], ps[k][:, 0:W],
                                              ALU.add).then_inc(added0, 1)
                    windows_move(dve, windows0, BODIES0)
                    dve.wait_ge(windows0, 2 * first + 2 * BODIES0 + 2)

            @block.tensor
            def _(pe):
                total = all_bodies(pe, 0, BODIES0)
                with pe.Fori(0, total) as j:
                    for k in range(U0):
                        s = j * U0 + k
                        pe.wait_ge(hot0, j * 2 * U0 + 2 * U0)
                        pe.wait_ge(edges_loaded[k], j * 16 + 16)
                        pe.wait_ge(added0, s + 1)
                        for g in range(SPLIT0, G):
                            nc.tensor.matmul(ps[k][:, 0:W], edges0[:, k, g * D:(g + 1) * D],
                                             onehot0_f[:, k, g - SPLIT0, :], start=(g == SPLIT0), stop=False)
                        for g in range(SPLIT0):
                            nc.tensor.matmul(ps[k][:, 0:W], edges0_top[:, k, 2 * g * D + 1:2 * (g + 1) * D:2],
                                             onehot0_b[:, k, g, :], start=False, stop=False)
                        pe.wait_ge(rests0, s + 1)
                        for g in range(SPLIT0):
                            nc.tensor.matmul(ps[k][:, 0:W], rest0_top[:, k % U, 2 * g * D + 1:2 * (g + 1) * D:2],
                                             onehot0_b[:, k, g, :], start=False, stop=False)
                        pe.wait_ge(parts0, s + 1)
                        for g in range(SPLIT0):
                            last = nc.tensor.matmul(ps[k][:, 0:W], part0[:, k % U, g * D:(g + 1) * D],
                                                    onehot0_b[:, k, g, :], start=False, stop=(g == SPLIT0 - 1))
                        last.then_inc(summed0, 1)

        tile_done = sem("tile_done")
        hidden_ps0 = sem("hidden_ps0")
        hidden0 = sem("hidden0")
        mlp0 = sem("mlp0")
        sum0 = sem("sum0")
        x_kept = sem("x_kept")
        qkv_ps = sem("qkv_ps")
        qkv_rows = sem("qkv_rows")
        qkv_stored = sem("qkv_stored")
        MB = HIDDEN // P
        with nc.Block("layer0_nodes") as block:
            @block.tensor
            def _(pe):
                with pe.Fori(0, STEPS) as n:
                    for l in range(LANES):
                        c = n * LANES + l
                        pe.wait_ge(tile_done, c + 1)
                        for m in range(MB):
                            nc.tensor.matmul(bank(l, m)[:, 0:T], w1_sb[:, 0, m * P:(m + 1) * P], acc[:, columns(c)],
                                             start=True, stop=False)
                            nc.tensor.matmul(bank(l, m)[:, 0:T], w1_sb[:, 1, m * P:(m + 1) * P], x[:, columns(c)],
                                             start=False, stop=True).then_inc(hidden_ps0, 1)
                    for l in range(LANES):
                        for m in range(MB):
                            pe.wait_ge(hidden0, (n * LANES + l) * MB + m + 1)
                            last = nc.tensor.matmul(bank(l, 0)[:, 0:T], w2_sb[:, m, :], hid[l][:, m, :],
                                                    start=(m == 0), stop=(m == MB - 1))
                        last.then_inc(mlp0, 1)
                    norm_pe(pe, n * LANES, sum0, lambda l: n * LANES + l)
                    for l in range(LANES):
                        pe.wait_ge(normed, n * LANES + l + 1)
                        for j in range(TJ):
                            nc.tensor.matmul(bank(l, j)[:, 0:3 * D], y[l][:, j * P:(j + 1) * P], wqkv_sb[:, :],
                                             start=True, stop=True).then_inc(qkv_ps, 1)

            @block.scalar
            def _(act):
                with act.Fori(0, STEPS) as n:
                    load_sqrt_table(act)
                    for l in range(LANES):
                        for m in range(MB):
                            act.wait_ge(hidden_ps0, (n * LANES + l) * MB + m + 1)
                            act.activation(hid[l][:, m, :], bank(l, m)[:, 0:T], ACT.Relu,
                                           bias=v(f"b1_{m}")).then_inc(hidden0, 1)
                    norm_act(act, n * LANES)
                    for l in range(LANES):
                        act.wait_ge(normed, n * LANES + l + 1)
                        act.activation(x[:, columns(n * LANES + l)], y[l][:, :], ACT.Copy).then_inc(x_kept, 1)

            @block.vector
            def _(dve):
                with dve.Fori(0, STEPS) as n:
                    for l in range(LANES):
                        c = n * LANES + l
                        dve.wait_ge(mlp0, c + 1)
                        dve.scalar_tensor_tensor(res[l], bank(l, 0)[:, 0:T], v("b2"), x[:, columns(c)], ALU.add,
                                                 ALU.add).then_inc(sum0, 1)
                    norm_dve(dve, n * LANES)
                    for l in range(LANES):
                        for j in range(TJ):
                            dve.wait_ge(qkv_ps, (n * LANES + l) * TJ + j + 1)
                            dve.tensor_tensor(node_rows[l][:, j, :], bank(l, j)[:, 0:3 * D], bias_qkv[:, :],
                                              ALU.add).then_inc(qkv_rows, 1)

            @block.gpsimd
            def _(pool):
                with pool.Fori(0, STEPS) as n:
                    for l in range(LANES):
                        c = n * LANES + l
                        pool.wait_ge(qkv_rows, c * TJ + TJ)
                        pool.sem_inc(pool_waited, 1)
                        split_rows(pool, 0 + c, l, 0)

            @block.sync
            def _(sp):
                sp.sem_inc(tile_done, LANES)
                with sp.Fori(0, STEPS) as n:
                    for l in range(LANES):
                        c = n * LANES + l
                        sp.wait_ge(qkv_rows, c * TJ + TJ)
                        sp.sem_inc(sp_waited, 1)
                        sp.wait_ge(split_step, (0 + c) * SPLITS + SPLITS)
                        sp.sem_inc(sp_waited, 1)
                        sp.dma_start(q_rows[columns(c), :].rearrange("(j p) f -> p j f", p=P),
                                     parts_b[l][:, :, :]).then_inc(qkv_stored, 16)
                        sp.dma_start(kv_rows[columns(c), :].rearrange("(j p) f -> p j f", p=P),
                                     node_rows[l][:, :, D:3 * D]).then_inc(qkv_stored, 16)
                        sp.wait_ge(qkv_stored, c * 32 + 32)
                        sp.sem_inc(sp_waited, 1)
                        sp.wait_ge(x_kept, c + 1)
                        sp.sem_inc(tile_done, 1)

        index_loaded1 = [sem(f"index_loaded1_{k}") for k in range(U)]
        window_loaded1 = [sem(f"window_loaded1_{k}") for k in range(U)]
        gathered1 = [sem(f"gathered1_{k}") for k in range(U)]
        hot_f1 = sem("hot_f1")
        hot_t1 = sem("hot_t1")
        dst_loaded1 = sem("dst_loaded1")
        expanded1 = sem("expanded1")
        product1 = sem("product1")
        score1 = sem("score1")
        clipped1 = sem("clipped1")
        weight1 = sem("weight1")
        message1 = sem("message1")
        summed1 = sem("summed1")
        added1 = sem("added1")
        windows1 = sem("windows1")
        cleared1 = sem("cleared1")
        tables_zeroed = sem("tables_zeroed")
        Z = ps[7][0:HEADS, 0:W]
        with nc.Block("layer1_edges") as block:
            @block.sync
            def _(sp):
                total = all_bodies(sp)
                sp.sem_inc(message1, U)
                sp.sem_inc(expanded1, U)
                sp.sem_inc(hot_t1, U)
                for k in range(U):
                    sp.dma_start(index[:, k, :], src_index[:, k * G:(k + 1) * G]).then_inc(index_loaded1[k], 16)
                with sp.Fori(0, total, BODIES) as first:
                    sp.wait_ge(windows1, 3 * first + 3)
                    sp.sem_inc(sp_waited, 1)
                    with sp.Fori(0, BODIES) as i:
                        at = window_starts(mybir.EngineType.SP, i)
                        sp.wait_ge(hot_t1, (first + i) * U + U)
                        sp.sem_inc(sp_waited, 1)
                        sp.dma_start(dst_free[:, :], dst_list.rearrange("c p e -> (c p) e")[ds(i * U, U), :]
                                     .rearrange("u e -> (u e)").unsqueeze(0).broadcast_to([3 * W, U * SC])
                                     ).then_inc(dst_loaded1, 16)
                        for k in range(U):
                            s = (first + i) * U + k
                            sp.wait_ge(expanded1, s + 1)
                            sp.sem_inc(sp_waited, 1)
                            sp.dma_start(window_p[:, k, :],
                                         q_rows.rearrange("n (q f) -> (n q) f", q=3)[ds(at[k] * 3, 3 * W), :]
                                         ).then_inc(window_loaded1[k], 16)
                        for k in range(U):
                            sp.wait_ge(gathered1[k], (first + i) * 16 * G + 16 * G)
                            sp.sem_inc(sp_waited, 1)
                            sp.dma_start(index[:, k, :], src_index[:, ds((i * U + U + k) * G, G)]
                                         ).then_inc(index_loaded1[k], 16)
                for k in range(U):
                    sp.wait_ge(index_loaded1[k], total * 16 + 16)
                    sp.sem_inc(sp_waited, 1)

            @block.gpsimd
            def _(pool):
                total = all_bodies(pool)
                with pool.Fori(0, total) as j:
                    for k in range(U):
                        pool.wait_ge(index_loaded1[k], j * 16 + 16)
                        pool.wait_ge(message1, j * U + k + 1)
                        pool.sem_inc(pool_waited, 1)
                        for g in range(G):
                            pool.indirect_dma_start(rows[:, k, g * 2 * D:(g + 1) * 2 * D], None, kv_rows[:, :],
                                                    bass.IndirectOffsetOnAxis(ap=index[:, k, g:g + 1], axis=0)
                                                    ).then_inc(gathered1[k], 16)

            @block.scalar
            def _(act):
                total = all_bodies(act)
                for t in range(TABLES):
                    act.dma_start(table[t].rearrange("(j p) f -> p j f", p=P),
                                  zeros[:, :].unsqueeze(1).broadcast_to([P, NODES // P + 2, D])
                                  ).then_inc(tables_zeroed, 16)
                with act.Fori(0, total) as j:
                    def exp(k):
                        act.wait_ge(clipped1, j * U + k + 1)
                        act.wait_ge(summed1, j * U + k + 1)
                        act.activation(weight[:, k, :], clipped[:, k, :], ACT.Exp).then_inc(weight1, 1)

                    exp(0)
                    exp(1)
                    exp(2)
                    exp(3)
                act.wait_ge(tables_zeroed, 16 * TABLES)

            @block.vector
            def _(dve):
                total = all_bodies(dve)
                dve.sem_inc(product1, 2)
                dve.sem_inc(added1, 2)
                dve.memset(acc[:, :], 0.0).then_inc(cleared1, 1)
                windows_reset(dve, windows1)
                nodes_reset(dve, windows1)
                dve.wait_ge(windows1, 3)
                dve.wait_ge(cleared1, 1)
                with dve.Fori(0, total, BODIES) as first:
                    with dve.Fori(0, BODIES) as i:
                        def turned(k):
                            dve.wait_ge(dst_loaded1, (first + i) * 16 + 16)
                            dve.wait_ge(expanded1, (first + i) * U + k + 1)
                            dve.tensor_scalar(onehot_p[:, k, :], dst_free[:, k * SC:(k + 1) * SC],
                                              node_of[:, ds(i * U + k, 1)], None, ALU.is_equal).then_inc(hot_t1, 1)

                        def scores(k):
                            s = (first + i) * U + k
                            dve.wait_ge(expanded1, s + U + 1)
                            dve.wait_ge(gathered1[k], (first + i) * 16 * G + 16 * G)
                            dve.tensor_tensor(prod[:, k, :].rearrange("p (g f) -> p g f", g=G),
                                              ps[2 + k % 2][:, :].rearrange("p (g f) -> p g f", g=G),
                                              rows[:, k, :].rearrange("p (g f) -> p g f", g=G)[:, :, 0:D],
                                              ALU.mult).then_inc(product1, 1)
                            dve.wait_ge(product1, s + 3)
                            dve.tensor_reduce(score[:, k, :], prod[:, k, :].rearrange("p (h c) -> p h c", c=HEAD),
                                              AX.X, ALU.add).then_inc(score1, 1)
                            dve.wait_ge(score1, s + 1)
                            dve.tensor_scalar(clipped[:, k, :], score[:, k, :], CLIP, -CLIP, ALU.min,
                                              ALU.max).then_inc(clipped1, 1)

                        def message(k):
                            s = (first + i) * U + k
                            dve.wait_ge(weight1, s + 1)
                            dve.tensor_tensor(
                                prod[:, k, :].rearrange("p (g h c) -> p g h c", g=G, c=HEAD),
                                rows[:, k, :].rearrange("p (g f) -> p g f", g=G)[:, :, D:2 * D]
                                .rearrange("p g (h c) -> p g h c", c=HEAD),
                                weight[:, k, :].rearrange("p (g h) -> p g h", g=G).unsqueeze(3)
                                .broadcast_to([P, G, HEADS, HEAD]), ALU.mult).then_inc(message1, 1)

                        def add(k):
                            s = (first + i) * U + k
                            dve.wait_ge(summed1, s + U + 1)
                            dve.wait_ge(added1, s + 2)
                            dve.tensor_tensor(acc[:, ds(at[k], W)], acc[:, ds(at[k], W)], ps[4 + k % 2][:, 0:W],
                                              ALU.add).then_inc(added1, 1)

                        dve.wait_ge(summed1, (first + i) * U + U)
                        turned(0)
                        turned(1)
                        scores(0)
                        one_hot(dve, onehot, i).then_inc(hot_f1, U)
                        message(0)
                        turned(2)
                        turned(3)
                        at = window_starts(mybir.EngineType.DVE, i)
                        scores(1)
                        for k in range(2, U):
                            scores(k)
                            message(k - 1)
                            add(k - 2)
                        message(U - 1)
                        add(U - 2)
                        add(U - 1)
                    windows_move(dve, windows1)
                    nodes_move(dve, windows1)
                    dve.wait_ge(windows1, 3 * first + 3 * BODIES + 3)

            @block.tensor
            def _(pe):
                total = all_bodies(pe)
                pe.sem_inc(summed1, U)
                nc.tensor.matmul(Z, zeros[:, 0:HEADS], zeros[:, 0:W], start=True, stop=False, skip_group_check=True)
                with pe.Fori(0, total) as j:
                    def expand(k):
                        pe.wait_ge(hot_t1, j * U + k + U + 1)
                        pe.wait_ge(window_loaded1[k], j * 16 + 16)
                        pe.wait_ge(product1, j * U + k + 1)
                        for g in range(G):
                            last = nc.tensor.matmul(ps[2 + k % 2][:, g * P:(g + 1) * P], onehot_p[:, k, g::G],
                                                    window_p[:, k, :], start=True, stop=True)
                        last.then_inc(expanded1, 1)

                    def window_sum(k):
                        pe.wait_ge(message1, j * U + k + U + 1)
                        pe.wait_ge(hot_f1, j * U + k + 1)
                        pe.wait_ge(added1, j * U + k + 1)
                        for g in range(G):
                            nc.tensor.matmul(ps[4 + k % 2][:, 0:W], prod[:, k, g * D:(g + 1) * D],
                                             onehot[:, k, g, :], start=(g == 0), stop=(g == G - 1))
                        for g in range(G):
                            last = nc.tensor.matmul(Z, weight[:, k, g * HEADS:(g + 1) * HEADS], onehot[:, k, g, :],
                                                    start=False, stop=False, skip_group_check=True)
                        last.then_inc(summed1, 1)

                    expand(0)
                    expand(1)
                    expand(2)
                    window_sum(0)
                    expand(3)
                    window_sum(1)
                    window_sum(2)
                    window_sum(3)

        z_summed = sem("z_summed")
        z_spread = sem("z_spread")
        heads1 = sem("heads1")
        out_ps1 = sem("out_ps1")
        sum1a = sem("sum1a")
        scaled1a = sem("scaled1a")
        ffn_ps1 = sem("ffn_ps1")
        ffn_relu1 = sem("ffn_relu1")
        ffn_out1 = sem("ffn_out1")
        sum1b = sem("sum1b")
        scaled1b = sem("scaled1b")
        sum1c = sem("sum1c")
        ab_ps = sem("ab_ps")
        ab_rows = sem("ab_rows")
        ab_stored = sem("ab_stored")

        def nth1(n, q):
            return (n * 3 + q) * LANES + NTILES

        with nc.Block("layer1_nodes") as block:
            @block.tensor
            def _(pe):
                pe.wait_ge(z_summed, 1)
                nc.tensor.matmul(ps[6][:, 0:1], head_of, z_heads[:, :], start=True, stop=True).then_inc(z_spread, 1)
                with pe.Fori(0, STEPS) as n:
                    def tile(l):
                        return n * LANES + l

                    for l in range(LANES):
                        pe.wait_ge(heads1, tile(l) + 1)
                        nc.tensor.matmul(bank(l, 0)[:, 0:T], wo_sb[:, :], tmp[l],
                                         start=True, stop=True).then_inc(out_ps1, 1)
                    norm_pe(pe, nth1(n, 0), sum1a, tile)
                    for l in range(LANES):
                        pe.wait_ge(scaled1a, tile(l) + 1)
                        nc.tensor.matmul(bank(l, 0)[:, 0:T], aw1_sb[:, :], y2[l][:, :],
                                         start=True, stop=True).then_inc(ffn_ps1, 1)
                    for l in range(LANES):
                        pe.wait_ge(ffn_relu1, tile(l) + 1)
                        nc.tensor.matmul(bank(l, 2)[:, 0:T], aw2_sb[:, :], hid[l][:, 0, :],
                                         start=True, stop=True).then_inc(ffn_out1, 1)
                    norm_pe(pe, nth1(n, 1), sum1b, tile)
                    norm_pe(pe, nth1(n, 2), sum1c, tile)
                    for l in range(LANES):
                        pe.wait_ge(normed, nth1(n, 2) + l + 1)
                        for j in range(TJ):
                            nc.tensor.matmul(bank(l, j)[:, 0:2 * D], y[l][:, j * P:(j + 1) * P], we1_sb[:, :],
                                             start=True, stop=True).then_inc(ab_ps, 1)

            @block.scalar
            def _(act):
                with act.Fori(0, STEPS) as n:
                    load_sqrt_table(act)
                    norm_act(act, nth1(n, 0))
                    for l in range(LANES):
                        act.wait_ge(ffn_ps1, n * LANES + l + 1)
                        act.activation(hid[l][:, 0, :], bank(l, 0)[:, 0:T], ACT.Relu,
                                       bias=v("a_b1")).then_inc(ffn_relu1, 1)
                    norm_act(act, nth1(n, 1))
                    norm_act(act, nth1(n, 2))
                    for l in range(LANES):
                        act.wait_ge(normed, nth1(n, 2) + l + 1)
                        act.activation(x[:, columns(n * LANES + l)], y[l][:, :], ACT.Copy).then_inc(x_kept, 1)

            @block.vector
            def _(dve):
                dve.tensor_reduce(z_heads[:, :], Z, AX.X, ALU.add).then_inc(z_summed, 1)
                dve.wait_ge(z_spread, 1)
                dve.reciprocal(inv_z[:, :], ps[6][:, 0:1]).then_inc(z_summed, 1)
                dve.wait_ge(z_summed, 2)
                with dve.Fori(0, STEPS) as n:
                    for l in range(LANES):
                        c = n * LANES + l
                        dve.wait_ge(tile_done, NTILES + c + 1)
                        dve.tensor_scalar(tmp[l], acc[:, columns(c)], inv_z[:, :], None, ALU.mult).then_inc(heads1, 1)
                    for l in range(LANES):
                        c = n * LANES + l
                        dve.wait_ge(out_ps1, c + 1)
                        dve.scalar_tensor_tensor(res[l], bank(l, 0)[:, 0:T], v("bO"), x[:, columns(c)], ALU.add,
                                                 ALU.add).then_inc(sum1a, 1)
                    norm_dve(dve, nth1(n, 0))
                    for l in range(LANES):
                        dve.wait_ge(normed, nth1(n, 0) + l + 1)
                        dve.tensor_scalar(y2[l][:, :], y[l][:, :], v("ln1_g"), v("ln1_b"), ALU.mult,
                                          ALU.add).then_inc(scaled1a, 1)
                    for l in range(LANES):
                        dve.wait_ge(scaled1a, n * LANES + l + 1)
                        dve.wait_ge(ffn_out1, n * LANES + l + 1)
                        dve.scalar_tensor_tensor(res[l], bank(l, 2)[:, 0:T], v("a_b2"), y2[l][:, :], ALU.add,
                                                 ALU.add).then_inc(sum1b, 1)
                    norm_dve(dve, nth1(n, 1))
                    for l in range(LANES):
                        dve.wait_ge(normed, nth1(n, 1) + l + 1)
                        dve.tensor_scalar(y2[l][:, :], y[l][:, :], v("ln2_g"), v("ln2_b"), ALU.mult,
                                          ALU.add).then_inc(scaled1b, 1)
                    for l in range(LANES):
                        dve.wait_ge(scaled1b, n * LANES + l + 1)
                        dve.tensor_tensor(res[l], y2[l][:, :], x[:, columns(n * LANES + l)], ALU.add).then_inc(sum1c, 1)
                    norm_dve(dve, nth1(n, 2))
                    for l in range(LANES):
                        for j in range(TJ):
                            dve.wait_ge(ab_ps, (n * LANES + l) * TJ + j + 1)
                            dve.tensor_tensor(node_rows[l][:, j, 0:2 * D], bank(l, j)[:, 0:2 * D], bias_ab[:, :],
                                              ALU.add).then_inc(ab_rows, 1)

            @block.gpsimd
            def _(pool):
                with pool.Fori(0, STEPS) as n:
                    for l in range(LANES):
                        c = n * LANES + l
                        pool.wait_ge(ab_rows, c * TJ + TJ)
                        pool.sem_inc(pool_waited, 1)
                        split_rows(pool, NTILES + c, l, D)

            @block.sync
            def _(sp):
                with sp.Fori(0, STEPS) as n:
                    for l in range(LANES):
                        c = n * LANES + l
                        sp.wait_ge(ab_rows, c * TJ + TJ)
                        sp.sem_inc(sp_waited, 1)
                        sp.dma_start(a_rows[columns(c), :].rearrange("(j p) f -> p j f", p=P),
                                     node_rows[l][:, :, 0:D]).then_inc(ab_stored, 16)
                        sp.wait_ge(split_step, (NTILES + c) * SPLITS + SPLITS)
                        sp.sem_inc(sp_waited, 1)
                        sp.dma_start(b_rows[columns(c), :].rearrange("(j p) f -> p j f", p=P),
                                     parts_b[l][:, :, :]).then_inc(ab_stored, 16)
                        sp.wait_ge(ab_stored, c * 32 + 32)
                        sp.sem_inc(sp_waited, 1)
                        sp.wait_ge(x_kept, NTILES + c + 1)
                        sp.sem_inc(tile_done, 1)

        index_loaded2 = [sem(f"index_loaded2_{k}") for k in range(U)]
        window_loaded2 = [sem(f"window_loaded2_{k}") for k in range(U)]
        gathered2 = [sem(f"gathered2_{k}") for k in range(U)]
        hot_f2 = sem("hot_f2")
        hot_t2 = sem("hot_t2")
        dst_loaded2 = sem("dst_loaded2")
        expanded2 = sem("expanded2")
        pair2 = sem("pair2")
        relu2 = sem("relu2")
        split2 = sem("split2")
        summed2 = sem("summed2")
        added2 = sem("added2")
        windows2 = sem("windows2")
        cleared2 = sem("cleared2")
        DEG = ps[7][:, 0:HI]
        with nc.Block("layer2_edges") as block:
            @block.sync
            def _(sp):
                total = all_bodies(sp)
                sp.sem_inc(relu2, U)
                sp.sem_inc(expanded2, U)
                sp.sem_inc(hot_t2, U)
                for k in range(U):
                    sp.dma_start(index[:, k, :], src_index[:, k * G:(k + 1) * G]).then_inc(index_loaded2[k], 16)
                with sp.Fori(0, total, BODIES) as first:
                    sp.wait_ge(windows2, 4 * first + 3)
                    sp.sem_inc(sp_waited, 1)
                    with sp.Fori(0, BODIES) as i:
                        at = window_starts(mybir.EngineType.SP, i)
                        sp.wait_ge(hot_t2, (first + i) * U + U)
                        sp.sem_inc(sp_waited, 1)
                        sp.dma_start(dst_free[:, :], dst_list.rearrange("c p e -> (c p) e")[ds(i * U, U), :]
                                     .rearrange("u e -> (u e)").unsqueeze(0).broadcast_to([3 * W, U * SC])
                                     ).then_inc(dst_loaded2, 16)
                        for k in range(U):
                            s = (first + i) * U + k
                            sp.wait_ge(expanded2, s + 1)
                            sp.sem_inc(sp_waited, 1)
                            sp.dma_start(window_p[:, k, :],
                                         b_rows.rearrange("n (q f) -> (n q) f", q=3)[ds(at[k] * 3, 3 * W), :]
                                         ).then_inc(window_loaded2[k], 16)
                        for k in range(U):
                            sp.wait_ge(gathered2[k], (first + i) * 16 * G + 16 * G)
                            sp.sem_inc(sp_waited, 1)
                            sp.dma_start(index[:, k, :], src_index[:, ds((i * U + U + k) * G, G)]
                                         ).then_inc(index_loaded2[k], 16)
                for k in range(U):
                    sp.wait_ge(index_loaded2[k], total * 16 + 16)
                    sp.sem_inc(sp_waited, 1)

            @block.gpsimd
            def _(pool):
                total = all_bodies(pool)
                with pool.Fori(0, total) as j:
                    for k in range(U):
                        pool.wait_ge(index_loaded2[k], j * 16 + 16)
                        pool.wait_ge(pair2, j * U + k + 1)
                        pool.sem_inc(pool_waited, 1)
                        for g in range(G):
                            pool.indirect_dma_start(rows[:, k, g * D:(g + 1) * D], None, a_rows[:, :],
                                                    bass.IndirectOffsetOnAxis(ap=index[:, k, g:g + 1], axis=0)
                                                    ).then_inc(gathered2[k], 16)

            @block.scalar
            def _(act):
                total = all_bodies(act)
                with act.Fori(0, total) as j:
                    def relu(k):
                        act.wait_ge(pair2, j * U + k + U + 1)
                        act.wait_ge(summed2, j * U + k + 1)
                        act.activation(rows[:, k, G * D:2 * G * D], prod[:, k, :], ACT.Relu).then_inc(relu2, 1)

                    relu(0)
                    relu(1)
                    relu(2)
                    relu(3)

            @block.vector
            def _(dve):
                total = all_bodies(dve)
                dve.sem_inc(pair2, U)
                dve.sem_inc(added2, 4)
                dve.memset(acc[:, :], 0.0).then_inc(cleared2, 1)
                windows_reset(dve, windows2)
                nodes_reset(dve, windows2)
                dve.wait_ge(windows2, 3)
                dve.wait_ge(cleared2, 1)
                with dve.Fori(0, total, BODIES) as first:
                    with dve.Fori(0, BODIES) as i:
                        def turned(k):
                            dve.wait_ge(dst_loaded2, (first + i) * 16 + 16)
                            dve.wait_ge(expanded2, (first + i) * U + k + 1)
                            dve.tensor_scalar(onehot_p[:, k, :], dst_free[:, k * SC:(k + 1) * SC],
                                              node_of[:, ds(i * U + k, 1)], None, ALU.is_equal).then_inc(hot_t2, 1)

                        def split(k):
                            col = (i * U + k) * G
                            dve.tensor_tensor(lo_hot[:, k, :, :], iota_p.unsqueeze(1).broadcast_to([P, G, P]),
                                              src_lo[:, ds(col, G)].unsqueeze(2).broadcast_to([P, G, P]),
                                              ALU.is_equal)
                            dve.tensor_tensor(hi_hot[:, k, :, :], iota_p[:, 0:HI].unsqueeze(1).broadcast_to([P, G, HI]),
                                              src_hi[:, ds(col, G)].unsqueeze(2).broadcast_to([P, G, HI]),
                                              ALU.is_equal).then_inc(split2, 1)

                        def pair(k):
                            s = (first + i) * U + k
                            dve.wait_ge(expanded2, s + U + 1)
                            dve.wait_ge(gathered2[k], (first + i) * 16 * G + 16 * G)
                            dve.wait_ge(relu2, s + 1)
                            dve.tensor_tensor(prod[:, k, :], ps[2 + k % 2][:, :], rows[:, k, 0:G * D],
                                              ALU.add).then_inc(pair2, 1)

                        def add(k):
                            s = (first + i) * U + k
                            dve.wait_ge(summed2, s + U + 1)
                            dve.wait_ge(added2, 2 * s + 4)
                            dve.tensor_tensor(acc[:, ds(at[k], W)], acc[:, ds(at[k], W)], ps[4 + k % 2][:, 0:W],
                                              ALU.add).then_inc(added2, 1)
                            dve.tensor_tensor(count[:, ds(at[k], W)], count[:, ds(at[k], W)], ps[4 + k % 2][0:1, W:2 * W],
                                              ALU.add).then_inc(added2, 1)

                        dve.wait_ge(summed2, (first + i) * U + U)
                        turned(0)
                        turned(1)
                        at = window_starts(mybir.EngineType.DVE, i)
                        turned(2)
                        turned(3)
                        one_hot(dve, onehot, i).then_inc(hot_f2, U)
                        split(0)
                        pair(0)
                        for k in range(1, U):
                            split(k)
                            pair(k)
                            if k >= 2:
                                add(k - 2)
                        add(U - 2)
                        add(U - 1)
                    windows_move(dve, windows2)
                    nodes_move(dve, windows2)
                    dve.memset(src_hi[:, :], -1.0).then_inc(windows2, BODIES)
                    dve.wait_ge(windows2, 4 * first + 4 * BODIES + 3)

            @block.tensor
            def _(pe):
                total = all_bodies(pe)
                pe.sem_inc(summed2, U)
                nc.tensor.matmul(DEG, zeros[:, :], zeros[:, 0:HI], start=True, stop=False, skip_group_check=True)
                with pe.Fori(0, total) as j:
                    def expand(k):
                        pe.wait_ge(hot_t2, j * U + k + U + 1)
                        pe.wait_ge(window_loaded2[k], j * 16 + 16)
                        pe.wait_ge(pair2, j * U + k + U - 1)
                        for g in range(G):
                            last = nc.tensor.matmul(ps[2 + k % 2][:, g * P:(g + 1) * P], onehot_p[:, k, g::G],
                                                    window_p[:, k, :], start=True, stop=True)
                        last.then_inc(expanded2, 1)

                    def window_sum(k):
                        pe.wait_ge(split2, j * U + k + 1)
                        for g in range(G):
                            nc.tensor.matmul(DEG, lo_hot[:, k, g, :], hi_hot[:, k, g, :],
                                             start=False, stop=False, skip_group_check=True)
                        pe.wait_ge(relu2, j * U + k + U + 1)
                        pe.wait_ge(hot_f2, j * U + k + 1)
                        pe.wait_ge(added2, 2 * (j * U + k) + 2)
                        for g in range(G):
                            nc.tensor.matmul(ps[4 + k % 2][:, 0:W], rows[:, k, (G + g) * D:(G + g + 1) * D],
                                             onehot[:, k, g, :], start=(g == 0), stop=(g == G - 1))
                        for g in range(G):
                            last = nc.tensor.matmul(ps[4 + k % 2][0:1, W:2 * W], ones[:, 0:1], onehot[:, k, g, :],
                                                    start=(g == 0), stop=(g == G - 1))
                        last.then_inc(summed2, 1)

                    expand(0)
                    expand(1)
                    expand(2)
                    window_sum(0)
                    expand(3)
                    window_sum(1)
                    window_sum(2)
                    window_sum(3)

        degree = sem("degree")
        degree_sqrt = sem("degree_sqrt")
        agg_ps2 = sem("agg_ps2")
        agg2 = sem("agg2")
        hidden_ps2 = sem("hidden_ps2")
        hidden2 = sem("hidden2")
        mlp2 = sem("mlp2")
        twice2 = sem("twice2")
        sum2 = sem("sum2")
        y_ps = sem("y_ps")
        y_scaled = sem("y_scaled")
        y_stored = sem("y_stored")
        with nc.Block("layer2_nodes") as block:
            @block.tensor
            def _(pe):
                with pe.Fori(0, STEPS) as n:
                    def tile(l):
                        return n * LANES + l

                    for l in range(LANES):
                        pe.wait_ge(tile_done, 2 * NTILES + tile(l) + 1)
                        nc.tensor.matmul(bank(l, 0)[:, 0:T], we2_sb[:, :], acc[:, columns(tile(l))],
                                         start=True, stop=False)
                        nc.tensor.matmul(bank(l, 0)[:, 0:T], be2_sb[:, :], count[:, columns(tile(l))],
                                         start=False, stop=True).then_inc(agg_ps2, 1)
                    for l in range(LANES):
                        nc.tensor.matmul(bank(l, 2)[:, 0:T], wn1_sb[:, 0, :], x[:, columns(tile(l))],
                                         start=True, stop=False)
                        pe.wait_ge(agg2, tile(l) + 1)
                        nc.tensor.matmul(bank(l, 2)[:, 0:T], wn1_sb[:, 1, :], tmp[l],
                                         start=False, stop=True).then_inc(hidden_ps2, 1)
                    for l in range(LANES):
                        pe.wait_ge(hidden2, tile(l) + 1)
                        nc.tensor.matmul(bank(l, 0)[:, 0:T], wn2_sb[:, :], hid[l][:, 0, :],
                                         start=True, stop=True).then_inc(mlp2, 1)
                    norm_pe(pe, 4 * NTILES + n * LANES, sum2, tile)
                    for l in range(LANES):
                        pe.wait_ge(normed, 4 * NTILES + tile(l) + 1)
                        for j in range(TJ):
                            nc.tensor.transpose(bank(l, 2 * j)[:, 0:P], y[l][:, j * P:(j + 1) * P],
                                                ident).then_inc(y_ps, 1)

            @block.scalar
            def _(act):
                act.wait_ge(degree, 1)
                act.activation(dis_raw[:, :], deg_sb[:, :], ACT.Sqrt).then_inc(degree_sqrt, 1)
                with act.Fori(0, STEPS) as n:
                    load_sqrt_table(act)
                    for l in range(LANES):
                        act.wait_ge(agg_ps2, n * LANES + l + 1)
                        act.activation(tmp[l], bank(l, 0)[:, 0:T], ACT.Copy).then_inc(agg2, 1)
                    for l in range(LANES):
                        act.wait_ge(hidden_ps2, n * LANES + l + 1)
                        act.activation(hid[l][:, 0, :], bank(l, 2)[:, 0:T], ACT.Relu,
                                       bias=v("bn1")).then_inc(hidden2, 1)
                    norm_act(act, 4 * NTILES + n * LANES)
                    for l in range(LANES):
                        act.wait_ge(normed, 4 * NTILES + n * LANES + l + 1)
                        act.activation(x[:, columns(n * LANES + l)], y[l][:, :], ACT.Copy).then_inc(x_kept, 1)

            @block.vector
            def _(dve):
                dve.tensor_scalar(deg_sb[:, :], DEG, 1.0, None, ALU.max).then_inc(degree, 1)
                dve.tensor_scalar(deg_pos[:, :], DEG, 0.0, None, ALU.is_gt).then_inc(degree, 1)
                dve.wait_ge(degree_sqrt, 1)
                dve.reciprocal(dis_raw[:, :], dis_raw[:, :]).then_inc(degree, 1)
                dve.wait_ge(degree, 3)
                dve.tensor_tensor(dis[:, :], dis_raw[:, :], deg_pos[:, :], ALU.mult).then_inc(degree, 1)
                dve.wait_ge(degree, 4)
                with dve.Fori(0, STEPS) as n:
                    for l in range(LANES):
                        c = n * LANES + l
                        dve.wait_ge(tile_done, 2 * NTILES + c + 1)
                        dve.tensor_scalar(y2[l][:, :], x[:, columns(c)], 2.0, v("bn2"), ALU.mult,
                                          ALU.add).then_inc(twice2, 1)
                    for l in range(LANES):
                        dve.wait_ge(twice2, n * LANES + l + 1)
                        dve.wait_ge(mlp2, n * LANES + l + 1)
                        dve.tensor_tensor(res[l], bank(l, 0)[:, 0:T], y2[l][:, :], ALU.add).then_inc(sum2, 1)
                    norm_dve(dve, 4 * NTILES + n * LANES)
                    for l in range(LANES):
                        for j in range(TJ):
                            t = (n * LANES + l) * TJ + j
                            dve.wait_ge(y_ps, t + 1)
                            dve.tensor_scalar(node_rows[l][:, j, 0:D], bank(l, 2 * j)[:, 0:P], dis[:, ds(t, 1)], None,
                                              ALU.mult).then_inc(y_scaled, 1)

            @block.gpsimd
            def _(pool):
                with pool.Fori(0, STEPS) as n:
                    for l in range(LANES):
                        c = n * LANES + l
                        pool.wait_ge(y_scaled, c * TJ + TJ)
                        pool.sem_inc(pool_waited, 1)
                        split_rows(pool, 2 * NTILES + c, l, 0)

            @block.sync
            def _(sp):
                with sp.Fori(0, STEPS) as n:
                    for l in range(LANES):
                        c = n * LANES + l
                        sp.wait_ge(y_scaled, c * TJ + TJ)
                        sp.sem_inc(sp_waited, 1)
                        sp.wait_ge(split_step, (2 * NTILES + c) * SPLITS + SPLITS)
                        sp.sem_inc(sp_waited, 1)
                        sp.dma_start(y_rows[columns(c), :].rearrange("(j p) f -> p j f", p=P),
                                     parts_b[l][:, :, :]).then_inc(y_stored, 16)
                        sp.wait_ge(y_stored, c * 16 + 16)
                        sp.sem_inc(sp_waited, 1)
                        sp.wait_ge(x_kept, 2 * NTILES + c + 1)
                        sp.sem_inc(tile_done, 1)

        window_loaded3 = [sem(f"window_loaded3_{k}") for k in range(U)]
        scattered = [sem(f"scattered{k}") for k in range(U)]
        landed = [sem(f"landed{k}") for k in range(U)]
        picked3 = sem("picked3")
        hot3 = sem("hot3")
        spread3 = sem("spread3")
        same3 = sem("same3")
        earlier3 = sem("earlier3")
        to_spare3 = sem("to_spare3")
        shift3 = sem("shift3")
        target3 = sem("target3")
        counted3 = sem("counted3")
        counts3 = sem("counts3")
        expanded3 = sem("expanded3")
        value3 = sem("value3")
        windows3 = sem("windows3")
        with nc.Block("layer3_edges") as block:
            @block.sync
            def _(sp):
                total = all_bodies(sp)
                for k in range(U):
                    sp.sem_inc(landed[k], 1)
                with sp.Fori(0, total) as j:
                    for k in range(U):
                        sp.wait_ge(scattered[k], j * 16 * G + 16 * G)
                        sp.sem_inc(landed[k], 1)

            @block.scalar
            def _(act):
                total = all_bodies(act)
                act.sem_inc(counts3, 2)
                act.sem_inc(value3, 2)
                act.sem_inc(expanded3, U)
                with act.Fori(0, total, BODIES) as first:
                    act.wait_ge(windows3, 2 * first + 2)
                    with act.Fori(0, BODIES) as i:
                        at = window_starts(mybir.EngineType.Activation, i)
                        j = first + i
                        for k in range(U):
                            act.wait_ge(expanded3, j * U + k + 1)
                            act.dma_start(window[:, k, :], y_rows[ds(at[k], W), :]).then_inc(window_loaded3[k], 16)

                        def counts(k):
                            act.wait_ge(counted3, j * U + k + U + 1)
                            act.wait_ge(expanded3, j * U + k + 1)
                            act.activation(onehot_t[:, k, :], ps[2 + k % 2][0:W, :], ACT.Copy).then_inc(counts3, 1)

                        def values(k):
                            act.wait_ge(expanded3, j * U + k + U + 1)
                            act.wait_ge(landed[k], j + 1)
                            act.activation(rows[:, k, 0:G * D], ps[4 + k % 2][:, :], ACT.Copy).then_inc(value3, 1)

                        counts(0)
                        for k in range(1, U):
                            counts(k)
                            values(k - 1)
                        values(U - 1)

            @block.gpsimd
            def _(pool):
                total = all_bodies(pool)
                with pool.Fori(0, total) as j:
                    for k in range(U):
                        pool.wait_ge(value3, j * U + k + 3)
                        pool.wait_ge(target3, j * U + k + 1)
                        pool.sem_inc(pool_waited, 1)
                        pool.wait_ge(landed[(k + 2) % U], j + 1 + (1 if k >= 2 else 0))
                        pool.sem_inc(pool_waited, 1)
                        for g in range(G):
                            pool.indirect_dma_start(table[(k % 2) * G + g][:, :],
                                                    bass.IndirectOffsetOnAxis(ap=index[:, k, g:g + 1], axis=0),
                                                    rows[:, k, g * D:(g + 1) * D], None,
                                                    compute_op=ALU.add).then_inc(scattered[k], 16)

            @block.vector
            def _(dve):
                total = all_bodies(dve)
                dve.sem_inc(same3, 2)
                dve.sem_inc(earlier3, 1)
                windows_reset(dve, windows3)
                dve.wait_ge(windows3, 2)
                with dve.Fori(0, total, BODIES) as first:
                    with dve.Fori(0, BODIES) as i:
                        def hot(k):
                            s = (first + i) * U + k
                            dve.wait_ge(counted3, s + 1)
                            dve.tensor_copy(src_s[:, k, :], src_num[:, ds((i * U + k) * G, G)]).then_inc(picked3, 1)
                            one_hot(dve, onehot_b, i, k, 1).then_inc(hot3, 1)

                        def equal(k):
                            s = (first + i) * U + k
                            dve.wait_ge(picked3, s + 1)
                            dve.wait_ge(spread3, s + 1)
                            dve.tensor_tensor(same[:, k, :, :], ps[k % 2][:, :].rearrange("p (g e) -> p g e", g=G),
                                              src_s[:, k, :].unsqueeze(2).broadcast_to([P, G, P]),
                                              ALU.is_equal).then_inc(same3, 1)

                        def targets(k):
                            s = (first + i) * U + k
                            dve.wait_ge(same3, s + 3)
                            for g in range(G):
                                dve.wait_ge(earlier3, s * G + g + 1)
                                dve.tensor_tensor_reduce(masked[:, :], same[:, k, g, :], lower, 1.0, 0.0, ALU.mult,
                                                         ALU.add, earlier[:, k, g:g + 1]).then_inc(earlier3, 1)
                            dve.tensor_scalar(to_spare[:, k, :], src_s[:, k, :], -1.0, spare_row[:, :], ALU.mult,
                                              ALU.add).then_inc(to_spare3, 1)
                            dve.wait_ge(earlier3, s * G + G + 1)
                            dve.wait_ge(to_spare3, s + 1)
                            dve.scalar_tensor_tensor(shift_by[:, k, :], earlier[:, k, :], 0.0, to_spare[:, k, :],
                                                     ALU.is_gt, ALU.mult).then_inc(shift3, 1)
                            dve.wait_ge(shift3, s + 1)
                            dve.wait_ge(landed[k], first + i + 1)
                            dve.tensor_tensor(index[:, k, :], src_s[:, k, :], shift_by[:, k, :],
                                              ALU.add).then_inc(target3, 1)

                        hot(0)
                        hot(1)
                        equal(0)
                        targets(0)
                        hot(2)
                        equal(1)
                        targets(1)
                        hot(3)
                        equal(2)
                        targets(2)
                        equal(3)
                        targets(3)
                    windows_move(dve, windows3)
                    dve.wait_ge(windows3, 2 * first + 2 * BODIES + 2)

            @block.tensor
            def _(pe):
                total = all_bodies(pe)
                pe.sem_inc(counted3, U)
                with pe.Fori(0, total) as j:
                    def spread(k):
                        pe.wait_ge(picked3, j * U + k + 1)
                        pe.wait_ge(same3, j * U + k + 1)
                        for g in range(G):
                            last = nc.tensor.matmul(ps[k % 2][:, g * P:(g + 1) * P],
                                                    src_s[:, k, g:g + 1].broadcast_to([P, P]), ident,
                                                    start=True, stop=True)
                        last.then_inc(spread3, 1)

                    def counts(k):
                        pe.wait_ge(same3, j * U + k + 3)
                        pe.wait_ge(hot3, j * U + k + 1)
                        pe.wait_ge(counts3, j * U + k + 1)
                        for g in range(G):
                            last = nc.tensor.matmul(ps[2 + k % 2][0:W, g * P:(g + 1) * P], onehot_b[:, k, g, :],
                                                    same[:, k, g, :], start=True, stop=True)
                        last.then_inc(counted3, 1)

                    def expand(k):
                        pe.wait_ge(counts3, j * U + k + 3)
                        pe.wait_ge(window_loaded3[k], j * 16 + 16)
                        pe.wait_ge(value3, j * U + k + 1)
                        for g in range(G):
                            for part in range(3):
                                last = nc.tensor.matmul(ps[4 + k % 2][:, g * P:(g + 1) * P],
                                                        onehot_t[:, k, g * P:(g + 1) * P],
                                                        window[:, k, part * D:(part + 1) * D],
                                                        start=(part == 0), stop=(part == 2))
                        last.then_inc(expanded3, 1)

                    spread(0)
                    spread(1)
                    counts(0)
                    for k in range(2, U):
                        spread(k)
                        counts(k - 1)
                        expand(k - 2)
                    counts(U - 1)
                    expand(U - 2)
                    expand(U - 1)


        tables_loaded = [sem(f"tables_loaded{l}") for l in range(LANES)]
        diag3 = sem("diag3")
        agg_ps3 = sem("agg_ps3")
        agg3 = sem("agg3")
        lin3 = sem("lin3")
        sum3 = sem("sum3")
        out_stored = sem("out_stored")
        parts = [rows[:, 2 * l:2 * l + 2, :].rearrange("p u c -> p (u c)")
                 .rearrange("p (t j f) -> p t j f", t=TABLES, f=D) for l in range(LANES)]
        diag = [hid[l][:, 1, :] for l in range(LANES)]
        nth3 = 5 * NTILES
        with nc.Block("layer3_nodes") as block:
            @block.tensor
            def _(pe):
                with pe.Fori(0, STEPS) as n:
                    def tile(l):
                        return n * LANES + l

                    for l in range(LANES):
                        pe.wait_ge(tables_loaded[l], n * 16 * TABLES + 16 * TABLES)
                        pe.wait_ge(diag3, tile(l) * TJ + TJ)
                        for j in range(TJ):
                            for t in range(TABLES):
                                last = nc.tensor.matmul(bank(l, 0)[:, j * P:(j + 1) * P], parts[l][:, t, j, :],
                                                        diag[l][:, j * P:(j + 1) * P],
                                                        start=(t == 0), stop=(t == TABLES - 1))
                        last.then_inc(agg_ps3, 1)
                    for l in range(LANES):
                        pe.wait_ge(agg3, tile(l) + 1)
                        nc.tensor.matmul(bank(l, 2)[:, 0:T], w3t_sb[:, :], tmp[l], start=True, stop=True).then_inc(lin3, 1)
                    norm_pe(pe, nth3 + n * LANES, sum3, tile)

            @block.scalar
            def _(act):
                with act.Fori(0, STEPS) as n:
                    load_sqrt_table(act)
                    for l in range(LANES):
                        act.wait_ge(agg_ps3, n * LANES + l + LANES + 1)
                        act.activation(tmp[l], bank(l, 0)[:, 0:T], ACT.Copy).then_inc(agg3, 1)
                    norm_act(act, nth3 + n * LANES)

            @block.vector
            def _(dve):
                with dve.Fori(0, STEPS) as n:
                    for l in range(LANES):
                        c = n * LANES + l
                        dve.wait_ge(tile_done, 3 * NTILES + c + 1)
                        for j in range(TJ):
                            dve.tensor_scalar(diag[l][:, j * P:(j + 1) * P], ident, dis[:, ds(c * TJ + j, 1)], None,
                                              ALU.mult).then_inc(diag3, 1)
                    for l in range(LANES):
                        c = n * LANES + l
                        dve.wait_ge(lin3, c + 1)
                        dve.scalar_tensor_tensor(res[l], bank(l, 2)[:, 0:T], v("b3"), x[:, columns(c)], ALU.add,
                                                 ALU.add).then_inc(sum3, 1)
                    norm_dve(dve, nth3 + n * LANES)

            @block.sync
            def _(sp):
                sp.sem_inc(agg_ps3, LANES)
                with sp.Fori(0, STEPS) as n:
                    for l in range(LANES):
                        c = n * LANES + l
                        sp.wait_ge(agg_ps3, c + 1)
                        sp.sem_inc(sp_waited, 1)
                        for t in range(TABLES):
                            sp.dma_start(parts[l][:, t, :, :],
                                         table[t][columns(c), :].rearrange("(j p) f -> p j f", p=P)
                                         ).then_inc(tables_loaded[l], 16)

            @block.gpsimd
            def _(pool):
                with pool.Fori(0, STEPS) as n:
                    for l in range(LANES):
                        c = n * LANES + l
                        pool.wait_ge(normed, nth3 + c + 1)
                        pool.sem_inc(pool_waited, 1)
                        pool.dma_start(out[:, columns(c)], y[l][:, :]).then_inc(out_stored, 16)
                        pool.wait_ge(out_stored, c * 16 + 16)
                        pool.sem_inc(tile_done, 1)
                pool.wait_ge(out_stored, 16 * NTILES)


def layouts(inputs):
    import numpy as np
    a = {k: np.asarray(x) for k, x in inputs.items()}
    n, e = a["x"].shape[0], a["src"].shape[0]
    nodes, scs, scs_others = sizes(n, e)
    first = np.arange(scs) * SC
    start = np.minimum(first, e - SC).astype(np.int32)
    edge = (start[:, None] + np.arange(SC)[None, :])
    own = edge >= first[:, None]
    place = lambda m: np.ascontiguousarray(m.reshape(scs, P, G).transpose(1, 0, 2).reshape(P, scs * G))
    minus = np.int32(-1)
    by_rows = a["dst"][np.where(own, edge, e - 1)]
    xt = np.zeros((P, nodes), np.float32)
    xt[:, :n] = a["x"].T
    ramp = np.broadcast_to(np.arange(P, dtype=np.float32), (P, P))
    consts = np.concatenate([np.eye(P, dtype=np.float32), np.tril(np.ones((P, P), np.float32), -1),
                             np.eye(P, dtype=np.float32) - np.float32(1.0 / D), ramp[:, :W], ramp,
                             nodes + np.arange(P, dtype=np.float32)[:, None],
                             (np.arange(P)[:, None] == np.arange(P)[None, :] // HEAD).astype(np.float32),
                             (np.arange(P) // 3).astype(np.float32)[:, None]], axis=1)
    b1 = a["L0_gnn_b1"].reshape(4, P)
    vectors = np.stack([*b1, a["L0_gnn_b2"], a["L1_gnn_bO"], a["L1_gnn_ln1_g"], a["L1_gnn_ln1_b"], a["L1_gnn_b1"],
                        a["L1_gnn_b2"], a["L1_gnn_ln2_g"], a["L1_gnn_ln2_b"], a["L2_gnn_bn1"], a["L2_gnn_bn2"],
                        a["L3_gnn_b"]], axis=1)
    be1 = a["L2_gnn_be1"]
    index = place(np.where(own, a["src"][edge], np.int32(0)))
    return {
        "xT": xt, "edge_attr": a["edge_attr_128"],
        "src_index": np.concatenate([index[:, :scs_others * G], index[:, :U * G]], axis=1),
        "src_id": place(np.where(own, a["src"][edge], minus)),
        "dst_id": place(np.where(own, a["dst"][edge], minus)),
        "dst_rows": np.ascontiguousarray(by_rows.reshape(4, scs // 4, SC).transpose(1, 0, 2)),
        "consts": np.ascontiguousarray(consts),
        "w1": a["L0_gnn_W1"], "w2": a["L0_gnn_W2"],
        "wqkv": np.concatenate([a["L1_gnn_WQ"], a["L1_gnn_WK"], a["L1_gnn_WV"]], axis=1),
        "wo": a["L1_gnn_WO"], "aw1": a["L1_gnn_W1"], "aw2": a["L1_gnn_W2"],
        "we1": a["L2_gnn_We1"], "we2": a["L2_gnn_We2"], "wn1": a["L2_gnn_Wn1"], "wn2": a["L2_gnn_Wn2"],
        "w3t": np.ascontiguousarray(a["L3_gnn_W"].T), "vectors": np.ascontiguousarray(vectors),
        "row_bqkv": np.concatenate([a["L1_gnn_bQ"], a["L1_gnn_bK"], a["L1_gnn_bV"]])[None, :],
        "row_be1": np.concatenate([np.zeros_like(be1), be1])[None, :], "row_be2": a["L2_gnn_be2"][None, :],
    }


def kernel(**inputs):
    import numpy as np
    import concourse.bacc as bacc
    from concourse import mybir as mb
    from concourse.bass_utils import run_bass_kernel_spmd

    n = np.asarray(inputs["x"]).shape[0]
    arrays = layouts(inputs)
    nc = bacc.Bacc("TRN2", target_bir_lowering=False, num_devices=1)
    args = {}
    for name, a in arrays.items():
        args[name] = nc.dram_tensor(f"in_{name}", a.shape, mb.dt.from_np(a.dtype), kind="ExternalInput").ap()
    nodes = arrays["xT"].shape[1]
    args["out"] = nc.dram_tensor("out_0", (P, nodes), mb.dt.float32, kind="ExternalOutput").ap()
    gnn_program(nc, **args)
    r = run_bass_kernel_spmd(nc, [{f"in_{name}": a for name, a in arrays.items()}], core_ids=[0])
    return np.ascontiguousarray(r.results[0]["out_0"][:, :n].T)
```
